# Optimizing a Trainium2 kernel written in Bass

```python
import numpy as np
import jax
import jax.numpy as jnp

def _softmax(x, axis=-1):
    return jax.nn.softmax(x, axis=axis)

def _gelu(x):
    return jax.nn.gelu(x, approximate=True)

def _silu(x):
    return jax.nn.silu(x)

def _sigmoid(x):
    return jax.nn.sigmoid(x)

def _layernorm(x, axis=-1, eps=1e-05):
    m = jnp.mean(x, axis=axis, keepdims=True)
    v = jnp.var(x, axis=axis, keepdims=True)
    return (x - m) / jnp.sqrt(v + eps)

def _scatter_add(tgt, idx, src, axis=0):
    return tgt.at[idx].add(src)

def _segment_sum(src, seg, n):
    return jax.ops.segment_sum(src, seg, n)
kernel_name = 'mk_gnn_preln_d4_gnn_r64_c2c470'

def setup_inputs(seed: int=0):
    np.random.seed(seed)
    _w = jnp.asarray

    def _rec_inputs():
        import jax
        import jax.numpy as jnp
        _gk = jax.random.key(seed)
        x = -0.000202 + 1 * jax.random.normal(jax.random.fold_in(_gk, 1), (100000, 128), jnp.float32)
        src = jax.random.randint(jax.random.fold_in(_gk, 2), (25000,), 0, 100000, jnp.int32)
        dst = jnp.minimum((100000 * jax.random.uniform(jax.random.fold_in(_gk, 3), (25000,)) ** 2.0).astype(jnp.int32), 99999)
        _o = jnp.argsort(dst, stable=True)
        src = src[_o]
        dst = dst[_o]
        edge_attr_3 = 0.000669165 + 0.999965 * jax.random.normal(jax.random.fold_in(_gk, 12), (25000, 3), jnp.float32)
        edge_attr_32 = 0.000196303 + 1.00016 * jax.random.normal(jax.random.fold_in(_gk, 13), (25000, 32), jnp.float32)
        edge_weight = jax.random.uniform(jax.random.fold_in(_gk, 15), (25000,), jnp.float32, 0.0, 0.999999)
        return (x, src, dst, edge_attr_3, edge_attr_32, edge_weight)
    x, src, dst, edge_attr_3, edge_attr_32, edge_weight = _rec_inputs()

    def _L0_gnn_setup():
        import jax, jax.numpy as jnp
        import numpy as np
        N_NODES = 50000
        N_EDGES = 12500
        IN_DIM = 128
        EDGE_DIM = 32
        HIDDEN = 128
        NUM_LAYERS = 3
        BN_EPS = 1e-05
        RES_SCALE = 0.1
        key = jax.random.key(seed)
        ks = jax.random.split(key, 10)
        x = jax.random.normal(ks[0], (N_NODES, IN_DIM), dtype=jnp.float32)
        edge_index = jax.random.randint(ks[1], (2, N_EDGES), 0, N_NODES, dtype=jnp.int64)
        edge_attr = jax.random.normal(ks[2], (N_EDGES, EDGE_DIM), dtype=jnp.float32)
        s = 0.05
        We = jax.random.normal(ks[3], (NUM_LAYERS, EDGE_DIM, HIDDEN), dtype=jnp.float32) * s
        be = jax.random.normal(ks[4], (NUM_LAYERS, HIDDEN), dtype=jnp.float32) * s
        W1 = jax.random.normal(ks[5], (NUM_LAYERS, HIDDEN, HIDDEN), dtype=jnp.float32) * s
        b1 = jax.random.normal(ks[6], (NUM_LAYERS, HIDDEN), dtype=jnp.float32) * s
        W2 = jax.random.normal(ks[7], (NUM_LAYERS, HIDDEN, HIDDEN), dtype=jnp.float32) * s
        b2 = jax.random.normal(ks[8], (NUM_LAYERS, HIDDEN), dtype=jnp.float32) * s
        gamma = jnp.ones((NUM_LAYERS, HIDDEN), dtype=jnp.float32)
        beta = jnp.zeros((NUM_LAYERS, HIDDEN), dtype=jnp.float32)
        return {'x': x, 'edge_index': edge_index, 'edge_attr': edge_attr, 'We': We, 'be': be, 'W1': W1, 'b1': b1, 'W2': W2, 'b2': b2, 'gamma': gamma, 'beta': beta}
    _L0_gnn_all = _L0_gnn_setup()
    _L0_gnn_in = {k: v for k, v in _L0_gnn_all.items() if k in ('We', 'be', 'W1', 'b1', 'W2', 'b2', 'gamma', 'beta')}
    del _L0_gnn_all

    def _L1_gnn_setup():
        import jax, jax.numpy as jnp
        import numpy as np
        NUM_LAYERS = 3

        def _scatter_mean_layer(x, src, dst, num_nodes):
            msgs = x[src]
            summed = jax.ops.segment_sum(msgs, dst, num_segments=num_nodes)
            counts = jax.ops.segment_sum(jnp.ones((src.shape[0],), dtype=x.dtype), dst, num_segments=num_nodes)
            return summed / jnp.maximum(counts, 1.0)[:, None]
        key = jax.random.key(seed)
        k1, k2, k3 = jax.random.split(key, 3)
        N, E, D = (100000, 50000, 128)
        x = jax.random.normal(k1, (N, D), dtype=jnp.float32)
        src = jax.random.randint(k2, (E,), 0, N)
        dst = jax.random.randint(k3, (E,), 0, N)
        edge_index = jnp.stack([src, dst], axis=0).astype(jnp.int64)
        return {'x': x, 'edge_index': edge_index}
    _L1_gnn_all = _L1_gnn_setup()
    _L1_gnn_in = {k: v for k, v in _L1_gnn_all.items() if k in ()}
    del _L1_gnn_all

    def _L2_gnn_setup():
        import jax, jax.numpy as jnp
        import numpy as np
        N = 50000
        E = 12500
        IN_DIM = 128
        OUT_DIM = 128
        EDGE_DIM = 3
        H = 4
        HD = OUT_DIM // H
        SCALE = HD ** (-0.5)
        key = jax.random.key(seed)
        ks = jax.random.split(key, 10)
        x = jax.random.normal(ks[0], (N, IN_DIM), dtype=jnp.float32)
        edge_index = jax.random.randint(ks[1], (2, E), 0, N, dtype=jnp.int64)
        edge_attr = jax.random.normal(ks[2], (E, EDGE_DIM), dtype=jnp.float32)
        s = 1.0 / np.sqrt(IN_DIM)
        Wq = jax.random.normal(ks[3], (IN_DIM, H * HD), dtype=jnp.float32) * s
        Wk = jax.random.normal(ks[4], (IN_DIM, H * HD), dtype=jnp.float32) * s
        Wv = jax.random.normal(ks[5], (IN_DIM, H * HD), dtype=jnp.float32) * s
        We = jax.random.normal(ks[6], (EDGE_DIM, H), dtype=jnp.float32) * (1.0 / np.sqrt(EDGE_DIM))
        Wo = jax.random.normal(ks[7], (H * HD, OUT_DIM), dtype=jnp.float32) * (1.0 / np.sqrt(H * HD))
        bo = jnp.zeros((OUT_DIM,), dtype=jnp.float32)
        Wm = jax.random.normal(ks[8], (IN_DIM + OUT_DIM, OUT_DIM), dtype=jnp.float32) * (1.0 / np.sqrt(IN_DIM + OUT_DIM))
        bm = jnp.zeros((OUT_DIM,), dtype=jnp.float32)
        return {'x': x, 'edge_index': edge_index, 'edge_attr': edge_attr, 'Wq': Wq, 'Wk': Wk, 'Wv': Wv, 'We': We, 'Wo': Wo, 'bo': bo, 'Wm': Wm, 'bm': bm}
    _L2_gnn_all = _L2_gnn_setup()
    _L2_gnn_in = {k: v for k, v in _L2_gnn_all.items() if k in ('Wq', 'Wk', 'Wv', 'We', 'Wo', 'bo', 'Wm', 'bm')}
    del _L2_gnn_all

    def _L3_gnn_setup():
        import jax, jax.numpy as jnp
        import numpy as np
        N_NODES = 50000
        N_EDGES = 12500
        HIDDEN = 128
        key = jax.random.key(seed)
        k1, k2, k3, k4, k5, k6 = jax.random.split(key, 6)
        node_features = jax.random.normal(k1, (N_NODES, HIDDEN), dtype=jnp.float32)
        src = jax.random.randint(k2, (N_EDGES,), 0, N_NODES)
        tgt = jax.random.randint(k3, (N_EDGES,), 0, N_NODES)
        gcn_norm = jax.random.uniform(k4, (N_EDGES,), dtype=jnp.float32)
        scale = 1.0 / np.sqrt(HIDDEN)
        W1 = jax.random.normal(k5, (HIDDEN, HIDDEN), dtype=jnp.float32) * scale
        b1 = jnp.zeros((HIDDEN,), dtype=jnp.float32)
        W2 = jax.random.normal(k6, (HIDDEN, HIDDEN), dtype=jnp.float32) * scale
        b2 = jnp.zeros((HIDDEN,), dtype=jnp.float32)
        return {'node_features': node_features, 'src': src, 'tgt': tgt, 'gcn_norm': gcn_norm, 'W1': W1, 'b1': b1, 'W2': W2, 'b2': b2}
    _L3_gnn_all = _L3_gnn_setup()
    _L3_gnn_in = {k: v for k, v in _L3_gnn_all.items() if k in ('W1', 'b1', 'W2', 'b2')}
    del _L3_gnn_all
    return {'x': x, 'src': src, 'dst': dst, 'edge_attr_3': edge_attr_3, 'edge_attr_32': edge_attr_32, 'edge_weight': edge_weight, 'L0_gnn_We': _L0_gnn_in['We'], 'L0_gnn_be': _L0_gnn_in['be'], 'L0_gnn_W1': _L0_gnn_in['W1'], 'L0_gnn_b1': _L0_gnn_in['b1'], 'L0_gnn_W2': _L0_gnn_in['W2'], 'L0_gnn_b2': _L0_gnn_in['b2'], 'L0_gnn_gamma': _L0_gnn_in['gamma'], 'L0_gnn_beta': _L0_gnn_in['beta'], 'L2_gnn_Wq': _L2_gnn_in['Wq'], 'L2_gnn_Wk': _L2_gnn_in['Wk'], 'L2_gnn_Wv': _L2_gnn_in['Wv'], 'L2_gnn_We': _L2_gnn_in['We'], 'L2_gnn_Wo': _L2_gnn_in['Wo'], 'L2_gnn_bo': _L2_gnn_in['bo'], 'L2_gnn_Wm': _L2_gnn_in['Wm'], 'L2_gnn_bm': _L2_gnn_in['bm'], 'L3_gnn_W1': _L3_gnn_in['W1'], 'L3_gnn_b1': _L3_gnn_in['b1'], 'L3_gnn_W2': _L3_gnn_in['W2'], 'L3_gnn_b2': _L3_gnn_in['b2']}

def reference(x, src, dst, edge_attr_3, edge_attr_32, edge_weight, L0_gnn_We, L0_gnn_be, L0_gnn_W1, L0_gnn_b1, L0_gnn_W2, L0_gnn_b2, L0_gnn_gamma, L0_gnn_beta, L2_gnn_Wq, L2_gnn_Wk, L2_gnn_Wv, L2_gnn_We, L2_gnn_Wo, L2_gnn_bo, L2_gnn_Wm, L2_gnn_bm, L3_gnn_W1, L3_gnn_b1, L3_gnn_W2, L3_gnn_b2):
    import jax
    import jax.numpy as jnp

    def _L0_gnn_ref(x, edge_index, edge_attr, We, be, W1, b1, W2, b2, gamma, beta):
        import jax, jax.numpy as jnp
        import numpy as np
        N_NODES = 50000
        N_EDGES = 12500
        IN_DIM = 128
        EDGE_DIM = 32
        HIDDEN = 128
        NUM_LAYERS = 3
        BN_EPS = 1e-05
        RES_SCALE = 0.1
        src = edge_index[0]
        dst = edge_index[1]
        n = x.shape[0]
        h = x
        for l in range(NUM_LAYERS):
            h_res = h
            e = edge_attr @ We[l] + be[l]
            msg = jax.nn.relu(h[src] + e)
            agg = jax.ops.segment_sum(msg, dst, num_segments=n)
            z = h + agg
            z = jax.nn.relu(z @ W1[l] + b1[l]) @ W2[l] + b2[l]
            mu = jnp.mean(z, axis=0)
            var = jnp.var(z, axis=0)
            z = (z - mu) * jax.lax.rsqrt(var + BN_EPS) * gamma[l] + beta[l]
            z = jax.nn.relu(z)
            h = z + RES_SCALE * h_res
        return h

    def _L1_gnn_ref(x, edge_index):
        import jax, jax.numpy as jnp
        import numpy as np
        NUM_LAYERS = 3

        def _scatter_mean_layer(x, src, dst, num_nodes):
            msgs = x[src]
            summed = jax.ops.segment_sum(msgs, dst, num_segments=num_nodes)
            counts = jax.ops.segment_sum(jnp.ones((src.shape[0],), dtype=x.dtype), dst, num_segments=num_nodes)
            return summed / jnp.maximum(counts, 1.0)[:, None]
        src = edge_index[0]
        dst = edge_index[1]
        num_nodes = x.shape[0]
        for _ in range(NUM_LAYERS):
            x = _scatter_mean_layer(x, src, dst, num_nodes)
        return x

    def _L2_gnn_ref(x, edge_index, edge_attr, Wq, Wk, Wv, We, Wo, bo, Wm, bm):
        import jax, jax.numpy as jnp
        import numpy as np
        N = 50000
        E = 12500
        IN_DIM = 128
        OUT_DIM = 128
        EDGE_DIM = 3
        H = 4
        HD = OUT_DIM // H
        SCALE = HD ** (-0.5)
        n = x.shape[0]
        src = edge_index[0]
        dst = edge_index[1]
        Q = (x @ Wq).reshape(n, H, HD)
        K = (x @ Wk).reshape(n, H, HD)
        V = (x @ Wv).reshape(n, H, HD)
        edge_bias = edge_attr @ We
        attn = jnp.sum(Q[dst] * K[src], axis=-1) * SCALE + edge_bias
        attn = jnp.where(attn >= 0, attn, 0.2 * attn)
        attn_exp = jnp.exp(attn - jnp.max(attn))
        attn_sum = jax.ops.segment_sum(attn_exp, dst, num_segments=n)
        attn_norm = attn_exp / jnp.maximum(attn_sum[dst], 1e-12)
        weighted_V = V[src] * attn_norm[:, :, None]
        agg = jax.ops.segment_sum(weighted_V, dst, num_segments=n)
        agg = agg.reshape(n, H * HD) @ Wo + bo
        h = jnp.concatenate([x, agg], axis=1) @ Wm + bm
        return jax.nn.relu(h)

    def _L3_gnn_ref(node_features, src, tgt, gcn_norm, W1, b1, W2, b2):
        import jax, jax.numpy as jnp
        import numpy as np
        N_NODES = 50000
        N_EDGES = 12500
        HIDDEN = 128
        edge_states = node_features[src]
        messages = gcn_norm[:, None] * jax.nn.relu(edge_states @ W1 + b1)
        pooled = jax.ops.segment_sum(messages, tgt, num_segments=node_features.shape[0])
        hidden = jax.nn.relu(pooled @ W2 + b2)
        return hidden + node_features
    edge_index = jnp.stack([src, dst])
    h = jnp.maximum(_layernorm(x, axis=-1), 0.0)
    x = x + _L0_gnn_ref(h, edge_index, edge_attr_32, L0_gnn_We, L0_gnn_be, L0_gnn_W1, L0_gnn_b1, L0_gnn_W2, L0_gnn_b2, L0_gnn_gamma, L0_gnn_beta)
    h = jnp.maximum(_layernorm(x, axis=-1), 0.0)
    x = x + _L1_gnn_ref(h, edge_index)
    h = jnp.maximum(_layernorm(x, axis=-1), 0.0)
    x = x + _L2_gnn_ref(h, edge_index, edge_attr_3, L2_gnn_Wq, L2_gnn_Wk, L2_gnn_Wv, L2_gnn_We, L2_gnn_Wo, L2_gnn_bo, L2_gnn_Wm, L2_gnn_bm)
    h = jnp.maximum(_layernorm(x, axis=-1), 0.0)
    x = x + _L3_gnn_ref(h, src, dst, edge_weight, L3_gnn_W1, L3_gnn_b1, L3_gnn_W2, L3_gnn_b2)
    return x

_drawn_inputs = setup_inputs


def setup_inputs(seed=0):
    import zlib

    import numpy as np

    out = dict(_drawn_inputs(seed))
    spreads = {'L0_gnn_gamma': (1.0, 0.2),
     'L0_gnn_beta': (0.0, 0.1),
     'L2_gnn_bo': (0.0, 0.1),
     'L2_gnn_bm': (0.0, 0.1),
     'L3_gnn_b1': (0.0, 0.8),
     'L3_gnn_b2': (0.0, 0.1)}
    factors = {'edge_attr_3': 150.155,
     'L0_gnn_b2': 200.0,
     'L2_gnn_Wq': 8.0,
     'L2_gnn_Wk': 64.0,
     'L2_gnn_We': 170.502,
     'L2_gnn_Wv': 21.454,
     'L2_gnn_Wo': 24.517}
    for name, (base, spread) in spreads.items():
        noise = np.random.default_rng([zlib.crc32(name.encode()), seed]).standard_normal(out[name].shape)
        drawn = base * np.exp(spread * noise) if base else spread * noise
        out[name] = jnp.asarray(drawn.astype(out[name].dtype))
    for name, factor in factors.items():
        out[name] = (out[name] * factor).astype(out[name].dtype)
    return out
```

```python
import concourse.bass as bass
from concourse import mybir
from contextlib import ExitStack, contextmanager

F32 = mybir.dt.float32
BF16 = mybir.dt.bfloat16
I32 = mybir.dt.int32
ALU = mybir.AluOpType
ACT = mybir.ActivationFunctionType
AX = mybir.AxisListType
REDUCE_MAX = bass.bass_isa.ReduceOp.max

P = 128
N = 100000
E = 25000
CH = 512
U = 4
GRP = U * CH
HALF = GRP // 2
GD = -(-N // GRP)
NP = GD * GRP
GE = -(-E // HALF)
EP = GE * HALF
ET = EP // P
ZR = EP
TAIL_P = (N - (2 * GD - 1) * HALF) // 8
H = 4
HD = P // H
LAYERS = 3
EA = 32
EB = 3
EPS = 1e-5
RES = 0.1
FAR = 1000000
assert N % 8 == 0 and 0 < TAIL_P <= P


class Steps:

    def __init__(self, eng, sem, per):
        self.eng, self.sem, self.per, self.k, self.base = eng, sem, per, 0, 0

    def at(self, i):
        self.base, self.k = i * self.per, 0

    def did(self, ins):
        self.k += 1
        assert self.k <= self.per
        ins.then_inc(self.sem, 1)

    def sync(self):
        self.eng.wait_ge(self.sem, self.base + self.k)


def groups(eng, n, start=0, written=None, ended=0):
    written = start + 1 if written is None else written

    def run(body):
        for g in range(start, written):
            body(g)
        with eng.Fori(written, n - ended) as g:
            body(g)
        for g in range(n - ended, n):
            body(g)

    return run


def reuse(eng, sem, n):
    if not isinstance(n, int) or n > 0:
        eng.wait_ge(sem, n)


def apart(eng, passed):
    eng.sem_inc(passed, 1)


def gnn_kernel(nc, A, out):
    ctx = ExitStack()
    with ctx:
        build(nc, ctx, A, out)


def build(nc, ctx, A, out):
    def dram(name, shape, dt):
        return nc.dram_tensor(name, shape, dt).ap()

    def keep(name, shape, dt=F32):
        return ctx.enter_context(nc.sbuf_tensor(name, shape, dt))

    own_sems = []

    def sem(name):
        own_sems.append(nc.alloc_semaphore(name))
        return own_sems[-1]

    @contextmanager
    def stage():
        with ExitStack() as ph:
            yield ph
        nc.clear_and_free_semaphores(own_sems)
        own_sems.clear()
        nc.all_engine_barrier()

    bank = [ctx.enter_context(nc.psum_tensor(f"psum{i}", [P, U, CH], F32)) for i in range(2)]

    dst_line = dram("dst_line", [EP + 2], I32)
    table = dram("table", [NP, 1], I32)
    dense_mask = dram("dense_mask", [GD * 16, P], BF16)
    edge_mask = dram("edge_mask", [ET, P], BF16)
    keep_line = dram("keep_line", [ET, P], BF16)
    pad_line = dram("pad_line", [1, EP], F32)
    attr_t = dram("attr_t", [EA + EB, EP], F32)
    zd, hd = dram("zd", [P, NP], F32), dram("hd", [P, NP], F32)
    ze, he = dram("ze", [P, GE * GRP], F32), dram("he", [P, GE * GRP], F32)
    xe = dram("xe", [GE * GRP, P], F32)
    agg = [dram(f"agg{i}", [EP + P, P], F32) for i in range(2)]
    x2d = dram("x2d", [EP + P, P], F32)
    gathered = dram("gathered", [EP, P], F32)
    attn_t, v_t = dram("attn_t", [P, EP], F32), dram("v_t", [P, EP], F32)

    x = A["x"]

    def x_half(ap, k):
        return ap[bass.ds(k * HALF, HALF), :].rearrange("(p j) f -> p (j f)", p=P)

    def x_tail(ap):
        k0 = (2 * GD - 1) * HALF
        return ap[k0:N, :].rearrange("(p j) f -> p (j f)", p=TAIL_P)

    def tiles(ap, row, n):
        return ap[bass.ds(row, n * P), :].rearrange("(t p) f -> p t f", p=P)

    ident = keep("ident", [P, P])
    w_e = keep("w_e", [P, LAYERS, P])
    w1, w2 = keep("w1", [P, LAYERS, P]), keep("w2", [P, LAYERS, P])
    cols = keep("cols", [P, 5 * LAYERS])
    be, b1, b2, gamma, beta = (cols[:, LAYERS * k:LAYERS * k + LAYERS] for k in range(5))
    wq, wk, wv, wo = (keep(n, [P, P]) for n in ("wq", "wk", "wv", "wo"))
    wm = keep("wm", [P, 2, P])
    w_bias = keep("w_bias", [P, P])
    w_bias4 = keep("w_bias4", [EB, H])
    heads = keep("heads", [P, P])
    wg1, wg2 = keep("wg1", [P, P]), keep("wg2", [P, P])
    gcols = keep("gcols", [P, 3])
    b2_row = keep("b2_row", [P, P])
    w_om = keep("w_om", [P, P])
    c_row = keep("c_row", [P, U, P])
    c_parts = keep("c_parts", [P, U, P], BF16)
    three = keep("three", [P, P], BF16)
    tenth = keep("tenth", [P, P])
    row0 = keep("row0", [P, P])
    big0 = keep("big0", [P, P], BF16)
    eps = keep("eps", [P, 1])
    src_i, gdst_i, put_i, src_e, dst_e, num_i = (
        keep(n, [P, ET], I32) for n in ("src_i", "gdst_i", "put_i", "src_e", "dst_e", "num_i"))
    rcount = keep("rcount", [P, ET])
    stat_all = keep("stat_all", [P, GD * U + GE * 2, 6])
    norm_a, norm_c = keep("norm_a", [P, LAYERS]), keep("norm_c", [P, LAYERS])
    top = keep("top", [P, 2])

    passed = ctx.enter_context(nc.semaphore("passed"))

    with stage() as ph:
        def tmp(name, shape, dt=F32):
            return ph.enter_context(nc.sbuf_tensor(name, shape, dt))

        wo_t = tmp("wo_t", [P, P])
        bm_row = tmp("bm_row", [1, P])
        part = tmp("part", [1, 3, P], BF16)
        left = tmp("left", [1, 2, P])
        split = sem("c_split")
        loaded, zeroed, made, turned, did = (sem("c_" + n) for n in ("loaded", "zeroed", "made", "turned", "did"))
        block = ph.enter_context(nc.Block())
        loads = [(w_e[0:EA, :, :], A["L0_gnn_We"].rearrange("l e h -> e l h")),
                 (w1[:, :, :], A["L0_gnn_W1"].rearrange("l e h -> e l h")),
                 (w2[:, :, :], A["L0_gnn_W2"].rearrange("l e h -> e l h"))]
        for k, n in enumerate(("be", "b1", "b2", "gamma", "beta")):
            loads.append((cols[:, LAYERS * k:LAYERS * k + LAYERS], A["L0_gnn_" + n].rearrange("l h -> h l")))
        for t, n in ((wq, "Wq"), (wk, "Wk"), (wv, "Wv"), (wo, "Wo")):
            loads.append((t[:, :], A["L2_gnn_" + n]))
        loads += [(wm[:, :, :], A["L2_gnn_Wm"].rearrange("(a k) h -> k a h", a=2)),
                  (w_bias4[:, :], A["L2_gnn_We"]),
                  (wg1[:, :], A["L3_gnn_W1"]), (wg2[:, :], A["L3_gnn_W2"]),
                  (gcols[:, 0:1], A["L3_gnn_b1"].rearrange("(h a) -> h a", a=1)),
                  (gcols[:, 1:2], A["L3_gnn_b2"].rearrange("(h a) -> h a", a=1)),
                  (gcols[:, 2:3], A["L2_gnn_bo"].rearrange("(h a) -> h a", a=1)),
                  (bm_row[:, :], A["L2_gnn_bm"].rearrange("(a h) -> a h", a=1)),
                  (b2_row[:, :], A["L3_gnn_b2"].rearrange("(a h) -> a h", a=1).to_broadcast([P, P]))]

        @block.sync
        def _(sp):
            sp.wait_ge(zeroed, 1)
            with nc.allow_non_contiguous_dma(reason="biases as columns, once"):
                for to, of in loads:
                    sp.dma_start(to, of).then_inc(loaded, 16)
            sp.wait_ge(loaded, 16 * len(loads))

        @block.gpsimd
        def _(pool):
            pool.memset(w_e[:, :, :], 0.0).then_inc(zeroed, 1)
            pool.memset(ident[:, :], 0.0).then_inc(made, 1)
            pool.wait_ge(made, 1)
            pool.affine_select(out=ident[:, :], in_=ident[:, :], compare_op=ALU.not_equal, fill=1.0,
                               base=0, pattern=[[-1, P]], channel_multiplier=1).then_inc(made, 1)

        @block.vector
        def _(dve):
            for t, v in ((heads, 0.0), (w_bias, 0.0), (row0, 0.0), (big0, 0.0), (eps, EPS)):
                dve.memset(t[:, :], v).then_inc(did, 1)
            dve.memset(c_row[:, :, :], 0.0).then_inc(did, 1)
            dve.wait_ge(did, 6)
            for h in range(H):
                s = slice(h * HD, (h + 1) * HD)
                dve.memset(heads[s, s], HD ** -0.5).then_inc(did, 1)
            dve.memset(row0[0:1, :], 1.0).then_inc(did, 1)
            dve.memset(big0[0:1, :], -1e30).then_inc(did, 1)
            dve.memset(w_bias[HD:HD + 1, :], -1e30).then_inc(did, 1)
            dve.wait_ge(loaded, 16 * len(loads))
            dve.tensor_copy(w_bias[0:EB, :].rearrange("e (h d) -> e h d", h=H),
                            w_bias4[:, :].unsqueeze(2).to_broadcast([EB, H, HD])).then_inc(did, 1)
            dve.wait_ge(turned, 1)
            dve.tensor_copy(wo_t[:, :], bank[0][:, 0, 0:P]).then_inc(did, 1)
            dve.wait_ge(turned, 3)
            dve.tensor_copy(w_om[:, :], bank[0][:, 1, 0:P]).then_inc(did, 1)
            dve.tensor_tensor(c_row[0:1, 0, :], bank[0][0:1, 2, 0:P], bm_row[:, :], ALU.add).then_inc(did, 1)
            dve.wait_ge(did, 17)
            for k in range(1, U):
                dve.tensor_copy(c_row[0:1, k, :], c_row[0:1, 0, :]).then_inc(did, 1)
            dve.memset(c_parts[:, :, :], 0.0).then_inc(split, 1)
            dve.memset(three[:, :], 0.0).then_inc(split, 1)
            dve.tensor_copy(part[:, 0, :], c_row[0:1, 0, :]).then_inc(split, 1)
            dve.wait_ge(split, 3)
            dve.tensor_tensor(left[:, 0, :], c_row[0:1, 0, :], part[:, 0, :], ALU.subtract).then_inc(split, 1)
            dve.wait_ge(split, 4)
            dve.tensor_copy(part[:, 1, :], left[:, 0, :]).then_inc(split, 1)
            dve.wait_ge(split, 5)
            dve.tensor_tensor(left[:, 1, :], left[:, 0, :], part[:, 1, :], ALU.subtract).then_inc(split, 1)
            dve.wait_ge(split, 6)
            dve.tensor_copy(part[:, 2, :], left[:, 1, :]).then_inc(split, 1)
            dve.wait_ge(split, 7)
            for k in range(3):
                dve.memset(three[32 * k:32 * k + 1, :], 1.0).then_inc(split, 1)
                for a in range(U):
                    dve.tensor_copy(c_parts[32 * k:32 * k + 1, a, :], part[:, k, :]).then_inc(split, 1)
            dve.wait_ge(made, 2)
            dve.tensor_scalar(tenth[:, :], ident[:, :], RES, None, ALU.mult).then_inc(split, 1)

        @block.tensor
        def _(pe):
            pe.wait_ge(loaded, 16 * len(loads))
            pe.wait_ge(made, 2)
            pe.transpose(bank[0][:, 0, 0:P], wo[:, :], ident[:, :]).then_inc(turned, 1)
            pe.matmul(bank[0][0:1, 2, 0:P], gcols[:, 2:3], wm[:, 1, :], start=True, stop=True).then_inc(turned, 1)
            pe.wait_ge(did, 15)
            pe.matmul(bank[0][:, 1, 0:P], wo_t[:, :], wm[:, 1, :], start=True, stop=True).then_inc(turned, 1)

    RT = ET // 2
    FULL = E // P
    REST = E - FULL * P
    with stage() as ph:
        def tmp(name, shape, dt=F32):
            return ph.enter_context(nc.sbuf_tensor(name, shape, dt))

        ends = tmp("ends", [1, 2], I32)
        near = tmp("near", [RT, 2, 4, P], I32)
        nearf = tmp("nearf", [RT, 2, 4, P])
        last = tmp("last", [RT, 2, P])
        keepb = tmp("keepb", [RT, 2, P], BF16)
        maskb = tmp("maskb", [RT, 2, P], BF16)
        colf = tmp("colf", [P, 3, ET])
        putf = tmp("putf", [P, ET])
        fill = tmp("fill", [P, NP // P], I32)
        zero, one = tmp("zero", [P, 2 * P]), tmp("one", [1, EP - E])
        l1, l2, l3, zeroed, did, turned, numbered, stored = (
            sem("i_" + n) for n in ("l1", "l2", "l3", "zeroed", "did", "turned", "numbered", "stored"))
        l4, l5 = sem("i_l4"), sem("i_l5")
        block = ph.enter_context(nc.Block())
        @block.gpsimd
        def _(pool):
            pool.iota(num_i[:, :], pattern=[[P, ET]], base=0, channel_multiplier=1).then_inc(numbered, 1)

        @block.sync
        def _(sp):
            sp.wait_ge(zeroed, 7)
            for a, name in ((0, "src"), (1, "dst")):
                v = A[name]
                sp.dma_start(near[:, 0, a, :], v[0:RT * P].rearrange("(t p) -> t p", p=P)).then_inc(l1, 16)
                sp.dma_start(near[0:FULL - RT, 1, a, :],
                             v[RT * P:FULL * P].rearrange("(t p) -> t p", p=P)).then_inc(l1, 16)
                sp.dma_start(near[FULL - RT:FULL - RT + 1, 1, a, 0:REST],
                             v[FULL * P:E].rearrange("(t p) -> t p", t=1)).then_inc(l1, 16)
            sp.dma_start(table.rearrange("(p c) a -> p (c a)", p=P), fill[:, :]).then_inc(l5, 16)
            sp.wait_ge(l5, 16)
            sp.dma_start(table[N:NP, :].rearrange("(p c) a -> p (c a)", p=32), zero[0:32, 0:(NP - N) // 32].bitcast(I32)).then_inc(l5, 16)
            for a in (*agg, x2d):
                sp.dma_start(a[EP:EP + P, :], zero[:, 0:P]).then_inc(l4, 16)
            sp.dma_start(pad_line[0:1, 0:E].rearrange("a (p n) -> (a p) n", p=125),
                         zero[0:125, 0:E // 125]).then_inc(l4, 16)
            sp.dma_start(pad_line[0:1, E:EP], one[:, :]).then_inc(l4, 16)
            sp.dma_start(dst_line[0:1].rearrange("(a b) -> a b", a=1), ends[:, 0:1]).then_inc(l2, 16)
            sp.dma_start(dst_line[EP + 1:EP + 2].rearrange("(a b) -> a b", a=1), ends[:, 1:2]).then_inc(l2, 16)
            sp.wait_ge(l1, 96)
            sp.dma_start(dst_line[1:EP + 1].rearrange("(s t p) -> t s p", s=2, p=P), near[:, :, 1, :]).then_inc(l2, 16)
            sp.wait_ge(l2, 48)
            for a, at in ((2, 0), (3, 2)):
                sp.dma_start(near[:, :, a, :],
                             dst_line[at:at + EP].rearrange("(s t p) -> t s p", s=2, p=P)).then_inc(l3, 16)
            sp.wait_ge(did, 4)
            sp.dma_start(keep_line.rearrange("(s t) p -> t s p", s=2), keepb[:, :, :]).then_inc(stored, 16)
            sp.dma_start(edge_mask.rearrange("(s t) p -> t s p", s=2), maskb[:, :, :]).then_inc(stored, 16)
            sp.wait_ge(stored, 32)
            sp.wait_ge(l4, 80)
            sp.wait_ge(l5, 32)

        @block.vector
        def _(dve):
            dve.memset(near[:, :, 0, :], 0).then_inc(zeroed, 1)
            dve.memset(near[:, :, 1, :], N).then_inc(zeroed, 1)
            dve.memset(ends[:, 0:1], -1).then_inc(zeroed, 1)
            dve.memset(ends[:, 1:2], N).then_inc(zeroed, 1)
            dve.memset(zero[:, :], 0.0).then_inc(zeroed, 1)
            dve.memset(fill[:, :], ZR).then_inc(zeroed, 1)
            dve.memset(one[:, :], 1.0).then_inc(zeroed, 1)
            dve.wait_ge(l3, 32)
            dve.tensor_copy(nearf[:, :, :, :], near[:, :, :, :]).then_inc(did, 1)
            dve.wait_ge(did, 1)
            dve.tensor_tensor(keepb[:, :, :], nearf[:, :, 1, :], nearf[:, :, 2, :], ALU.is_equal).then_inc(did, 1)
            dve.tensor_tensor(maskb[:, :, :], nearf[:, :, 1, :], nearf[:, :, 3, :], ALU.is_equal).then_inc(did, 1)
            dve.tensor_tensor(last[:, :, :], nearf[:, :, 1, :], nearf[:, :, 3, :], ALU.not_equal).then_inc(did, 1)
            dve.wait_ge(turned, 6)
            dve.tensor_copy(colf[:, :, :].rearrange("p a (s t) -> p s a t", s=2),
                            bank[0][:, 0:2, 0:3 * RT].rearrange("p s (a t) -> p s a t", a=3)).then_inc(did, 1)
            dve.wait_ge(did, 5)
            dve.tensor_copy(src_i[:, :], colf[:, 0, :]).then_inc(did, 1)
            dve.tensor_scalar(gdst_i[:, :], colf[:, 1, :], float(N - 1), None, ALU.min).then_inc(did, 1)
            dve.tensor_scalar(putf[:, :], colf[:, 2, :], -float(FAR), float(FAR), ALU.mult, ALU.add).then_inc(did, 1)
            dve.wait_ge(did, 8)
            dve.tensor_tensor(put_i[:, :], putf[:, :], colf[:, 1, :], ALU.add).then_inc(did, 1)

        @block.tensor
        def _(pe):
            pe.wait_ge(did, 4)
            for s in range(2):
                for a, v in enumerate((nearf[:, s, 0, :], nearf[:, s, 1, :], last[:, s, :])):
                    pe.transpose(bank[0][:, s, a * RT:(a + 1) * RT], v, ident[0:RT, 0:RT]).then_inc(turned, 1)

    R = 4
    with stage() as ph:
        def tmp(name, shape, dt=F32):
            return ph.enter_context(nc.sbuf_tensor(name, shape, dt))

        at_i = tmp("at_i", [P, R, 2], I32)
        got = tmp("got", [P, R, 2], I32)
        mrow = tmp("mrow", [P, GD * 16], I32)
        mrowf = tmp("mrowf", [P, GD * 16])
        mask_t = tmp("mask_t", [P, 7, P], BF16)
        slot, took = sem("t_slot"), sem("t_took")
        put = [sem(f"t_put{r}") for r in range(R)]
        look = [sem(f"t_look{r}") for r in range(R)]
        loaded, did, turned, stored = (sem("t_" + n) for n in ("loaded", "did", "turned", "stored"))
        block = ph.enter_context(nc.Block())
        MT = GD * 16 // 7

        @block.gpsimd
        def _(pool):
            @groups(pool, ET // R)
            def _(i):
                for r in range(R):
                    pool.wait_ge(put[r], 16 * i)
                    pool.tensor_copy(at_i[:, r, 0:1], put_i[:, bass.ds(i * R + r, 1)]).then_inc(slot, 1)
                    pool.tensor_copy(at_i[:, r, 1:2], num_i[:, bass.ds(i * R + r, 1)]).then_inc(slot, 1)
                    pool.wait_ge(slot, (i * R + r) * 2 + 2)
                    apart(pool, passed)
                    pool.indirect_dma_start(table[:, :], bass.IndirectOffsetOnAxis(ap=at_i[:, r, 0:1], axis=0),
                                            at_i[:, r, 1:2], None, bounds_check=N - 1,
                                            oob_is_err=False).then_inc(put[r], 16)
            for r in range(R):
                pool.wait_ge(put[r], 16 * (ET // R))
            @groups(pool, ET // R)
            def _(i):
                for r in range(R):
                    for a, (ids, found) in enumerate(((src_i, src_e), (gdst_i, dst_e))):
                        pool.wait_ge(took, i * R * 2)
                        pool.tensor_copy(at_i[:, r, a:a + 1], ids[:, bass.ds(i * R + r, 1)]).then_inc(slot, 1)
                for r in range(R):
                    pool.wait_ge(slot, 2 * ET + (i + 1) * R * 2)
                    apart(pool, passed)
                    for a in range(2):
                        pool.indirect_dma_start(got[:, r, a:a + 1], None, table[:, :],
                                                bass.IndirectOffsetOnAxis(ap=at_i[:, r, a:a + 1], axis=0),
                                                bounds_check=N - 1, oob_is_err=False).then_inc(look[r], 16)
                for r in range(R):
                    pool.wait_ge(look[r], 32 * i + 32)
                    for a, (ids, found) in enumerate(((src_i, src_e), (gdst_i, dst_e))):
                        pool.tensor_copy(found[:, bass.ds(i * R + r, 1)], got[:, r, a:a + 1]).then_inc(took, 1)

        @block.sync
        def _(sp):
            for r in range(R):
                sp.wait_ge(put[r], 16 * (ET // R))
            sp.dma_start(mrow[:, :].rearrange("p (h j) -> p h j", j=8),
                         table.rearrange("(h p j) a -> p h (j a)", p=P, j=8)).then_inc(loaded, 16)
            sp.wait_ge(did, 2 + 7)
            sp.dma_start(dense_mask.rearrange("(k r) p -> r k p", k=7), mask_t[0:MT, :, :]).then_inc(stored, 16)
            sp.wait_ge(stored, 16)

        @block.vector
        def _(dve):
            dve.wait_ge(loaded, 16)
            dve.tensor_copy(mrowf[:, :], mrow[:, :]).then_inc(did, 1)
            dve.wait_ge(did, 1)
            dve.tensor_scalar(mrowf[:, :], mrowf[:, :], float(ZR), None, ALU.not_equal).then_inc(did, 1)
            dve.wait_ge(did, 2)
            for k in range(7):
                dve.wait_ge(turned, k + 1)
                dve.tensor_copy(mask_t[0:MT, k, :], bank[k // 4][0:MT, k % 4, 0:P]).then_inc(did, 1)

        @block.tensor
        def _(pe):
            pe.wait_ge(did, 2)
            for k in range(7):
                pe.transpose(bank[k // 4][0:MT, k % 4, 0:P], mrowf[:, k * MT:(k + 1) * MT],
                             ident[:, :]).then_inc(turned, 1)

    with stage() as ph:
        def tmp(name, shape, dt=F32):
            return ph.enter_context(nc.sbuf_tensor(name, shape, dt))

        attr = tmp("attr", [P, 8, P])
        attr_out = tmp("attr_out", [EA + EB, HALF])
        kept = tmp("kept", [P, HALF], BF16)
        ones = tmp("ones", [P, CH])
        run = tmp("run", [P, 2, CH])
        carry = tmp("carry", [P, 1])
        loaded, loadk, did, turned, moved, counted, picked, stored = (
            sem("e_" + n) for n in ("loaded", "loadk", "did", "turned", "moved", "counted", "picked", "stored"))
        fresh = sem("e_fresh")
        block = ph.enter_context(nc.Block())
        WHOLE = (E - (GE - 1) * HALF) // P

        @block.sync
        def _(sp):
            def load(i, whole=8, rest=0):
                sp.wait_ge(turned, 2 * i)
                for a, name in ((slice(0, EA), "edge_attr_32"), (slice(EA, EA + EB), "edge_attr_3")):
                    v = A[name]
                    sp.dma_start(attr[:, 0:whole, a], tiles(v, i * HALF, whole)).then_inc(loaded, 16)
                    if rest:
                        sp.dma_start(attr[0:rest, whole, a], v[i * HALF + whole * P:E, :]).then_inc(loaded, 16)
                sp.wait_ge(counted, 2 * i)
                sp.dma_start(kept[:, :], keep_line[bass.ds(i * 8, 8), :].rearrange("(a t) p -> a (t p)", a=1)
                             .to_broadcast([P, HALF])).then_inc(loadk, 16)

            def store(i):
                sp.wait_ge(moved, 2 * i + 2)
                sp.dma_start(attr_t[:, bass.ds(i * HALF, HALF)], attr_out[:, :]).then_inc(stored, 16)

            sp.wait_ge(fresh, 1)
            with nc.allow_non_contiguous_dma(reason="three edge features"):
                load(0)
                with sp.Fori(0, GE - 2) as i:
                    load(i + 1)
                    store(i)
                load(GE - 1, WHOLE, E - (GE - 1) * HALF - WHOLE * P)
                store(GE - 2)
            store(GE - 1)
            sp.wait_ge(stored, 16 * GE)

        def each(eng, body):
            body(0, False)
            with eng.Fori(1, GE - 1) as i:
                body(i, False)
            body(GE - 1, True)

        @block.tensor
        def _(pe):
            def body(i, tail):
                for c in range(2):
                    pe.wait_ge(loaded, 32 * i + (64 if tail else 32))
                    reuse(pe, moved, 2 * i + c - 1)
                    for j in range(4):
                        t = pe.transpose(bank[0][:, c, j * P:(j + 1) * P], attr[:, 4 * c + j, :], ident[:, :])
                    t.then_inc(turned, 1)
                for c in range(2):
                    pe.wait_ge(counted, 2 * i + c + 1)
                    reuse(pe, did, 2 * i + c - 1)
                    for j in range(4):
                        t = pe.matmul(bank[1][:, c, j:j + 1], run[:, c, j * P:(j + 1) * P], row0[:, 0:1],
                                      start=True, stop=True)
                    t.then_inc(picked, 1)

            each(pe, body)

        @block.scalar
        def _(act):
            def body(i, tail):
                for c in range(2):
                    act.wait_ge(turned, 2 * i + c + 1)
                    act.wait_ge(stored, 16 * i)
                    act.activation(attr_out[:, c * CH:(c + 1) * CH], bank[0][0:EA + EB, c, :],
                                   ACT.Copy).then_inc(moved, 1)

            each(act, body)

        @block.vector
        def _(dve):
            dve.memset(attr[:, :, :], 0.0).then_inc(fresh, 1)
            dve.memset(ones[:, :], 1.0).then_inc(fresh, 1)
            dve.memset(carry[:, :], 0.0).then_inc(fresh, 1)
            dve.wait_ge(fresh, 3)

            def body(i, tail):
                dve.wait_ge(loadk, 16 * i + 16)
                dve.wait_ge(picked, 2 * i)
                for c in range(2):
                    if c:
                        dve.wait_ge(counted, 2 * i + c)
                    else:
                        dve.wait_ge(fresh, i + 3)
                    dve.tensor_tensor_scan(run[:, c, :], kept[:, c * CH:(c + 1) * CH], ones[:, :],
                                           run[:, 0, CH - 1:CH] if c else carry[:, :],
                                           ALU.mult, ALU.add).then_inc(counted, 1)
                dve.wait_ge(counted, 2 * i + 2)
                dve.tensor_copy(carry[:, :], run[:, 1, CH - 1:CH]).then_inc(fresh, 1)
                for c in range(2):
                    dve.wait_ge(picked, 2 * i + c + 1)
                    dve.tensor_scalar(rcount[:, bass.ds(i * 8 + c * 4, 4)], bank[1][:, c, 0:4], 1.0, None,
                                      ALU.mult).then_inc(did, 1)

            each(dve, body)
            dve.wait_ge(did, 2 * GE)
            dve.reciprocal(rcount[:, :], rcount[:, :]).then_inc(did, 1)

    def ln_sums(dve, steps, x_, st, mv, n, var_ready):
        for t in range(n):
            steps.did(dve.bn_stats(st[:, t, :], x_[:, t, :]))
        steps.sync()
        steps.did(dve.tensor_tensor(mv[:, 0, 0:n], st[:, 0:n, 1], st[:, 0:n, 4], ALU.add))
        steps.did(dve.tensor_tensor(mv[:, 1, 0:n], st[:, 0:n, 1], st[:, 0:n, 4], ALU.subtract))
        steps.did(dve.tensor_tensor(mv[:, 2, 0:n], st[:, 0:n, 2], st[:, 0:n, 5], ALU.add))
        steps.sync()
        steps.did(dve.tensor_scalar(mv[:, 0, 0:n], mv[:, 0, 0:n], -0.5, None, ALU.mult))
        steps.did(dve.tensor_tensor(mv[:, 1, 0:n], mv[:, 1, 0:n], mv[:, 1, 0:n], ALU.mult))
        steps.sync()
        dve.scalar_tensor_tensor(mv[:, 2, 0:n], mv[:, 1, 0:n], P / 4.0, mv[:, 2, 0:n], ALU.mult,
                                 ALU.add).then_inc(var_ready, 1)

    def ln_root(act, mv, n, sd_ready):
        act.activation(mv[:, 3, 0:n], mv[:, 2, 0:n], ACT.Sqrt, scale=1.0 / P, bias=eps[:, :]).then_inc(sd_ready, 1)

    def ln_apply(dve, steps, out_, x_, mv, n, normed, each=4):
        steps.did(dve.reciprocal(mv[:, 4, 0:n], mv[:, 3, 0:n]))
        steps.sync()
        for t in range(n):
            r = dve.tensor_scalar(out_[:, t, :], x_[:, t, :], mv[:, 0, t:t + 1], mv[:, 4, t:t + 1],
                                  ALU.add, ALU.mult)
            if t % each == each - 1:
                r.then_inc(normed, 1)

    LN_STEPS = 14

    def first(dense):
        G = GD if dense else GE
        tag = "fd_" if dense else "fe_"
        with stage() as ph:
            def tmp(name, shape, dt=F32):
                return ph.enter_context(nc.sbuf_tensor(tag + name, shape, dt))

            def sm(name):
                return sem(tag + name)

            xin, xn = tmp("xin", [P, 16, P]), tmp("xn", [P, 16, P])
            st = [tmp(f"st{k}", [P, 8, 6]) for k in range(2)]
            mv = [tmp(f"mv{k}", [P, 5, 8]) for k in range(2)]
            h = tmp("h", [P, U, CH])
            loaded = [sm(f"loaded{k}") for k in range(2)]
            stored_h = [sm(f"stored_h{k}") for k in range(2)]
            own, var_ready, sd_ready, normed, turned, h_ready = (
                sm(n) for n in ("own", "var", "sd", "normed", "turned", "h"))
            if dense:
                hid, z = tmp("hid", [P, U, CH]), tmp("z", [P, U, CH])
                zst = tmp("zst", [P, U, 6])
                mask = tmp("mask", [P, GRP], BF16)
                loaded_m, mm1, hid_ready, mm2, z_ready, z_stat, z_kept, mzero = (
                    sm(n) for n in ("loaded_m", "mm1", "hid", "mm2", "z", "zstat", "zkept", "mzero"))
                stored_z = [sm(f"stored_z{k}") for k in range(2)]
            else:
                at_i = tmp("at_i", [P, 16], I32)
                slot, stored_x = sm("slot"), [sm(f"stored_x{k}") for k in range(2)]
            block = ph.enter_context(nc.Block())
            LOAD = 16 if dense else 16 * 8

            @block.sync
            def _(sp):
                def store(g):
                    for k in range(2):
                        if not dense:
                            sp.wait_ge(loaded[k], LOAD * g + LOAD)
                            sp.dma_start(tiles(xe, g * GRP + k * HALF, 8), xin[:, 8 * k:8 * k + 8, :])\
                              .then_inc(stored_x[k], 16)
                        sp.wait_ge(h_ready, 4 * g + 2 * k + 2)
                        apart(sp, passed)
                        sp.dma_start((hd if dense else he)[:, bass.ds(g * GRP + k * HALF, HALF)],
                                     h[:, 2 * k:2 * k + 2, :].rearrange("p c n -> p (c n)")).then_inc(stored_h[k], 16)
                    for k in range(2 if dense else 0):
                        sp.wait_ge(z_ready, 4 * g + 2 * k + 2)
                        sp.dma_start(zd[:, bass.ds(g * GRP + k * HALF, HALF)],
                                     z[:, 2 * k:2 * k + 2, :].rearrange("p c n -> p (c n)")).then_inc(stored_z[k], 16)

                with sp.Fori(0, G) as g:
                    store(g)
                for k in range(2):
                    sp.wait_ge(stored_h[k], 16 * G)
                    sp.wait_ge((stored_z if dense else stored_x)[k], 16 * G)

            if not dense:
                @block.gpsimd
                def _(pool):
                    @groups(pool, G)
                    def _(g):
                        for k, ids in enumerate((gdst_i, src_i)):
                            pool.wait_ge(loaded[k], LOAD * g)
                            pool.tensor_copy(at_i[:, 8 * k:8 * k + 8], ids[:, bass.ds(g * 8, 8)]).then_inc(slot, 1)
                            pool.wait_ge(slot, 2 * g + k + 1)
                            pool.wait_ge(normed, 4 * g)
                            pool.wait_ge(stored_x[k], 16 * g)
                            apart(pool, passed)
                            for t in range(8 * k, 8 * k + 8):
                                pool.indirect_dma_start(xin[:, t, :], None, x[:, :],
                                                        bass.IndirectOffsetOnAxis(ap=at_i[:, t:t + 1], axis=0),
                                                        bounds_check=N - 1, oob_is_err=False).then_inc(loaded[k], 16)

            @block.vector
            def _(dve):
                steps = Steps(dve, own, 2 * LN_STEPS)

                def normalise(g):
                    steps.at(g)
                    for k in range(2):
                        dve.wait_ge(loaded[k], LOAD * g + LOAD)
                        ln_sums(dve, steps, xin[:, 8 * k:8 * k + 8, :], st[k], mv[k], 8, var_ready)
                    for k in range(2):
                        dve.wait_ge(sd_ready, 2 * g + k + 1)
                        reuse(dve, turned, 4 * g + 2 * k - 2)
                        ln_apply(dve, steps, xn[:, 8 * k:8 * k + 8, :], xin[:, 8 * k:8 * k + 8, :], mv[k], 8, normed)
                    assert steps.k == steps.per

                if not dense:
                    @groups(dve, G)
                    def _(g):
                        normalise(g)
                    return
                dve.memset(mask[:, :], 0.0).then_inc(mzero, 1)
                normalise(0)

                @groups(dve, G, 1, 2)
                def _(g):
                    normalise(g)
                    z_out(dve, g - 1, mm2, stored_z, z, zst, z_ready, z_stat, z_kept, 0)

                z_out(dve, G - 1, mm2, stored_z, z, zst, z_ready, z_stat, z_kept, 0)

            @block.scalar
            def _(act):
                def load(g, tail=False):
                    for k in range(2):
                        reuse(act, normed, 4 * g + 2 * k - 2)
                        if tail and k:
                            act.dma_start(xin[0:TAIL_P, 8:16, :].rearrange("p j f -> p (j f)"),
                                         x_tail(x)).then_inc(loaded[k], 16)
                        else:
                            act.dma_start(xin[:, 8 * k:8 * k + 8, :].rearrange("p j f -> p (j f)"),
                                         x_half(x, 2 * g + k)).then_inc(loaded[k], 16)
                    act.wait_ge(mm1, 4 * g)
                    act.dma_start(mask[0:1, :], dense_mask[bass.ds(g * 16, 16), :]
                                 .rearrange("(a j) p -> a (j p)", a=1)).then_inc(loaded_m, 16)

                if dense:
                    act.wait_ge(mzero, 1)
                    load(0)

                @groups(act, G, ended=2)
                def _(g):
                    static = isinstance(g, int)
                    for k in range(2):
                        act.wait_ge(var_ready, 2 * g + k + 1)
                        ln_root(act, mv[k], 8, sd_ready)
                    for c in range(U):
                        act.wait_ge(turned, 4 * g + c + 1)
                        act.wait_ge(stored_h[c // 2], 16 * g)
                        if dense:
                            reuse(act, mm1, 4 * g + c - 3)
                        act.activation(h[:, c, :], bank[0][:, c, :], ACT.Relu).then_inc(h_ready, 1)
                    if dense:
                        if not (static and g == G - 1):
                            load(g + 1, tail=static and g == G - 2)
                        hidden(act, g, 0, mm1, mm2, hid, hid_ready)

            @block.tensor
            def _(pe):
                @groups(pe, G)
                def _(g):
                    for c in range(U):
                        pe.wait_ge(normed, 4 * g + c + 1)
                        reuse(pe, h_ready, 4 * g + c - 3)
                        for j in range(4):
                            t = pe.transpose(bank[0][:, c, j * P:(j + 1) * P], xn[:, 4 * c + j, :], ident[:, :])
                        t.then_inc(turned, 1)
                    if dense:
                        products(pe, g, 0, h, h_ready, z_ready, mask, loaded_m, (0, 1, 2, 3), hid, hid_ready, mm1, mm2)

    def products(pe, g, l, h, h_ready, z_free, mask, loaded_m, masked, hid, hid_ready, mm1, mm2):
        for c in range(U):
            pe.wait_ge(h_ready, 4 * g + c + 1)
            reuse(pe, z_free, 4 * g + c - 3)
            m = pe.matmul(bank[1][:, c, :], w1[:, l, :], h[:, c, :], start=True, stop=c not in masked)
            if c in masked:
                if c == masked[0]:
                    pe.wait_ge(loaded_m, 16 * g + 16)
                m = pe.matmul(bank[1][:, c, :], big0[:, :], mask[:, c * CH:(c + 1) * CH], start=False, stop=True)
            m.then_inc(mm1, 1)
        for c in range(U):
            pe.wait_ge(hid_ready, 4 * g + c + 1)
            pe.matmul(bank[1][:, c, :], w2[:, l, :], hid[:, c, :], start=True, stop=True).then_inc(mm2, 1)

    def hidden(act, g, l, mm1, mm2, hid, hid_ready):
        for c in range(U):
            act.wait_ge(mm1, 4 * g + c + 1)
            reuse(act, mm2, 4 * g + c - 3)
            act.activation(hid[:, c, :], bank[1][:, c, :], ACT.Relu, bias=b1[:, l:l + 1]).then_inc(hid_ready, 1)

    def z_out(dve, g, mm2, stored_z, z, zst, z_ready, z_stat, z_kept, edge):
        with_stats = 2 if edge else U
        for c in range(U):
            dve.wait_ge(mm2, 4 * g + c + 1)
            dve.wait_ge(stored_z[c // 2], 16 * g)
            if c < with_stats:
                if c == 0:
                    dve.wait_ge(z_kept, g)
                dve.bn_stats(zst[:, c, :], bank[1][:, c, :]).then_inc(z_stat, 1)
            dve.tensor_copy(z[:, c, :], bank[1][:, c, :]).then_inc(z_ready, 1)
        dve.wait_ge(z_stat, with_stats * (g + 1))
        to = (stat_all[:, bass.ds(GD * U + g * 2, 2), :] if edge else stat_all[:, bass.ds(g * U, U), :])
        dve.tensor_scalar(to, zst[:, 0:with_stats, :], 1.0, None, ALU.mult).then_inc(z_kept, 1)

    def layer(l, dense):
        G = GD if dense else GE
        tag = f"l{l}{'d' if dense else 'e'}_"
        bn = l > 0
        zt, ht = (zd, hd) if dense else (ze, he)
        with stage() as ph:
            def tmp(name, shape, dt=F32):
                return ph.enter_context(nc.sbuf_tensor(tag + name, shape, dt))

            def sm(name):
                return sem(tag + name)

            hin = tmp("hin", [P, U, CH])
            hid, z, zst = tmp("hid", [P, U, CH]), tmp("z", [P, U, CH]), tmp("zst", [P, U, 6])
            mask = tmp("mask", [P, GRP], BF16)
            loaded_h = [sm(f"loaded_h{k}") for k in range(2)]
            stored_z = [sm(f"stored_z{k}") for k in range(2)]
            loaded_m, mm1, hid_ready, mm2, z_ready, z_stat, z_kept, mzero, x_ready = (
                sm(n) for n in ("loaded_m", "mm1", "hid", "mm2", "z", "zstat", "zkept", "mzero", "x"))
            if bn:
                zin, unit, hout = tmp("zin", [P, U, CH]), tmp("unit", [P, U, CH]), tmp("hout", [P, U, CH])
                loaded_z = [sm(f"loaded_z{k}") for k in range(2)]
                stored_h = [sm(f"stored_h{k}") for k in range(2)]
                unit_ready, h_ready = sm("unit"), sm("h")
            if not dense:
                sums, summed = tmp("sums", [P, 16, P]), tmp("summed", [P, U, CH])
                at_i = tmp("at_i", [P, 8], I32)
                slot, turned = sm("slot"), sm("turned")
                got = [sm(f"got{k}") for k in range(3)]
            else:
                summed, turned = (hout, None) if bn else (None, None)
            block = ph.enter_context(nc.Block())
            h_used = h_ready if bn else x_ready

            @block.sync
            def _(sp):
                def store(g):
                    for k in range(2 if bn else 0):
                        sp.wait_ge(h_ready, 4 * g + 2 * k + 2)
                        sp.dma_start(ht[:, bass.ds(g * GRP + k * HALF, HALF)],
                                     hout[:, 2 * k:2 * k + 2, :].rearrange("p c n -> p (c n)")).then_inc(stored_h[k], 16)
                    for k in range(2):
                        sp.wait_ge(z_ready, 4 * g + 2 * k + 2)
                        sp.dma_start(zt[:, bass.ds(g * GRP + k * HALF, HALF)],
                                     z[:, 2 * k:2 * k + 2, :].rearrange("p c n -> p (c n)")).then_inc(stored_z[k], 16)

                with sp.Fori(0, G) as g:
                    store(g)
                for k in range(2):
                    if bn:
                        sp.wait_ge(stored_h[k], 16 * G)
                    sp.wait_ge(stored_z[k], 16 * G)

            if not dense:
                @block.gpsimd
                def _(pool):
                    @groups(pool, G)
                    def _(g):
                        pool.wait_ge(got[1], 64 * g)
                        pool.wait_ge(got[2], 64 * g)
                        pool.tensor_copy(at_i[:, :], src_e[:, bass.ds(g * 8, 8)]).then_inc(slot, 1)
                        pool.wait_ge(slot, g + 1)
                        pool.wait_ge(turned, 4 * g)
                        apart(pool, passed)
                        for t in range(8):
                            pool.indirect_dma_start(sums[:, 8 + t, :], None, agg[0][:, :],
                                                    bass.IndirectOffsetOnAxis(ap=at_i[:, t:t + 1], axis=0),
                                                    bounds_check=ZR, oob_is_err=False).then_inc(got[1 + t // 4], 16)

            @block.scalar
            def _(act):
                def load(g):
                    for k in range(2):
                        cols_ = bass.ds(g * GRP + k * HALF, HALF)
                        if bn:
                            reuse(act, unit_ready, 4 * g + 2 * k - 2)
                            act.dma_start(zin[:, 2 * k:2 * k + 2, :].rearrange("p c n -> p (c n)"),
                                         zt[:, cols_]).then_inc(loaded_z[k], 16)
                        reuse(act, h_used, 4 * g + 2 * k - 2)
                        act.dma_start(hin[:, 2 * k:2 * k + 2, :].rearrange("p c n -> p (c n)"),
                                     ht[:, cols_]).then_inc(loaded_h[k], 16)
                    if dense:
                        act.wait_ge(mm1, 4 * g)
                        act.dma_start(mask[0:1, :], dense_mask[bass.ds(g * 16, 16), :]
                                     .rearrange("(a j) p -> a (j p)", a=1)).then_inc(loaded_m, 16)
                    else:
                        act.wait_ge(turned, 4 * g)
                        act.dma_start(sums[:, 0:8, :], tiles(agg[0], g * HALF, 8)).then_inc(got[0], 16)
                        act.wait_ge(mm1, 4 * g)
                        act.dma_start(mask[0:1, 0:HALF], edge_mask[bass.ds(g * 8, 8), :]
                                     .rearrange("(a j) p -> a (j p)", a=1)).then_inc(loaded_m, 16)

                act.wait_ge(mzero, 1)
                load(0)

                @groups(act, G, ended=1)
                def _(g):
                    for c in range(U if bn else 0):
                        act.wait_ge(loaded_z[c // 2], 16 * g + 16)
                        reuse(act, h_ready, 4 * g + c - 3)
                        act.activation(unit[:, c, :], zin[:, c, :], ACT.Relu, bias=norm_c[:, l - 1:l],
                                       scale=norm_a[:, l - 1:l]).then_inc(unit_ready, 1)
                    if not (isinstance(g, int) and g == G - 1):
                        load(g + 1)
                    hidden(act, g, l, mm1, mm2, hid, hid_ready)

            @block.vector
            def _(dve):
                def combine(g):
                    for c in range(U if bn else 0):
                        dve.wait_ge(loaded_h[c // 2], 16 * g + 16)
                        dve.wait_ge(unit_ready, 4 * g + c + 1)
                        dve.wait_ge(stored_h[c // 2], 16 * g)
                        reuse(dve, mm1 if dense else x_ready, 4 * g + c - 3)
                        dve.scalar_tensor_tensor(hout[:, c, :], hin[:, c, :], RES, unit[:, c, :], ALU.mult,
                                                 ALU.add).then_inc(h_ready, 1)
                    for c in range(0 if dense else U):
                        if bn:
                            dve.wait_ge(h_ready, 4 * g + c + 1)
                        else:
                            dve.wait_ge(loaded_h[c // 2], 16 * g + 16)
                        dve.wait_ge(turned, 4 * g + c + 1)
                        reuse(dve, mm1, 4 * g + c - 3)
                        dve.tensor_tensor(summed[:, c, :], (hout if bn else hin)[:, c, :], bank[0][:, c, :],
                                          ALU.add).then_inc(x_ready, 1)

                dve.memset(mask[:, :], 0.0).then_inc(mzero, 1)
                combine(0)

                @groups(dve, G, 1, 2)
                def _(g):
                    combine(g)
                    z_out(dve, g - 1, mm2, stored_z, z, zst, z_ready, z_stat, z_kept, not dense)

                z_out(dve, G - 1, mm2, stored_z, z, zst, z_ready, z_stat, z_kept, not dense)

            @block.tensor
            def _(pe):
                @groups(pe, G)
                def _(g):
                    for c in range(0 if dense else U):
                        pe.wait_ge(got[0 if c < 2 else c - 1], (16 if c < 2 else 64) * (g + 1))
                        reuse(pe, x_ready, 4 * g + c - 3)
                        for j in range(4):
                            t = pe.transpose(bank[0][:, c, j * P:(j + 1) * P], sums[:, 4 * c + j, :], ident[:, :])
                        t.then_inc(turned, 1)
                    products(pe, g, l, summed, h_ready if dense else x_ready, z_ready, mask, loaded_m,
                             (0, 1, 2, 3) if dense else (0, 1), hid, hid_ready, mm1, mm2)

    def messages(l):
        bn = l > 0
        tag = f"m{l}_"
        with stage() as ph:
            def tmp(name, shape, dt=F32):
                return ph.enter_context(nc.sbuf_tensor(tag + name, shape, dt))

            hin, attr = tmp("hin", [P, 2, CH]), tmp("attr", [P, 2, CH])
            kept = tmp("kept", [P, 2, CH], BF16)
            pre, msg, run, rows = (tmp(n, [P, 2, CH]) for n in ("pre", "msg", "run", "rows"))
            carry = tmp("carry", [P, 1])
            loaded_h, loaded_a, loaded_k, unit_ready, h_ready, mm, pre_ready, msg_ready, scanned, carried, turned, \
                row_ready, stored, zeroed = (sem(tag + n) for n in (
                    "loaded_h", "loaded_a", "loaded_k", "unit", "h", "mm", "pre", "msg", "scanned", "carried",
                    "turned", "row", "stored", "zeroed"))
            if bn:
                zin, unit, hout = tmp("zin", [P, 2, CH]), tmp("unit", [P, 2, CH]), tmp("hout", [P, 2, CH])
                loaded_z = sem(tag + "loaded_z")
            block = ph.enter_context(nc.Block())

            @block.sync
            def _(sp):
                def load(g):
                    s_cols = bass.ds(g * GRP + HALF, HALF)
                    if bn:
                        sp.wait_ge(unit_ready, 2 * g)
                        sp.dma_start(zin[:, :, :].rearrange("p c n -> p (c n)"), ze[:, s_cols]).then_inc(loaded_z, 16)
                    sp.wait_ge(h_ready if bn else pre_ready, 2 * g)
                    sp.dma_start(hin[:, :, :].rearrange("p c n -> p (c n)"), he[:, s_cols]).then_inc(loaded_h, 16)
                    sp.wait_ge(mm, 2 * g)
                    sp.dma_start(attr[0:EA, :, :].rearrange("p c n -> p (c n)"),
                                 attr_t[0:EA, bass.ds(g * HALF, HALF)]).then_inc(loaded_a, 16)
                    sp.wait_ge(scanned, 2 * g)
                    sp.dma_start(kept[:, :, :].rearrange("p c n -> p (c n)"), keep_line[bass.ds(g * 8, 8), :]
                                 .rearrange("(a t) p -> a (t p)", a=1).to_broadcast([P, HALF])).then_inc(loaded_k, 16)

                def store(g):
                    sp.wait_ge(row_ready, 2 * g + 2)
                    sp.dma_start(tiles(agg[0], g * HALF, 8),
                                 rows[:, :, :].rearrange("p c (t f) -> p (c t) f", f=P)).then_inc(stored, 16)

                sp.wait_ge(zeroed, 1)
                load(0)
                with sp.Fori(0, GE - 1) as g:
                    load(g + 1)
                    store(g)
                store(GE - 1)
                sp.wait_ge(stored, 16 * GE)

            @block.scalar
            def _(act):
                @groups(act, GE)
                def _(g):
                    for c in range(2 if bn else 0):
                        act.wait_ge(loaded_z, 16 * g + 16)
                        reuse(act, h_ready, 2 * g + c - 1)
                        act.activation(unit[:, c, :], zin[:, c, :], ACT.Relu, bias=norm_c[:, l - 1:l],
                                       scale=norm_a[:, l - 1:l]).then_inc(unit_ready, 1)
                    for c in range(2):
                        act.wait_ge(pre_ready, 2 * g + c + 1)
                        reuse(act, scanned, 2 * g + c - 1)
                        act.activation(msg[:, c, :], pre[:, c, :], ACT.Relu, bias=be[:, l:l + 1]).then_inc(msg_ready, 1)
                    for c in range(2):
                        act.wait_ge(turned, 2 * g + c + 1)
                        act.wait_ge(stored, 16 * g)
                        act.activation(rows[:, c, :], bank[1][:, c, :], ACT.Copy).then_inc(row_ready, 1)

            @block.vector
            def _(dve):
                dve.memset(attr[:, :, :], 0.0).then_inc(zeroed, 1)
                dve.memset(carry[:, :], 0.0).then_inc(carried, 1)
                @groups(dve, GE)
                def _(g):
                    for c in range(2 if bn else 0):
                        dve.wait_ge(loaded_h, 16 * g + 16)
                        dve.wait_ge(unit_ready, 2 * g + c + 1)
                        reuse(dve, pre_ready, 2 * g + c - 1)
                        dve.scalar_tensor_tensor(hout[:, c, :], hin[:, c, :], RES, unit[:, c, :], ALU.mult,
                                                 ALU.add).then_inc(h_ready, 1)
                    for c in range(2):
                        if bn:
                            dve.wait_ge(h_ready, 2 * g + c + 1)
                        else:
                            dve.wait_ge(loaded_h, 16 * g + 16)
                        dve.wait_ge(mm, 2 * g + c + 1)
                        reuse(dve, msg_ready, 2 * g + c - 1)
                        dve.tensor_tensor(pre[:, c, :], (hout if bn else hin)[:, c, :], bank[0][:, c, :],
                                          ALU.add).then_inc(pre_ready, 1)
                    dve.wait_ge(loaded_k, 16 * g + 16)
                    for c in range(2):
                        dve.wait_ge(msg_ready, 2 * g + c + 1)
                        reuse(dve, turned, 2 * g + c - 1)
                        scan(dve, g, c, run, kept, msg, carry, scanned, carried)

            @block.tensor
            def _(pe):
                @groups(pe, GE)
                def _(g):
                    pe.wait_ge(loaded_a, 16 * g + 16)
                    for c in range(2):
                        reuse(pe, pre_ready, 2 * g + c - 1)
                        pe.matmul(bank[0][:, c, :], w_e[:, l, :], attr[:, c, :], start=True, stop=True).then_inc(mm, 1)
                    for c in range(2):
                        pe.wait_ge(scanned, 2 * g + c + 1)
                        reuse(pe, row_ready, 2 * g + c - 1)
                        for j in range(4):
                            t = pe.transpose(bank[1][:, c, j * P:(j + 1) * P], run[:, c, j * P:(j + 1) * P], ident[:, :])
                        t.then_inc(turned, 1)

    def scan(dve, g, c, run, kept, of, carry, scanned, carried):
        if c:
            dve.wait_ge(scanned, 2 * g + 1)
        else:
            dve.wait_ge(carried, g + 1)
        dve.tensor_tensor_scan(run[:, c, :], kept[:, c, :], of[:, c, :],
                               run[:, 0, CH - 1:CH] if c else carry[:, :], ALU.mult, ALU.add).then_inc(scanned, 1)
        if c:
            dve.wait_ge(scanned, 2 * g + 2)
            dve.tensor_copy(carry[:, :], run[:, 1, CH - 1:CH]).then_inc(carried, 1)

    def batch_norm(l):
        tag = f"b{l}_"
        with stage() as ph:
            def tmp(name, shape, dt=F32):
                return ph.enter_context(nc.sbuf_tensor(tag + name, shape, dt))

            n = (GD * U + GE * 2) * 2
            parts = stat_all[:, :, :].rearrange("p n (a b) -> p (n a) b", a=2)
            sq = tmp("sq", [P, n])
            v = tmp("v", [P, 12])
            own, root = sem(tag + "own"), sem(tag + "root")
            block = ph.enter_context(nc.Block())

            @block.scalar
            def _(act):
                act.wait_ge(own, 9)
                act.activation(v[:, 7:8], v[:, 6:7], ACT.Sqrt, bias=eps[:, :]).then_inc(root, 1)

            @block.vector
            def _(dve):
                k = [0]

                def link(ins):
                    k[0] += 1
                    ins.then_inc(own, 1)
                    dve.wait_ge(own, k[0])

                each = float(CH // 2)
                link(dve.tensor_tensor(sq[:, :], parts[:, :, 1], parts[:, :, 1], ALU.mult))
                link(dve.tensor_reduce(v[:, 0:1], parts[:, :, 1], axis=AX.X, op=ALU.add))
                link(dve.tensor_reduce(v[:, 1:2], sq[:, :], axis=AX.X, op=ALU.add))
                link(dve.tensor_reduce(v[:, 2:3], parts[:, :, 2], axis=AX.X, op=ALU.add))
                link(dve.tensor_scalar(v[:, 3:4], v[:, 0:1], each / N, None, ALU.mult))
                link(dve.scalar_tensor_tensor(v[:, 4:5], v[:, 1:2], each, v[:, 2:3], ALU.mult, ALU.add))
                link(dve.tensor_tensor(v[:, 5:6], v[:, 3:4], v[:, 3:4], ALU.mult))
                link(dve.tensor_scalar(v[:, 4:5], v[:, 4:5], 1.0 / N, None, ALU.mult))
                link(dve.tensor_tensor(v[:, 6:7], v[:, 4:5], v[:, 5:6], ALU.subtract))
                dve.wait_ge(root, 1)
                link(dve.reciprocal(v[:, 8:9], v[:, 7:8]))
                link(dve.tensor_tensor(norm_a[:, l:l + 1], v[:, 8:9], gamma[:, l:l + 1], ALU.mult))
                link(dve.tensor_tensor(v[:, 9:10], v[:, 3:4], b2[:, l:l + 1], ALU.add))
                link(dve.tensor_tensor(v[:, 9:10], b2[:, l:l + 1], v[:, 9:10], ALU.subtract))
                link(dve.tensor_tensor(v[:, 10:11], v[:, 9:10], norm_a[:, l:l + 1], ALU.mult))
                link(dve.tensor_tensor(norm_c[:, l:l + 1], v[:, 10:11], beta[:, l:l + 1], ALU.add))

    def leave():
        tag = "v_"
        with stage() as ph:
            def tmp(name, shape, dt=F32):
                return ph.enter_context(nc.sbuf_tensor(tag + name, shape, dt))

            zin, hin, unit, h3 = (tmp(n, [P, U, CH]) for n in ("zin", "hin", "unit", "h3"))
            xin, x1, xn = tmp("xin", [P, 16, P]), tmp("x1", [P, 16, P]), tmp("xn", [P, 8, P])
            st, mv, h = tmp("st", [P, 8, 6]), tmp("mv", [P, 5, 8]), tmp("h", [P, 2, CH])
            own, var_ready, sd_ready, normed, unit_ready, h3_ready, turned, x1_ready, turned_h, h_ready, stored_h = (
                sem(tag + n) for n in ("own", "var", "sd", "normed", "unit", "h3", "turned", "x1", "turned_h",
                                       "h", "stored_h"))
            loaded_z, loaded_h, loaded_x, stored_x = (
                [sem(f"{tag}{n}{k}") for k in range(2)] for n in ("loaded_z", "loaded_h", "loaded_x", "stored_x"))
            block = ph.enter_context(nc.Block())

            @block.sync
            def _(sp):
                def load(g):
                    for k in range(2):
                        cols_ = bass.ds(g * GRP + k * HALF, HALF)
                        reuse(sp, unit_ready, 4 * g + 2 * k - 2)
                        sp.dma_start(zin[:, 2 * k:2 * k + 2, :].rearrange("p c n -> p (c n)"),
                                     ze[:, cols_]).then_inc(loaded_z[k], 16)
                        reuse(sp, h3_ready, 4 * g + 2 * k - 2)
                        sp.dma_start(hin[:, 2 * k:2 * k + 2, :].rearrange("p c n -> p (c n)"),
                                     he[:, cols_]).then_inc(loaded_h[k], 16)
                        reuse(sp, x1_ready, 4 * g + 2 * k - 2)
                        sp.dma_start(xin[:, 8 * k:8 * k + 8, :],
                                     tiles(xe, g * GRP + k * HALF, 8)).then_inc(loaded_x[k], 16)

                def store(g):
                    for k in range(2):
                        sp.wait_ge(x1_ready, 4 * g + 2 * k + 2)
                        sp.dma_start(tiles(xe, g * GRP + k * HALF, 8), x1[:, 8 * k:8 * k + 8, :])\
                          .then_inc(stored_x[k], 16)
                    sp.wait_ge(h_ready, 2 * g + 2)
                    apart(sp, passed)
                    sp.dma_start(he[:, bass.ds(g * GRP + HALF, HALF)],
                                 h[:, :, :].rearrange("p c n -> p (c n)")).then_inc(stored_h, 16)

                load(0)
                with sp.Fori(0, GE - 1) as g:
                    load(g + 1)
                    store(g)
                store(GE - 1)
                sp.wait_ge(stored_h, 16 * GE)
                for k in range(2):
                    sp.wait_ge(stored_x[k], 16 * GE)

            @block.scalar
            def _(act):
                @groups(act, GE)
                def _(g):
                    for c in range(U):
                        act.wait_ge(loaded_z[c // 2], 16 * g + 16)
                        reuse(act, h3_ready, 4 * g + c - 3)
                        act.activation(unit[:, c, :], zin[:, c, :], ACT.Relu, bias=norm_c[:, LAYERS - 1:],
                                       scale=norm_a[:, LAYERS - 1:]).then_inc(unit_ready, 1)
                    act.wait_ge(var_ready, g + 1)
                    ln_root(act, mv, 8, sd_ready)
                    for c in range(2):
                        act.wait_ge(turned_h, 2 * g + c + 1)
                        act.wait_ge(stored_h, 16 * g)
                        act.activation(h[:, c, :], bank[1][:, c, :], ACT.Relu).then_inc(h_ready, 1)

            @block.vector
            def _(dve):
                steps = Steps(dve, own, LN_STEPS)
                @groups(dve, GE)
                def _(g):
                    steps.at(g)
                    for c in range(U):
                        dve.wait_ge(loaded_h[c // 2], 16 * g + 16)
                        dve.wait_ge(unit_ready, 4 * g + c + 1)
                        reuse(dve, turned, 4 * g + c - 3)
                        dve.scalar_tensor_tensor(h3[:, c, :], hin[:, c, :], RES, unit[:, c, :], ALU.mult,
                                                 ALU.add).then_inc(h3_ready, 1)
                    for c in range(U):
                        dve.wait_ge(turned, 4 * g + c + 1)
                        dve.wait_ge(loaded_x[c // 2], 16 * g + 16)
                        dve.wait_ge(stored_x[c // 2], 16 * g)
                        dve.tensor_tensor(x1[:, 4 * c:4 * c + 4, :].rearrange("p t f -> p (t f)"),
                                          xin[:, 4 * c:4 * c + 4, :].rearrange("p t f -> p (t f)"),
                                          bank[0][:, c, :], ALU.add).then_inc(x1_ready, 1)
                    dve.wait_ge(x1_ready, 4 * g + 4)
                    ln_sums(dve, steps, x1[:, 8:16, :], st, mv, 8, var_ready)
                    dve.wait_ge(sd_ready, g + 1)
                    dve.wait_ge(turned_h, 2 * g)
                    ln_apply(dve, steps, xn, x1[:, 8:16, :], mv, 8, normed)

            @block.tensor
            def _(pe):
                @groups(pe, GE)
                def _(g):
                    for c in range(U):
                        pe.wait_ge(h3_ready, 4 * g + c + 1)
                        reuse(pe, x1_ready, 4 * g + c - 3)
                        for j in range(4):
                            t = pe.transpose(bank[0][:, c, j * P:(j + 1) * P], h3[:, c, j * P:(j + 1) * P], ident[:, :])
                        t.then_inc(turned, 1)
                    for c in range(2):
                        pe.wait_ge(normed, 2 * g + c + 1)
                        reuse(pe, h_ready, 2 * g + c - 1)
                        for j in range(4):
                            t = pe.transpose(bank[1][:, c, j * P:(j + 1) * P], xn[:, 4 * c + j, :], ident[:, :])
                        t.then_inc(turned_h, 1)

    def mean(r):
        tag = f"a{r}_"
        of, to = agg[(r + 1) % 2], agg[r % 2]
        last_one = r == 2
        with stage() as ph:
            def tmp(name, shape, dt=F32):
                return ph.enter_context(nc.sbuf_tensor(tag + name, shape, dt))

            h = tmp("h", [P, 2, CH])
            kept = tmp("kept", [P, 2, CH], BF16)
            run, rows = tmp("run", [P, 2, CH]), tmp("rows", [P, 8, P])
            carry = tmp("carry", [P, 1])
            h_ready, loaded_k, scanned, carried, turned, row_ready, stored = (
                sem(tag + n) for n in ("h", "loaded_k", "scanned", "carried", "turned", "row", "stored"))
            if r:
                sums, at_i = tmp("sums", [P, 8, P]), tmp("at_i", [P, 8], I32)
                slot, turned_s, got = sem(tag + "slot"), sem(tag + "turned_s"), [sem(f"{tag}got{k}") for k in range(2)]
            if last_one:
                x1, x2 = tmp("x1", [P, 8, P]), tmp("x2", [P, 8, P])
                loaded_x, x_ready, stored_x = (sem(tag + n) for n in ("loaded_x", "x", "stored_x"))
            block = ph.enter_context(nc.Block())
            H_UNIT = 1 if r else 16

            @block.sync
            def _(sp):
                def load(g):
                    if not r:
                        sp.wait_ge(scanned, 2 * g)
                        sp.dma_start(h[:, :, :].rearrange("p c n -> p (c n)"),
                                     he[:, bass.ds(g * GRP + HALF, HALF)]).then_inc(h_ready, 16)
                    sp.wait_ge(scanned, 2 * g)
                    sp.dma_start(kept[:, :, :].rearrange("p c n -> p (c n)"), keep_line[bass.ds(g * 8, 8), :]
                                 .rearrange("(a t) p -> a (t p)", a=1).to_broadcast([P, HALF])).then_inc(loaded_k, 16)
                    if last_one:
                        sp.wait_ge(x_ready, 2 * g)
                        sp.dma_start(x1[:, :, :], tiles(xe, g * GRP, 8)).then_inc(loaded_x, 16)

                def store(g):
                    sp.wait_ge(row_ready, 2 * g + 2)
                    sp.dma_start(tiles(to, g * HALF, 8), rows[:, :, :]).then_inc(stored, 16)
                    if last_one:
                        sp.wait_ge(x_ready, 2 * g + 2)
                        sp.dma_start(tiles(x2d, g * HALF, 8), x2[:, :, :]).then_inc(stored_x, 16)

                load(0)
                with sp.Fori(0, GE - 1) as g:
                    load(g + 1)
                    store(g)
                store(GE - 1)
                sp.wait_ge(stored, 16 * GE)
                if last_one:
                    sp.wait_ge(stored_x, 16 * GE)

            if r:
                @block.gpsimd
                def _(pool):
                    @groups(pool, GE)
                    def _(g):
                        pool.wait_ge(got[0], 64 * g)
                        pool.wait_ge(got[1], 64 * g)
                        pool.tensor_copy(at_i[:, :], src_e[:, bass.ds(g * 8, 8)]).then_inc(slot, 1)
                        pool.wait_ge(slot, g + 1)
                        pool.wait_ge(turned_s, 2 * g)
                        apart(pool, passed)
                        for t in range(8):
                            pool.indirect_dma_start(sums[:, t, :], None, of[:, :],
                                                    bass.IndirectOffsetOnAxis(ap=at_i[:, t:t + 1], axis=0),
                                                    bounds_check=ZR, oob_is_err=False).then_inc(got[t // 4], 16)

                @block.scalar
                def _(act):
                    @groups(act, GE)
                    def _(g):
                        for c in range(2):
                            act.wait_ge(turned_s, 2 * g + c + 1)
                            reuse(act, scanned, 2 * g + c - 1)
                            act.activation(h[:, c, :], bank[0][:, c, :], ACT.Copy).then_inc(h_ready, 1)

            @block.vector
            def _(dve):
                dve.memset(carry[:, :], 0.0).then_inc(carried, 1)
                @groups(dve, GE)
                def _(g):
                    dve.wait_ge(loaded_k, 16 * g + 16)
                    for c in range(2):
                        dve.wait_ge(h_ready, 2 * g + c + 1 if r else 16 * g + 16)
                        reuse(dve, turned, 2 * g + c - 1)
                        scan(dve, g, c, run, kept, h, carry, scanned, carried)
                    for c in range(2):
                        t4 = slice(4 * c, 4 * c + 4)
                        dve.wait_ge(turned, 2 * g + c + 1)
                        dve.wait_ge(stored, 16 * g)
                        dve.tensor_tensor(rows[:, t4, :], bank[1][:, c, :].rearrange("p (t f) -> p t f", f=P),
                                          rcount[:, bass.ds(g * 8 + 4 * c, 4)].unsqueeze(2).to_broadcast([P, 4, P]),
                                          ALU.mult).then_inc(row_ready, 1)
                    for c in range(2 if last_one else 0):
                        t4 = slice(4 * c, 4 * c + 4)
                        dve.wait_ge(row_ready, 2 * g + c + 1)
                        dve.wait_ge(loaded_x, 16 * g + 16)
                        dve.wait_ge(stored_x, 16 * g)
                        dve.tensor_tensor(x2[:, t4, :], x1[:, t4, :], rows[:, t4, :], ALU.add).then_inc(x_ready, 1)

            @block.tensor
            def _(pe):
                @groups(pe, GE)
                def _(g):
                    for c in range(2 if r else 0):
                        pe.wait_ge(got[c], 64 * g + 64)
                        reuse(pe, h_ready, 2 * g + c - 1)
                        for j in range(4):
                            t = pe.transpose(bank[0][:, c, j * P:(j + 1) * P], sums[:, 4 * c + j, :], ident[:, :])
                        t.then_inc(turned_s, 1)
                    for c in range(2):
                        pe.wait_ge(scanned, 2 * g + c + 1)
                        reuse(pe, row_ready, 2 * g + c - 1)
                        for j in range(4):
                            t = pe.transpose(bank[1][:, c, j * P:(j + 1) * P], run[:, c, j * P:(j + 1) * P], ident[:, :])
                        t.then_inc(turned, 1)

    def logits():
        tag = "q_"
        with stage() as ph:
            def tmp(name, shape, dt=F32):
                return ph.enter_context(nc.sbuf_tensor(tag + name, shape, dt))

            got_rows = tmp("got_rows", [P, 16, P])
            x1, x2, xn = tmp("x1", [P, 8, P]), tmp("x2", [P, 8, P]), tmp("xn", [P, 16, P])
            st = [tmp(f"st{k}", [P, 8, 6]) for k in range(2)]
            mv = [tmp(f"mv{k}", [P, 5, 8]) for k in range(2)]
            at_i = tmp("at_i", [P, 16], I32)
            h, q, v = tmp("h", [P, U, CH]), tmp("q", [P, 2, CH]), tmp("v", [P, 2, CH])
            qk, raw, low, lr = (tmp(n, [P, 2, CH]) for n in ("qk", "raw", "low", "lr"))
            attr = tmp("attr", [P, 2, CH])
            peak = tmp("peak", [P, 2])
            (own, var_ready, sd_ready, normed, slot, x2_ready, turned, h_ready, loaded_x, loaded_a, stored_v, stored_l,
             mm_q, q_ready, mm_k, mm_v, v_ready, qk_ready, mm_l, raw_ready, low_ready, lr_ready, peaked, zeroed,
             topped) = (
                sem(tag + n) for n in ("own", "var", "sd", "normed", "slot", "x2", "turned", "h", "loaded_x", "loaded_a",
                                       "stored_v", "stored_l", "mm_q", "q", "mm_k", "mm_v", "v", "qk", "mm_l", "raw",
                                       "low", "lr", "peaked", "zeroed", "topped"))
            got, stored_x, stored_h = ([sem(f"{tag}{n}{k}") for k in range(2)] for n in ("got", "stored_x", "stored_h"))
            block = ph.enter_context(nc.Block())

            @block.gpsimd
            def _(pool):
                @groups(pool, GE)
                def _(g):
                    for k, (ids, of) in enumerate(((dst_e, x2d), (src_e, agg[0]))):
                        pool.wait_ge(got[k], 128 * g)
                        pool.tensor_copy(at_i[:, 8 * k:8 * k + 8], ids[:, bass.ds(g * 8, 8)]).then_inc(slot, 1)
                        pool.wait_ge(slot, 2 * g + k + 1)
                        if k:
                            pool.wait_ge(x2_ready, 2 * g)
                        else:
                            pool.wait_ge(normed, 4 * g)
                            pool.wait_ge(stored_x[0], 16 * g)
                        apart(pool, passed)
                        for t in range(8):
                            pool.indirect_dma_start(got_rows[:, 8 * k + t, :], None, of[:, :],
                                                    bass.IndirectOffsetOnAxis(ap=at_i[:, 8 * k + t:8 * k + t + 1],
                                                                              axis=0),
                                                    bounds_check=ZR, oob_is_err=False).then_inc(got[k], 16)
                pool.wait_ge(peaked, 2 * GE + 1)
                pool.partition_all_reduce(top[:, 0:1], peak[:, 0:1], P, REDUCE_MAX).then_inc(topped, 1)

            @block.sync
            def _(sp):
                def load(g):
                    sp.wait_ge(x2_ready, 2 * g)
                    sp.dma_start(x1[:, :, :], tiles(xe, g * GRP + HALF, 8)).then_inc(loaded_x, 16)
                    sp.wait_ge(mm_l, 2 * g)
                    sp.dma_start(attr[0:EB, :, :].rearrange("p c n -> p (c n)"),
                                 attr_t[EA:EA + EB, bass.ds(g * HALF, HALF)]).then_inc(loaded_a, 16)
                    sp.dma_start(attr[HD:HD + 1, :, :].rearrange("p c n -> p (c n)"),
                                 pad_line[:, bass.ds(g * HALF, HALF)]).then_inc(loaded_a, 16)

                def store(g):
                    cols_ = bass.ds(g * HALF, HALF)
                    sp.wait_ge(got[0], 128 * g + 128)
                    sp.dma_start(tiles(xe, g * GRP, 8), got_rows[:, 0:8, :]).then_inc(stored_x[0], 16)
                    sp.wait_ge(x2_ready, 2 * g + 2)
                    sp.dma_start(tiles(xe, g * GRP + HALF, 8), x2[:, :, :]).then_inc(stored_x[1], 16)
                    for k in range(2):
                        sp.wait_ge(h_ready, 4 * g + 2 * k + 2)
                        apart(sp, passed)
                        sp.dma_start(he[:, bass.ds(g * GRP + k * HALF, HALF)],
                                     h[:, 2 * k:2 * k + 2, :].rearrange("p c n -> p (c n)")).then_inc(stored_h[k], 16)
                    sp.wait_ge(v_ready, 2 * g + 2)
                    sp.dma_start(v_t[:, cols_], v[:, :, :].rearrange("p c n -> p (c n)")).then_inc(stored_v, 16)
                    sp.wait_ge(lr_ready, 2 * g + 2)
                    sp.dma_start(attn_t[:, cols_], lr[:, :, :].rearrange("p c n -> p (c n)")).then_inc(stored_l, 16)

                sp.wait_ge(zeroed, 1)
                load(0)
                with sp.Fori(0, GE - 1) as g:
                    load(g + 1)
                    store(g)
                store(GE - 1)
                for s in (*stored_x, *stored_h, stored_v, stored_l):
                    sp.wait_ge(s, 16 * GE)

            @block.scalar
            def _(act):
                @groups(act, GE)
                def _(g):
                    for k in range(2):
                        act.wait_ge(var_ready, 2 * g + k + 1)
                        ln_root(act, mv[k], 8, sd_ready)
                    for c in range(U):
                        act.wait_ge(turned, 4 * g + c + 1)
                        act.wait_ge(stored_h[c // 2], 16 * g)
                        act.wait_ge(mm_v, 2 * g)
                        act.activation(h[:, c, :], bank[0][:, c, :], ACT.Relu).then_inc(h_ready, 1)
                    for c in range(2):
                        act.wait_ge(mm_q, 2 * g + c + 1)
                        reuse(act, qk_ready, 2 * g + c - 1)
                        act.activation(q[:, c, :], bank[1][:, c, :], ACT.Copy).then_inc(q_ready, 1)
                    for c in range(2):
                        act.wait_ge(mm_v, 2 * g + c + 1)
                        act.wait_ge(stored_v, 16 * g)
                        act.activation(v[:, c, :], bank[0][:, 2 + c, :], ACT.Copy).then_inc(v_ready, 1)
                    for c in range(2):
                        act.wait_ge(mm_l, 2 * g + c + 1)
                        reuse(act, lr_ready, 2 * g + c - 1)
                        act.activation(raw[:, c, :], bank[1][:, c, :], ACT.Copy).then_inc(raw_ready, 1)

            @block.vector
            def _(dve):
                steps = Steps(dve, own, 2 * LN_STEPS)
                dve.memset(attr[:, :, :], 0.0).then_inc(zeroed, 1)
                dve.memset(peak[:, :], -3e38).then_inc(peaked, 1)
                @groups(dve, GE)
                def _(g):
                    steps.at(g)
                    dve.wait_ge(got[0], 128 * g + 128)
                    ln_sums(dve, steps, got_rows[:, 0:8, :], st[0], mv[0], 8, var_ready)
                    for c in range(2):
                        t4 = slice(4 * c, 4 * c + 4)
                        dve.wait_ge(loaded_x, 16 * g + 16)
                        dve.wait_ge(got[1], 128 * g + 128)
                        dve.wait_ge(stored_x[1], 16 * g)
                        dve.tensor_tensor(x2[:, t4, :], x1[:, t4, :], got_rows[:, 8 + 4 * c:12 + 4 * c, :],
                                          ALU.add).then_inc(x2_ready, 1)
                    dve.wait_ge(x2_ready, 2 * g + 2)
                    ln_sums(dve, steps, x2, st[1], mv[1], 8, var_ready)
                    for k in range(2):
                        dve.wait_ge(sd_ready, 2 * g + k + 1)
                        reuse(dve, turned, 4 * g + 2 * k - 2)
                        ln_apply(dve, steps, xn[:, 8 * k:8 * k + 8, :], got_rows[:, 0:8, :] if k == 0 else x2, mv[k],
                                 8, normed)
                    for c in range(2):
                        dve.wait_ge(q_ready, 2 * g + c + 1)
                        dve.wait_ge(mm_k, 2 * g + c + 1)
                        reuse(dve, mm_l, 2 * g + c - 1)
                        dve.tensor_tensor(qk[:, c, :], q[:, c, :], bank[1][:, 2 + c, :], ALU.mult).then_inc(qk_ready, 1)
                    for c in range(2):
                        dve.wait_ge(raw_ready, 2 * g + c + 1)
                        reuse(dve, lr_ready, 2 * g + c - 1)
                        dve.wait_ge(stored_l, 16 * g)
                        dve.wait_ge(peaked, 2 * g + 1)
                        dve.scalar_tensor_tensor(lr[:, c, :], raw[:, c, :], 0.2, raw[:, c, :], ALU.mult,
                                                 ALU.max).then_inc(lr_ready, 1)
                    dve.wait_ge(lr_ready, 2 * g + 2)
                    dve.tensor_reduce(peak[:, 1:2], lr[:, :, :], axis=AX.XY, op=ALU.max).then_inc(peaked, 1)
                    dve.wait_ge(peaked, 2 * g + 2)
                    dve.tensor_tensor(peak[:, 0:1], peak[:, 0:1], peak[:, 1:2], ALU.max).then_inc(peaked, 1)

            @block.tensor
            def _(pe):
                @groups(pe, GE)
                def _(g):
                    for c in range(U):
                        pe.wait_ge(normed, 4 * g + c + 1)
                        reuse(pe, h_ready, 4 * g + c - 3)
                        if c >= 2:
                            pe.wait_ge(v_ready, 2 * g)
                        for j in range(4):
                            t = pe.transpose(bank[0][:, c, j * P:(j + 1) * P], xn[:, 4 * c + j, :], ident[:, :])
                        t.then_inc(turned, 1)
                    for c in range(2):
                        pe.wait_ge(h_ready, 4 * g + c + 1)
                        reuse(pe, raw_ready, 2 * g + c - 1)
                        pe.matmul(bank[1][:, c, :], wq[:, :], h[:, c, :], start=True, stop=True).then_inc(mm_q, 1)
                    for c in range(2):
                        pe.wait_ge(h_ready, 4 * g + 2 + c + 1)
                        reuse(pe, qk_ready, 2 * g + c - 1)
                        pe.matmul(bank[1][:, 2 + c, :], wk[:, :], h[:, 2 + c, :], start=True, stop=True).then_inc(mm_k, 1)
                    for c in range(2):
                        pe.matmul(bank[0][:, 2 + c, :], wv[:, :], h[:, 2 + c, :], start=True, stop=True).then_inc(mm_v, 1)
                    for c in range(2):
                        pe.wait_ge(qk_ready, 2 * g + c + 1)
                        pe.matmul(bank[1][:, c, :], heads[:, :], qk[:, c, :], start=True, stop=False)
                        pe.wait_ge(loaded_a, 32 * g + 32)
                        pe.matmul(bank[1][:, c, :], w_bias[:, :], attr[:, c, :], start=False, stop=True).then_inc(mm_l, 1)

    def softmax():
        tag = "s_"
        with stage() as ph:
            def tmp(name, shape, dt=F32):
                return ph.enter_context(nc.sbuf_tensor(tag + name, shape, dt))

            lr, v, ex, ev, run, runx = (tmp(n, [P, 2, CH]) for n in ("lr", "v", "ex", "ev", "run", "runx"))
            total, inv = tmp("total", [P, 8 * H]), tmp("inv", [P, 8 * H])
            kept, rows = tmp("kept", [P, 2, CH], BF16), tmp("rows", [P, 8, P])
            carry, carryx = tmp("carry", [P, 1]), tmp("carryx", [P, 1])
            (loaded_l, loaded_v, loaded_k, ex_ready, ev_ready, scanned, scannedx, carried, carriedx, inverted, turned,
             row_ready, stored, negated, floored) = (
                sem(tag + n) for n in ("loaded_l", "loaded_v", "loaded_k", "ex", "ev", "scanned", "scannedx", "carried",
                                       "carriedx", "inverted", "turned", "row", "stored", "negated", "floored"))
            block = ph.enter_context(nc.Block())

            @block.sync
            def _(sp):
                def load(g):
                    cols_ = bass.ds(g * HALF, HALF)
                    sp.wait_ge(ex_ready, 2 * g)
                    sp.dma_start(lr[:, :, :].rearrange("p c n -> p (c n)"), attn_t[:, cols_]).then_inc(loaded_l, 16)
                    sp.wait_ge(ev_ready, 2 * g)
                    sp.dma_start(v[:, :, :].rearrange("p c n -> p (c n)"), v_t[:, cols_]).then_inc(loaded_v, 16)
                    sp.wait_ge(scanned, 2 * g)
                    sp.wait_ge(scannedx, 2 * g)
                    sp.dma_start(kept[:, :, :].rearrange("p c n -> p (c n)"), keep_line[bass.ds(g * 8, 8), :]
                                 .rearrange("(a t) p -> a (t p)", a=1).to_broadcast([P, HALF])).then_inc(loaded_k, 16)

                def store(g):
                    sp.wait_ge(row_ready, 2 * g + 2)
                    sp.dma_start(tiles(agg[1], g * HALF, 8), rows[:, :, :]).then_inc(stored, 16)

                load(0)
                with sp.Fori(0, GE - 1) as g:
                    load(g + 1)
                    store(g)
                store(GE - 1)
                sp.wait_ge(stored, 16 * GE)

            @block.scalar
            def _(act):
                act.wait_ge(negated, 1)
                @groups(act, GE)
                def _(g):
                    for c in range(2):
                        act.wait_ge(loaded_l, 16 * g + 16)
                        reuse(act, ev_ready, 2 * g + c - 1)
                        reuse(act, scannedx, 2 * g + c - 1)
                        act.activation(ex[:, c, :], lr[:, c, :], ACT.Exp, bias=top[:, 1:2]).then_inc(ex_ready, 1)
            @block.vector
            def _(dve):
                dve.tensor_scalar(top[:, 1:2], top[:, 0:1], -1.0, None, ALU.mult).then_inc(negated, 1)
                dve.memset(carry[:, :], 0.0).then_inc(carried, 1)
                dve.memset(carryx[:, :], 0.0).then_inc(carriedx, 1)
                @groups(dve, GE)
                def _(g):
                    for c in range(2):
                        dve.wait_ge(loaded_v, 16 * g + 16)
                        dve.wait_ge(ex_ready, 2 * g + c + 1)
                        reuse(dve, scanned, 2 * g + c - 1)
                        dve.tensor_tensor(ev[:, c, :], ex[:, c, :], v[:, c, :], ALU.mult).then_inc(ev_ready, 1)
                    dve.wait_ge(loaded_k, 16 * g + 16)
                    dve.wait_ge(turned, 2 * g)
                    for c in range(2):
                        dve.wait_ge(ev_ready, 2 * g + c + 1)
                        scan(dve, g, c, run, kept, ev, carry, scanned, carried)
                        scan(dve, g, c, runx, kept, ex, carryx, scannedx, carriedx)
                    for c in range(2):
                        s4 = slice(4 * H * c, 4 * H * c + 4 * H)
                        dve.wait_ge(turned, 2 * g + c + 1)
                        dve.tensor_scalar(total[:, s4], bank[1][:, c, 0:4 * H], 1e-12, None, ALU.max).then_inc(floored, 1)
                        dve.wait_ge(floored, 2 * g + c + 1)
                        reuse(dve, row_ready, 2 * g + c - 1)
                        dve.reciprocal(inv[:, s4], total[:, s4]).then_inc(inverted, 1)
                        dve.wait_ge(inverted, 2 * g + c + 1)
                        dve.wait_ge(stored, 16 * g)
                        dve.tensor_tensor(rows[:, 4 * c:4 * c + 4, :].rearrange("p t (h d) -> p (t h) d", h=H),
                                          bank[0][:, c, :].rearrange("p (a d) -> p a d", d=HD),
                                          inv[:, s4].unsqueeze(2).to_broadcast([P, 4 * H, HD]),
                                          ALU.mult).then_inc(row_ready, 1)

            @block.tensor
            def _(pe):
                @groups(pe, GE)
                def _(g):
                    for c in range(2):
                        pe.wait_ge(scanned, 2 * g + c + 1)
                        pe.wait_ge(scannedx, 2 * g + c + 1)
                        reuse(pe, row_ready, 2 * g + c - 1)
                        for j in range(4):
                            s = slice(j * P, (j + 1) * P)
                            pe.transpose(bank[0][:, c, s], run[:, c, s], ident[:, :])
                            t = pe.matmul(bank[1][:, c, j * H:(j + 1) * H], runx[:, c, s], ident[:, 0:P:HD],
                                          start=True, stop=True)
                        t.then_inc(turned, 1)

    def finish():
        tag = "f_"
        with stage() as ph:
            def tmp(name, shape, dt=F32):
                return ph.enter_context(nc.sbuf_tensor(tag + name, shape, dt))

            zin, hin, unit, h = (tmp(n, [P, U, CH]) for n in ("zin", "hin", "unit", "h"))
            xin, x1, xn, x3, x3b, hn, res = (tmp(n, [P, 16, P]) for n in ("xin", "x1", "xn", "x3", "x3b", "hn", "res"))
            b2r = tmp("b2r", [P, 1, P])
            st = [tmp(f"st{k}", [P, 8, 6]) for k in range(4)]
            mv = [tmp(f"mv{k}", [P, 5, 8]) for k in range(4)]
            (own, var1, sd1, var3, sd3, normed, unit_ready, mm_x, x1_ready, turned, h_ready, mixed, x3_ready,
             x3b_ready, hn_ready, res_ready, scaled, b2_ready) = (
                sem(tag + n) for n in ("own", "var1", "sd1", "var3", "sd3", "normed", "unit", "mm_x", "x1", "turned", "h",
                                       "mixed", "x3", "x3b", "hn", "res", "scaled", "b2"))
            loaded_z, loaded_h, loaded_x, stored = (
                [sem(f"{tag}{n}{k}") for k in range(2)] for n in ("loaded_z", "loaded_h", "loaded_x", "stored"))
            block = ph.enter_context(nc.Block())

            def flat(t, c):
                return t[:, 4 * c:4 * c + 4, :].rearrange("p t f -> p (t f)")

            @block.sync
            def _(sp):
                def store(g, tail=False):
                    for k in range(2):
                        sp.wait_ge(res_ready, 4 * g + 2 * k + 2)
                        if tail and k:
                            sp.dma_start(x_tail(out), res[0:TAIL_P, 8:16, :].rearrange("p j f -> p (j f)"))\
                              .then_inc(stored[k], 16)
                        else:
                            sp.dma_start(x_half(out, 2 * g + k), res[:, 8 * k:8 * k + 8, :]
                                         .rearrange("p j f -> p (j f)")).then_inc(stored[k], 16)

                with sp.Fori(0, GD - 1) as g:
                    store(g)
                store(GD - 1, tail=True)
                for k in range(2):
                    sp.wait_ge(stored[k], 16 * GD)

            @block.gpsimd
            def _(pool):
                pool.wait_ge(b2_ready, 1)

                @groups(pool, GD)
                def _(g):
                    for c in range(U):
                        pool.wait_ge(x3_ready, 4 * g + c + 1)
                        reuse(pool, res_ready, 4 * g + c - 3)
                        apart(pool, passed)
                        pool.tensor_tensor(x3b[:, 4 * c:4 * c + 4, :], x3[:, 4 * c:4 * c + 4, :],
                                           b2r[:, :, :].to_broadcast([P, 4, P]), ALU.add).then_inc(x3b_ready, 1)

            @block.scalar
            def _(act):
                def load_z(g):
                    for k in range(2):
                        reuse(act, unit_ready, 4 * g + 2 * k - 2)
                        act.dma_start(zin[:, 2 * k:2 * k + 2, :].rearrange("p c n -> p (c n)"),
                                      zd[:, bass.ds(g * GRP + k * HALF, HALF)]).then_inc(loaded_z[k], 16)

                def load_hx(g, tail=False):
                    for k in range(2):
                        reuse(act, mm_x, 4 * g + 2 * k - 2)
                        act.dma_start(hin[:, 2 * k:2 * k + 2, :].rearrange("p c n -> p (c n)"),
                                      hd[:, bass.ds(g * GRP + k * HALF, HALF)]).then_inc(loaded_h[k], 16)
                        if tail and k:
                            act.dma_start(xin[0:TAIL_P, 8:16, :].rearrange("p j f -> p (j f)"),
                                          x_tail(x)).then_inc(loaded_x[k], 16)
                        else:
                            act.dma_start(xin[:, 8 * k:8 * k + 8, :].rearrange("p j f -> p (j f)"),
                                          x_half(x, 2 * g + k)).then_inc(loaded_x[k], 16)

                def units(g):
                    for c in range(U):
                        act.wait_ge(loaded_z[c // 2], 16 * g + 16)
                        reuse(act, mm_x, 4 * g + c - 3)
                        act.activation(unit[:, c, :], zin[:, c, :], ACT.Relu, bias=norm_c[:, LAYERS - 1:],
                                       scale=norm_a[:, LAYERS - 1:]).then_inc(unit_ready, 1)

                def relu_ln3(g, c):
                    act.wait_ge(scaled, 2 * g + c // 2 + 1)
                    reuse(act, res_ready, 4 * g + c - 3)
                    for j in range(4):
                        t, m = 4 * c + j, mv[2 + c // 2]
                        i = t % 8
                        a = act.activation(hn[:, t, :], x3[:, t, :], ACT.Relu, bias=m[:, 0, i:i + 1],
                                           scale=m[:, 4, i:i + 1])
                    a.then_inc(hn_ready, 1)

                load_z(0)
                load_hx(0)
                units(0)
                load_z(1)

                @groups(act, GD, written=2, ended=2)
                def _(g):
                    static = isinstance(g, int)
                    for c in range(U):
                        act.wait_ge(mm_x, 4 * g + c + 1)
                        reuse(act, x3_ready, 4 * g + c - 3)
                        act.activation(flat(x1, c), bank[0][:, c, :], ACT.Copy).then_inc(x1_ready, 1)
                    if not (static and g == GD - 1):
                        load_hx(g + 1, tail=static and g == GD - 2)
                    for k in range(2):
                        if not (static and g == 0):
                            relu_ln3(g - 1, k)
                        act.wait_ge(var1, 2 * g + k + 1)
                        ln_root(act, mv[k], 8, sd1)
                    for c in range(2, U):
                        if not (static and g == 0):
                            relu_ln3(g - 1, c)
                    for c in range(U):
                        act.wait_ge(turned, 4 * g + c + 1)
                        reuse(act, mixed, 4 * g + c - 3)
                        act.activation(h[:, c, :], bank[1][:, c, :], ACT.Relu).then_inc(h_ready, 1)
                    if not (static and g == GD - 1):
                        units(g + 1)
                    if not (static and g >= GD - 2):
                        load_z(g + 2)
                    for k in range(2):
                        act.wait_ge(var3, 2 * g + k + 1)
                        ln_root(act, mv[2 + k], 8, sd3)

                for c in range(U):
                    relu_ln3(GD - 1, c)

            @block.vector
            def _(dve):
                steps = Steps(dve, own, 2 * LN_STEPS + 2 * (LN_STEPS - 1) + 2)
                dve.tensor_scalar(b2r[:, 0, :], b2_row[:, :], 0.0, None, ALU.max).then_inc(b2_ready, 1)

                def result(g):
                    for c in range(U):
                        dve.wait_ge(hn_ready, 4 * g + c + 1)
                        dve.wait_ge(x3b_ready, 4 * g + c + 1)
                        reuse(dve, stored[c // 2], 16 * g)
                        dve.tensor_tensor(flat(res, c), flat(x3b, c), flat(hn, c), ALU.add).then_inc(res_ready, 1)

                @groups(dve, GD, written=2)
                def _(g):
                    steps.at(g)
                    for k in range(2):
                        dve.wait_ge(x1_ready, 4 * g + 2 * k + 2)
                        ln_sums(dve, steps, x1[:, 8 * k:8 * k + 8, :], st[k], mv[k], 8, var1)
                    for k in range(2):
                        dve.wait_ge(sd1, 2 * g + k + 1)
                        reuse(dve, turned, 4 * g + 2 * k - 2)
                        ln_apply(dve, steps, xn[:, 8 * k:8 * k + 8, :], x1[:, 8 * k:8 * k + 8, :], mv[k], 8, normed)
                    for c in range(U):
                        dve.wait_ge(mixed, 4 * g + c + 1)
                        reuse(dve, x3b_ready, 4 * g + c - 3)
                        reuse(dve, hn_ready, 4 * g + c - 3)
                        dve.scalar_tensor_tensor(flat(x3, c), bank[1][:, c, :], 0.0, flat(x1, c), ALU.max,
                                                 ALU.add).then_inc(x3_ready, 1)
                    for k in range(2):
                        dve.wait_ge(x3_ready, 4 * g + 2 * k + 2)
                        ln_sums(dve, steps, x3[:, 8 * k:8 * k + 8, :], st[2 + k], mv[2 + k], 8, var3)
                    if not (isinstance(g, int) and g == 0):
                        result(g - 1)
                    for k in range(2):
                        m = mv[2 + k]
                        dve.wait_ge(sd3, 2 * g + k + 1)
                        steps.did(dve.reciprocal(m[:, 4, :], m[:, 3, :]))
                        steps.sync()
                        dve.tensor_tensor(m[:, 0, :], m[:, 0, :], m[:, 4, :], ALU.mult).then_inc(scaled, 1)

                result(GD - 1)

            @block.tensor
            def _(pe):
                @groups(pe, GD)
                def _(g):
                    for c in range(U):
                        pe.wait_ge(loaded_x[c // 2], 16 * g + 16)
                        reuse(pe, x1_ready, 4 * g + c - 3)
                        pe.matmul(bank[0][:, c, :], ident[:, :], flat(xin, c), start=True, stop=False)
                        pe.wait_ge(loaded_h[c // 2], 16 * g + 16)
                        pe.wait_ge(unit_ready, 4 * g + c + 1)
                        for j in range(4):
                            s = slice(j * P, (j + 1) * P)
                            pe.matmul(bank[0][:, c, s], hin[:, c, s], tenth[:, :], start=False, stop=False)
                            m = pe.matmul(bank[0][:, c, s], unit[:, c, s], ident[:, :], start=False, stop=j == 3)
                        m.then_inc(mm_x, 1)

                    def turn(c):
                        pe.wait_ge(normed, 4 * g + c + 1)
                        reuse(pe, x3_ready, 4 * g + c - 3)
                        for j in range(4):
                            t = pe.transpose(bank[1][:, c, j * P:(j + 1) * P], xn[:, 4 * c + j, :], ident[:, :])
                        t.then_inc(turned, 1)

                    def mix(c):
                        pe.wait_ge(h_ready, 4 * g + c + 1)
                        pe.matmul(bank[1][:, c, :], three[:, :], c_parts[:, :, :].rearrange("p a f -> p (a f)"),
                                  start=True, stop=False)
                        for j in range(4):
                            m = pe.matmul(bank[1][:, c, j * P:(j + 1) * P], h[:, c, j * P:(j + 1) * P], wm[:, 0, :],
                                          start=False, stop=j == 3)
                        m.then_inc(mixed, 1)

                    turn(0)
                    for c in range(1, U):
                        turn(c)
                        mix(c - 1)
                    mix(U - 1)

    def last_layers():
        tag = "z_"
        with stage() as ph:
            def tmp(name, shape, dt=F32):
                return ph.enter_context(nc.sbuf_tensor(tag + name, shape, dt))

            sums, xin, x3 = tmp("sums", [P, 16, P]), tmp("xin", [P, 16, P]), tmp("x3", [P, 16, P])
            hin, agg_t = tmp("hin", [P, U, CH]), tmp("agg_t", [P, U, CH])
            xn, hs, m1, m2, run, hid = (tmp(n, [P, 2, CH]) for n in ("xn", "hs", "m1", "m2", "run", "hid"))
            hn, part, res = tmp("hn", [P, 8, P]), tmp("part", [P, 8, P]), tmp("res", [P, 8, P])
            weight, kept, carry = tmp("weight", [P, 2, CH]), tmp("kept", [P, 2, CH], BF16), tmp("carry", [P, 1])
            st = [tmp(f"st{k}", [P, 8, 6]) for k in range(2)]
            mv = [tmp(f"mv{k}", [P, 5, 8]) for k in range(2)]
            at_i, to_i = tmp("at_i", [P, 8], I32), tmp("to_i", [P, 8], I32)
            (own, var_ready, sd_ready, normed, slot, got_d, loaded_h, loaded_x, loaded_w, loaded_k, turned, t_ready, mixed,
             x3_ready, applied, turned_s, hs_ready, mm1, m1_ready, m2_ready, scanned, carried, mm2, hid_ready, turned_o,
             part_ready, res_ready, put, slot_put) = (
                sem(tag + n) for n in ("own", "var", "sd", "normed", "slot", "got_d", "loaded_h", "loaded_x", "loaded_w",
                                       "loaded_k", "turned", "t", "mixed", "x3", "applied", "turned_s", "hs", "mm1", "m1",
                                       "m2", "scanned", "carried", "mm2", "hid", "turned_o", "part", "res", "put",
                                       "slot_put"))
            got = [sem(f"{tag}got{k}") for k in range(2)]
            block = ph.enter_context(nc.Block())

            def flat(t, c):
                return t[:, 4 * c:4 * c + 4, :].rearrange("p t f -> p (t f)")

            @block.gpsimd
            def _(pool):
                def gather(g):
                    pool.wait_ge(got[0], 64 * g)
                    pool.wait_ge(got[1], 64 * g)
                    pool.tensor_copy(at_i[:, :], src_e[:, bass.ds(g * 8, 8)]).then_inc(slot, 1)
                    pool.wait_ge(slot, g + 1)
                    pool.wait_ge(turned, 4 * g)
                    apart(pool, passed)
                    for t in range(8):
                        pool.indirect_dma_start(sums[:, 8 + t, :], None, agg[1][:, :],
                                                bass.IndirectOffsetOnAxis(ap=at_i[:, t:t + 1], axis=0),
                                                bounds_check=ZR, oob_is_err=False).then_inc(got[t // 4], 16)

                def scatter(g):
                    pool.wait_ge(put, 128 * g)
                    pool.tensor_copy(to_i[:, :], put_i[:, bass.ds(g * 8, 8)]).then_inc(slot_put, 1)
                    pool.wait_ge(slot_put, g + 1)
                    pool.wait_ge(res_ready, 2 * g + 2)
                    apart(pool, passed)
                    for t in range(8):
                        pool.indirect_dma_start(out[:, :], bass.IndirectOffsetOnAxis(ap=to_i[:, t:t + 1], axis=0),
                                                res[:, t, :], None, bounds_check=N - 1, oob_is_err=False).then_inc(put, 16)

                gather(0)

                @groups(pool, GE - 1)
                def _(g):
                    gather(g + 1)
                    scatter(g)

                pool.wait_ge(put, 128 * (GE - 1))
                pool.tensor_copy(to_i[:, :], put_i[:, (GE - 1) * 8:GE * 8]).then_inc(slot_put, 1)
                pool.wait_ge(slot_put, GE)
                pool.wait_ge(res_ready, 2 * GE)
                for t in range(8):
                    pool.indirect_dma_start(out[:, :], bass.IndirectOffsetOnAxis(ap=to_i[:, t:t + 1], axis=0),
                                            res[:, t, :], None, bounds_check=N - 1, oob_is_err=False).then_inc(put, 16)
                pool.wait_ge(put, 128 * GE)

            @block.sync
            def _(sp):
                edge_w = A["edge_weight"].rearrange("(a n) -> a n", a=1)

                def load(g, cols_w=HALF):
                    sp.wait_ge(turned, 4 * g)
                    sp.dma_start(sums[:, 0:8, :], tiles(agg[1], g * HALF, 8)).then_inc(got_d, 16)
                    sp.wait_ge(mixed, 4 * g)
                    sp.dma_start(hin[:, :, :].rearrange("p c n -> p (c n)"),
                                 he[:, bass.ds(g * GRP, GRP)]).then_inc(loaded_h, 16)
                    sp.wait_ge(x3_ready, 4 * g)
                    for k in range(2):
                        sp.dma_start(xin[:, 8 * k:8 * k + 8, :], tiles(xe, g * GRP + k * HALF, 8)).then_inc(loaded_x, 16)
                    sp.wait_ge(m2_ready, 2 * g)
                    apart(sp, passed)
                    sp.dma_start(weight[:, :, :].rearrange("p c n -> p (c n)")[:, 0:cols_w],
                                 edge_w[:, bass.ds(g * HALF, cols_w)].to_broadcast([P, cols_w])).then_inc(loaded_w, 16)
                    sp.wait_ge(scanned, 2 * g)
                    sp.dma_start(kept[:, :, :].rearrange("p c n -> p (c n)"), keep_line[bass.ds(g * 8, 8), :]
                                 .rearrange("(a t) p -> a (t p)", a=1).to_broadcast([P, HALF])).then_inc(loaded_k, 16)

                @groups(sp, GE - 1)
                def _(g):
                    load(g)

                load(GE - 1, E - (GE - 1) * HALF)

            @block.scalar
            def _(act):
                @groups(act, GE)
                def _(g):
                    for c in range(U):
                        act.wait_ge(turned, 4 * g + c + 1)
                        reuse(act, mixed, 4 * g + c - 3)
                        act.activation(agg_t[:, c, :], bank[0][:, c, :], ACT.Copy).then_inc(t_ready, 1)
                    for k in range(2):
                        act.wait_ge(var_ready, 2 * g + k + 1)
                        ln_root(act, mv[k], 8, sd_ready)
                    for c in range(2):
                        act.wait_ge(turned_s, 2 * g + c + 1)
                        reuse(act, mm1, 2 * g + c - 1)
                        act.activation(hs[:, c, :], bank[0][:, c, :], ACT.Relu).then_inc(hs_ready, 1)
                    for c in range(2):
                        act.wait_ge(mm1, 2 * g + c + 1)
                        reuse(act, m2_ready, 2 * g + c - 1)
                        act.activation(m1[:, c, :], bank[0][:, 2 + c, :], ACT.Relu, bias=gcols[:, 0:1]).then_inc(m1_ready, 1)
                    for c in range(2):
                        act.wait_ge(mm2, 2 * g + c + 1)
                        reuse(act, turned_o, 2 * g + c - 1)
                        act.activation(hid[:, c, :], bank[0][:, c, :], ACT.Relu, bias=gcols[:, 1:2]).then_inc(hid_ready, 1)

            @block.vector
            def _(dve):
                steps = Steps(dve, own, 2 * LN_STEPS)
                dve.memset(carry[:, :], 0.0).then_inc(carried, 1)
                @groups(dve, GE)
                def _(g):
                    steps.at(g)
                    for c in range(U):
                        dve.wait_ge(mixed, 4 * g + c + 1)
                        dve.wait_ge(loaded_x, 32 * g + 32)
                        dve.scalar_tensor_tensor(flat(x3, c), bank[1][:, c, :], 0.0, flat(xin, c), ALU.max,
                                                 ALU.add).then_inc(x3_ready, 1)
                    for k in range(2):
                        dve.wait_ge(x3_ready, 4 * g + 2 * k + 2)
                        ln_sums(dve, steps, x3[:, 8 * k:8 * k + 8, :], st[k], mv[k], 8, var_ready)
                    for k in (1, 0):
                        dve.wait_ge(sd_ready, 2 * g + k + 1)
                        if k:
                            dve.wait_ge(turned_s, 2 * g)
                            ln_apply(dve, steps, xn[:, :, :].rearrange("p c (t f) -> p (c t) f", f=P), x3[:, 8:16, :],
                                     mv[k], 8, normed)
                        else:
                            ln_apply(dve, steps, hn, x3[:, 0:8, :], mv[k], 8, applied)
                    for c in range(2):
                        dve.wait_ge(applied, 2 * g + c + 1)
                        reuse(dve, res_ready, 2 * g + c - 1)
                        dve.scalar_tensor_tensor(flat(part, c), flat(hn, c), 0.0, flat(x3, c), ALU.max,
                                                 ALU.add).then_inc(part_ready, 1)
                    for c in range(2):
                        dve.wait_ge(m1_ready, 2 * g + c + 1)
                        dve.wait_ge(loaded_w, 16 * g + 16)
                        reuse(dve, scanned, 2 * g + c - 1)
                        dve.tensor_tensor(m2[:, c, :], m1[:, c, :], weight[:, c, :], ALU.mult).then_inc(m2_ready, 1)
                    dve.wait_ge(loaded_k, 16 * g + 16)
                    dve.wait_ge(mm2, 2 * g)
                    for c in range(2):
                        dve.wait_ge(m2_ready, 2 * g + c + 1)
                        scan(dve, g, c, run, kept, m2, carry, scanned, carried)
                    for c in range(2):
                        dve.wait_ge(turned_o, 2 * g + c + 1)
                        dve.wait_ge(part_ready, 2 * g + c + 1)
                        dve.wait_ge(put, 128 * g)
                        dve.tensor_tensor(flat(res, c), flat(part, c), bank[1][:, c, :], ALU.add).then_inc(res_ready, 1)

            @block.tensor
            def _(pe):
                @groups(pe, GE)
                def _(g):
                    for c in range(U):
                        if c < 2:
                            pe.wait_ge(got_d, 16 * g + 16)
                        else:
                            pe.wait_ge(got[c - 2], 64 * g + 64)
                        pe.wait_ge(hid_ready, 2 * g)
                        for j in range(4):
                            t = pe.transpose(bank[0][:, c, j * P:(j + 1) * P], sums[:, 4 * c + j, :], ident[:, :])
                        t.then_inc(turned, 1)
                    for c in range(U):
                        pe.wait_ge(loaded_h, 16 * g + 16)
                        pe.wait_ge(t_ready, 4 * g + c + 1)
                        pe.wait_ge(res_ready, 2 * g)
                        pe.matmul(bank[1][:, c, :], row0[:, :], c_row[:, :, :].rearrange("p a f -> p (a f)"),
                                  start=True, stop=False)
                        for j in range(4):
                            s = slice(j * P, (j + 1) * P)
                            pe.matmul(bank[1][:, c, s], hin[:, c, s], wm[:, 0, :], start=False, stop=False)
                            m = pe.matmul(bank[1][:, c, s], agg_t[:, c, s], w_om[:, :], start=False, stop=j == 3)
                        m.then_inc(mixed, 1)
                    for c in range(2):
                        pe.wait_ge(normed, 2 * g + c + 1)
                        for j in range(4):
                            t = pe.transpose(bank[0][:, c, j * P:(j + 1) * P], xn[:, c, j * P:(j + 1) * P], ident[:, :])
                        t.then_inc(turned_s, 1)
                    for c in range(2):
                        pe.wait_ge(hs_ready, 2 * g + c + 1)
                        pe.matmul(bank[0][:, 2 + c, :], wg1[:, :], hs[:, c, :], start=True, stop=True).then_inc(mm1, 1)
                    for c in range(2):
                        pe.wait_ge(scanned, 2 * g + c + 1)
                        pe.matmul(bank[0][:, c, :], wg2[:, :], run[:, c, :], start=True, stop=True).then_inc(mm2, 1)
                    for c in range(2):
                        pe.wait_ge(hid_ready, 2 * g + c + 1)
                        pe.wait_ge(x3_ready, 4 * g + 4)
                        for j in range(4):
                            t = pe.transpose(bank[1][:, c, j * P:(j + 1) * P], hid[:, c, j * P:(j + 1) * P], ident[:, :])
                        t.then_inc(turned_o, 1)

    first(True)
    first(False)
    for l in range(LAYERS):
        messages(l)
        if l:
            layer(l, True)
        layer(l, False)
        batch_norm(l)
    leave()
    for r in range(3):
        mean(r)
    finish()
    logits()
    softmax()
    last_layers()




NAMES = ["x", "src", "dst", "edge_attr_3", "edge_attr_32", "edge_weight",
         *(f"L0_gnn_{n}" for n in ("We", "be", "W1", "b1", "W2", "b2", "gamma", "beta")),
         *(f"L2_gnn_{n}" for n in ("Wq", "Wk", "Wv", "We", "Wo", "bo", "Wm", "bm")),
         *(f"L3_gnn_{n}" for n in ("W1", "b1", "W2", "b2"))]


def kernel(**inputs):
    import numpy as _np
    import concourse.bacc as _bacc
    from concourse import mybir as _mybir
    from concourse.bass_utils import run_bass_kernel_spmd as _run

    nc = _bacc.Bacc("TRN2", target_bir_lowering=False, num_devices=1)
    arrays, aps = {}, {}
    for name in NAMES:
        a = _np.ascontiguousarray(inputs[name])
        arrays[f"in_{name}"] = a
        aps[name] = nc.dram_tensor(f"in_{name}", a.shape, _mybir.dt.from_np(a.dtype), kind="ExternalInput").ap()
    out = nc.dram_tensor("out", (N, P), F32, kind="ExternalOutput").ap()
    gnn_kernel(nc, aps, out)
    r = _run(nc, [arrays], core_ids=[0])
    return r.results[0]["out"]
```

```python
import concourse.bass as bass
from concourse import mybir
from contextlib import ExitStack, contextmanager

F32 = mybir.dt.float32
BF16 = mybir.dt.bfloat16
I32 = mybir.dt.int32
ALU = mybir.AluOpType
ACT = mybir.ActivationFunctionType
AX = mybir.AxisListType
REDUCE_MAX = bass.bass_isa.ReduceOp.max

P = 128
N = 100000
E = 25000
CH = 512
U = 4
GRP = U * CH
HALF = GRP // 2
GD = -(-N // GRP)
NP = GD * GRP
GE = -(-E // HALF)
EP = GE * HALF
ET = EP // P
ZR = EP
TAIL_P = (N - (2 * GD - 1) * HALF) // 8
H = 4
HD = P // H
LAYERS = 3
EA = 32
EB = 3
EPS = 1e-5
RES = 0.1
FAR = 1000000
assert N % 8 == 0 and 0 < TAIL_P <= P


class Steps:

    def __init__(self, eng, sem, per):
        self.eng, self.sem, self.per, self.k, self.base = eng, sem, per, 0, 0

    def at(self, i):
        self.base, self.k = i * self.per, 0

    def did(self, ins):
        self.k += 1
        assert self.k <= self.per
        ins.then_inc(self.sem, 1)

    def sync(self):
        self.eng.wait_ge(self.sem, self.base + self.k)


def groups(eng, n, start=0, written=None, ended=0):
    written = start + 1 if written is None else written

    def run(body):
        for g in range(start, written):
            body(g)
        with eng.Fori(written, n - ended) as g:
            body(g)
        for g in range(n - ended, n):
            body(g)

    return run


def reuse(eng, sem, n):
    if not isinstance(n, int) or n > 0:
        eng.wait_ge(sem, n)


def apart(eng, passed):
    eng.sem_inc(passed, 1)


def gnn_kernel(nc, A, out):
    ctx = ExitStack()
    with ctx:
        build(nc, ctx, A, out)


def build(nc, ctx, A, out):
    def dram(name, shape, dt):
        return nc.dram_tensor(name, shape, dt).ap()

    def keep(name, shape, dt=F32):
        return ctx.enter_context(nc.sbuf_tensor(name, shape, dt))

    own_sems = []

    def sem(name):
        own_sems.append(nc.alloc_semaphore(name))
        return own_sems[-1]

    @contextmanager
    def stage():
        with ExitStack() as ph:
            yield ph
        nc.clear_and_free_semaphores(own_sems)
        own_sems.clear()
        nc.all_engine_barrier()

    bank = [ctx.enter_context(nc.psum_tensor(f"psum{i}", [P, U, CH], F32)) for i in range(2)]

    dst_line = dram("dst_line", [EP + 2], I32)
    table = dram("table", [NP, 1], I32)
    dense_mask = dram("dense_mask", [GD * 16, P], BF16)
    edge_mask = dram("edge_mask", [ET, P], BF16)
    keep_line = dram("keep_line", [ET, P], BF16)
    pad_line = dram("pad_line", [1, EP], F32)
    attr_t = dram("attr_t", [EA + EB, EP], F32)
    zd, hd = dram("zd", [P, NP], F32), dram("hd", [P, NP], F32)
    ze, he = dram("ze", [P, GE * GRP], F32), dram("he", [P, GE * GRP], F32)
    xe = dram("xe", [GE * GRP, P], F32)
    agg = [dram(f"agg{i}", [EP + P, P], F32) for i in range(2)]
    x2d = dram("x2d", [EP + P, P], F32)
    attn_t, v_t = dram("attn_t", [P, EP], F32), dram("v_t", [P, EP], F32)

    x = A["x"]

    def x_half(ap, k):
        return ap[bass.ds(k * HALF, HALF), :].rearrange("(p j) f -> p (j f)", p=P)

    def x_tail(ap):
        k0 = (2 * GD - 1) * HALF
        return ap[k0:N, :].rearrange("(p j) f -> p (j f)", p=TAIL_P)

    def tiles(ap, row, n):
        return ap[bass.ds(row, n * P), :].rearrange("(t p) f -> p t f", p=P)

    ident = keep("ident", [P, P])
    w_e = keep("w_e", [P, LAYERS, P])
    w1, w2 = keep("w1", [P, LAYERS, P]), keep("w2", [P, LAYERS, P])
    cols = keep("cols", [P, 5 * LAYERS])
    be, b1, b2, gamma, beta = (cols[:, LAYERS * k:LAYERS * k + LAYERS] for k in range(5))
    wq, wk, wv, wo = (keep(n, [P, P]) for n in ("wq", "wk", "wv", "wo"))
    wm = keep("wm", [P, 2, P])
    w_bias = keep("w_bias", [P, P])
    w_bias4 = keep("w_bias4", [EB, H])
    heads = keep("heads", [P, P])
    wg1, wg2 = keep("wg1", [P, P]), keep("wg2", [P, P])
    gcols = keep("gcols", [P, 3])
    b2_row = keep("b2_row", [P, P])
    w_om = keep("w_om", [P, P])
    c_row = keep("c_row", [P, U, P])
    c_parts = keep("c_parts", [P, U, P], BF16)
    three = keep("three", [P, P], BF16)
    tenth = keep("tenth", [P, P])
    row0 = keep("row0", [P, P])
    big0 = keep("big0", [P, P], BF16)
    eps = keep("eps", [P, 1])
    src_i, gdst_i, put_i, src_e, dst_e, num_i = (
        keep(n, [P, ET], I32) for n in ("src_i", "gdst_i", "put_i", "src_e", "dst_e", "num_i"))
    rcount = keep("rcount", [P, ET])
    stat_all = keep("stat_all", [P, GD * U + GE * 2, 6])
    norm_a, norm_c = keep("norm_a", [P, LAYERS]), keep("norm_c", [P, LAYERS])
    top = keep("top", [P, 2])

    passed = ctx.enter_context(nc.semaphore("passed"))

    with stage() as ph:
        def tmp(name, shape, dt=F32):
            return ph.enter_context(nc.sbuf_tensor(name, shape, dt))

        wo_t = tmp("wo_t", [P, P])
        bm_row = tmp("bm_row", [1, P])
        part = tmp("part", [1, 3, P], BF16)
        left = tmp("left", [1, 2, P])
        split = sem("c_split")
        loaded, zeroed, made, turned, did = (sem("c_" + n) for n in ("loaded", "zeroed", "made", "turned", "did"))
        block = ph.enter_context(nc.Block())
        loads = [(w_e[0:EA, :, :], A["L0_gnn_We"].rearrange("l e h -> e l h")),
                 (w1[:, :, :], A["L0_gnn_W1"].rearrange("l e h -> e l h")),
                 (w2[:, :, :], A["L0_gnn_W2"].rearrange("l e h -> e l h"))]
        for k, n in enumerate(("be", "b1", "b2", "gamma", "beta")):
            loads.append((cols[:, LAYERS * k:LAYERS * k + LAYERS], A["L0_gnn_" + n].rearrange("l h -> h l")))
        for t, n in ((wq, "Wq"), (wk, "Wk"), (wv, "Wv"), (wo, "Wo")):
            loads.append((t[:, :], A["L2_gnn_" + n]))
        loads += [(wm[:, :, :], A["L2_gnn_Wm"].rearrange("(a k) h -> k a h", a=2)),
                  (w_bias4[:, :], A["L2_gnn_We"]),
                  (wg1[:, :], A["L3_gnn_W1"]), (wg2[:, :], A["L3_gnn_W2"]),
                  (gcols[:, 0:1], A["L3_gnn_b1"].rearrange("(h a) -> h a", a=1)),
                  (gcols[:, 1:2], A["L3_gnn_b2"].rearrange("(h a) -> h a", a=1)),
                  (gcols[:, 2:3], A["L2_gnn_bo"].rearrange("(h a) -> h a", a=1)),
                  (bm_row[:, :], A["L2_gnn_bm"].rearrange("(a h) -> a h", a=1)),
                  (b2_row[:, :], A["L3_gnn_b2"].rearrange("(a h) -> a h", a=1).to_broadcast([P, P]))]

        @block.sync
        def _(sp):
            sp.wait_ge(zeroed, 1)
            with nc.allow_non_contiguous_dma(reason="biases as columns, once"):
                for to, of in loads:
                    sp.dma_start(to, of).then_inc(loaded, 16)
            sp.wait_ge(loaded, 16 * len(loads))

        @block.gpsimd
        def _(pool):
            pool.memset(w_e[:, :, :], 0.0).then_inc(zeroed, 1)
            pool.memset(ident[:, :], 0.0).then_inc(made, 1)
            pool.wait_ge(made, 1)
            pool.affine_select(out=ident[:, :], in_=ident[:, :], compare_op=ALU.not_equal, fill=1.0,
                               base=0, pattern=[[-1, P]], channel_multiplier=1).then_inc(made, 1)

        @block.vector
        def _(dve):
            for t, v in ((heads, 0.0), (w_bias, 0.0), (row0, 0.0), (big0, 0.0), (eps, EPS)):
                dve.memset(t[:, :], v).then_inc(did, 1)
            dve.memset(c_row[:, :, :], 0.0).then_inc(did, 1)
            dve.wait_ge(did, 6)
            for h in range(H):
                s = slice(h * HD, (h + 1) * HD)
                dve.memset(heads[s, s], HD ** -0.5).then_inc(did, 1)
            dve.memset(row0[0:1, :], 1.0).then_inc(did, 1)
            dve.memset(big0[0:1, :], -1e30).then_inc(did, 1)
            dve.memset(w_bias[HD:HD + 1, :], -1e30).then_inc(did, 1)
            dve.wait_ge(loaded, 16 * len(loads))
            dve.tensor_copy(w_bias[0:EB, :].rearrange("e (h d) -> e h d", h=H),
                            w_bias4[:, :].unsqueeze(2).to_broadcast([EB, H, HD])).then_inc(did, 1)
            dve.wait_ge(turned, 1)
            dve.tensor_copy(wo_t[:, :], bank[0][:, 0, 0:P]).then_inc(did, 1)
            dve.wait_ge(turned, 3)
            dve.tensor_copy(w_om[:, :], bank[0][:, 1, 0:P]).then_inc(did, 1)
            dve.tensor_tensor(c_row[0:1, 0, :], bank[0][0:1, 2, 0:P], bm_row[:, :], ALU.add).then_inc(did, 1)
            dve.wait_ge(did, 17)
            for k in range(1, U):
                dve.tensor_copy(c_row[0:1, k, :], c_row[0:1, 0, :]).then_inc(did, 1)
            dve.memset(c_parts[:, :, :], 0.0).then_inc(split, 1)
            dve.memset(three[:, :], 0.0).then_inc(split, 1)
            dve.tensor_copy(part[:, 0, :], c_row[0:1, 0, :]).then_inc(split, 1)
            dve.wait_ge(split, 3)
            dve.tensor_tensor(left[:, 0, :], c_row[0:1, 0, :], part[:, 0, :], ALU.subtract).then_inc(split, 1)
            dve.wait_ge(split, 4)
            dve.tensor_copy(part[:, 1, :], left[:, 0, :]).then_inc(split, 1)
            dve.wait_ge(split, 5)
            dve.tensor_tensor(left[:, 1, :], left[:, 0, :], part[:, 1, :], ALU.subtract).then_inc(split, 1)
            dve.wait_ge(split, 6)
            dve.tensor_copy(part[:, 2, :], left[:, 1, :]).then_inc(split, 1)
            dve.wait_ge(split, 7)
            for k in range(3):
                dve.memset(three[32 * k:32 * k + 1, :], 1.0).then_inc(split, 1)
                for a in range(U):
                    dve.tensor_copy(c_parts[32 * k:32 * k + 1, a, :], part[:, k, :]).then_inc(split, 1)
            dve.wait_ge(made, 2)
            dve.tensor_scalar(tenth[:, :], ident[:, :], RES, None, ALU.mult).then_inc(split, 1)

        @block.tensor
        def _(pe):
            pe.wait_ge(loaded, 16 * len(loads))
            pe.wait_ge(made, 2)
            pe.transpose(bank[0][:, 0, 0:P], wo[:, :], ident[:, :]).then_inc(turned, 1)
            pe.matmul(bank[0][0:1, 2, 0:P], gcols[:, 2:3], wm[:, 1, :], start=True, stop=True).then_inc(turned, 1)
            pe.wait_ge(did, 15)
            pe.matmul(bank[0][:, 1, 0:P], wo_t[:, :], wm[:, 1, :], start=True, stop=True).then_inc(turned, 1)

    RT = ET // 2
    FULL = E // P
    REST = E - FULL * P
    with stage() as ph:
        def tmp(name, shape, dt=F32):
            return ph.enter_context(nc.sbuf_tensor(name, shape, dt))

        ends = tmp("ends", [1, 2], I32)
        near = tmp("near", [RT, 2, 4, P], I32)
        nearf = tmp("nearf", [RT, 2, 4, P])
        last = tmp("last", [RT, 2, P])
        keepb = tmp("keepb", [RT, 2, P], BF16)
        maskb = tmp("maskb", [RT, 2, P], BF16)
        colf = tmp("colf", [P, 3, ET])
        putf = tmp("putf", [P, ET])
        fill = tmp("fill", [P, NP // P], I32)
        zero, one = tmp("zero", [P, 2 * P]), tmp("one", [1, EP - E])
        l1, l2, l3, zeroed, did, turned, numbered, stored = (
            sem("i_" + n) for n in ("l1", "l2", "l3", "zeroed", "did", "turned", "numbered", "stored"))
        l4, l5 = sem("i_l4"), sem("i_l5")
        block = ph.enter_context(nc.Block())
        @block.gpsimd
        def _(pool):
            pool.iota(num_i[:, :], pattern=[[P, ET]], base=0, channel_multiplier=1).then_inc(numbered, 1)
            pool.wait_ge(numbered, 1)

        @block.sync
        def _(sp):
            sp.wait_ge(zeroed, 7)
            for a, name in ((0, "src"), (1, "dst")):
                v = A[name]
                sp.dma_start(near[:, 0, a, :], v[0:RT * P].rearrange("(t p) -> t p", p=P)).then_inc(l1, 16)
                sp.dma_start(near[0:FULL - RT, 1, a, :],
                             v[RT * P:FULL * P].rearrange("(t p) -> t p", p=P)).then_inc(l1, 16)
                sp.dma_start(near[FULL - RT:FULL - RT + 1, 1, a, 0:REST],
                             v[FULL * P:E].rearrange("(t p) -> t p", t=1)).then_inc(l1, 16)
            sp.dma_start(table.rearrange("(p c) a -> p (c a)", p=P), fill[:, :]).then_inc(l5, 16)
            sp.wait_ge(l5, 16)
            sp.dma_start(table[N:NP, :].rearrange("(p c) a -> p (c a)", p=32), zero[0:32, 0:(NP - N) // 32].bitcast(I32)).then_inc(l5, 16)
            for a in (*agg, x2d):
                sp.dma_start(a[EP:EP + P, :], zero[:, 0:P]).then_inc(l4, 16)
            sp.dma_start(pad_line[0:1, 0:E].rearrange("a (p n) -> (a p) n", p=125),
                         zero[0:125, 0:E // 125]).then_inc(l4, 16)
            sp.dma_start(pad_line[0:1, E:EP], one[:, :]).then_inc(l4, 16)
            sp.dma_start(dst_line[0:1].rearrange("(a b) -> a b", a=1), ends[:, 0:1]).then_inc(l2, 16)
            sp.dma_start(dst_line[EP + 1:EP + 2].rearrange("(a b) -> a b", a=1), ends[:, 1:2]).then_inc(l2, 16)
            sp.wait_ge(l1, 96)
            sp.dma_start(dst_line[1:EP + 1].rearrange("(s t p) -> t s p", s=2, p=P), near[:, :, 1, :]).then_inc(l2, 16)
            sp.wait_ge(l2, 48)
            for a, at in ((2, 0), (3, 2)):
                sp.dma_start(near[:, :, a, :],
                             dst_line[at:at + EP].rearrange("(s t p) -> t s p", s=2, p=P)).then_inc(l3, 16)
            sp.wait_ge(did, 4)
            sp.dma_start(keep_line.rearrange("(s t) p -> t s p", s=2), keepb[:, :, :]).then_inc(stored, 16)
            sp.dma_start(edge_mask.rearrange("(s t) p -> t s p", s=2), maskb[:, :, :]).then_inc(stored, 16)
            sp.wait_ge(stored, 32)
            sp.wait_ge(l4, 80)
            sp.wait_ge(l5, 32)

        @block.vector
        def _(dve):
            dve.memset(near[:, :, 0, :], 0).then_inc(zeroed, 1)
            dve.memset(near[:, :, 1, :], N).then_inc(zeroed, 1)
            dve.memset(ends[:, 0:1], -1).then_inc(zeroed, 1)
            dve.memset(ends[:, 1:2], N).then_inc(zeroed, 1)
            dve.memset(zero[:, :], 0.0).then_inc(zeroed, 1)
            dve.memset(fill[:, :], ZR).then_inc(zeroed, 1)
            dve.memset(one[:, :], 1.0).then_inc(zeroed, 1)
            dve.wait_ge(l3, 32)
            dve.tensor_copy(nearf[:, :, :, :], near[:, :, :, :]).then_inc(did, 1)
            dve.wait_ge(did, 1)
            dve.tensor_tensor(keepb[:, :, :], nearf[:, :, 1, :], nearf[:, :, 2, :], ALU.is_equal).then_inc(did, 1)
            dve.tensor_tensor(maskb[:, :, :], nearf[:, :, 1, :], nearf[:, :, 3, :], ALU.is_equal).then_inc(did, 1)
            dve.tensor_tensor(last[:, :, :], nearf[:, :, 1, :], nearf[:, :, 3, :], ALU.not_equal).then_inc(did, 1)
            dve.wait_ge(turned, 6)
            dve.tensor_copy(colf[:, :, :].rearrange("p a (s t) -> p s a t", s=2),
                            bank[0][:, 0:2, 0:3 * RT].rearrange("p s (a t) -> p s a t", a=3)).then_inc(did, 1)
            dve.wait_ge(did, 5)
            dve.tensor_copy(src_i[:, :], colf[:, 0, :]).then_inc(did, 1)
            dve.tensor_scalar(gdst_i[:, :], colf[:, 1, :], float(N - 1), None, ALU.min).then_inc(did, 1)
            dve.tensor_scalar(putf[:, :], colf[:, 2, :], -float(FAR), float(FAR), ALU.mult, ALU.add).then_inc(did, 1)
            dve.wait_ge(did, 8)
            dve.tensor_tensor(put_i[:, :], putf[:, :], colf[:, 1, :], ALU.add).then_inc(did, 1)

        @block.tensor
        def _(pe):
            pe.wait_ge(did, 4)
            for s in range(2):
                for a, v in enumerate((nearf[:, s, 0, :], nearf[:, s, 1, :], last[:, s, :])):
                    pe.transpose(bank[0][:, s, a * RT:(a + 1) * RT], v, ident[0:RT, 0:RT]).then_inc(turned, 1)

    with stage() as ph:
        def tmp(name, shape, dt=F32):
            return ph.enter_context(nc.sbuf_tensor(name, shape, dt))

        attr = tmp("attr", [P, 8, P])
        attr_out = tmp("attr_out", [EA + EB, HALF])
        kept = tmp("kept", [P, HALF], BF16)
        ones = tmp("ones", [P, CH])
        run = tmp("run", [P, 2, CH])
        carry = tmp("carry", [P, 1])
        loaded, loadk, did, turned, moved, counted, picked, stored = (
            sem("e_" + n) for n in ("loaded", "loadk", "did", "turned", "moved", "counted", "picked", "stored"))
        at_i = tmp("at_i", [P, 2, 8], I32)
        num = tmp("num", [P, 2, 8], I32)
        slot = sem("t_slot")
        put = [sem(f"t_put{r}") for r in range(2)]
        fresh = sem("e_fresh")
        block = ph.enter_context(nc.Block())
        WHOLE = (E - (GE - 1) * HALF) // P

        @block.gpsimd
        def _(pool):
            def scatter(i, g, r):
                pool.wait_ge(put[r], 128 * i)
                pool.tensor_copy(at_i[:, r, :], put_i[:, bass.ds(g * 8, 8)]).then_inc(slot, 1)
                pool.tensor_copy(num[:, r, :], num_i[:, bass.ds(g * 8, 8)]).then_inc(slot, 1)
                pool.wait_ge(slot, g * 2 + 2)
                apart(pool, passed)
                for t in range(8):
                    pool.indirect_dma_start(table[:, :], bass.IndirectOffsetOnAxis(ap=at_i[:, r, t:t + 1], axis=0),
                                            num[:, r, t:t + 1], None, bounds_check=N - 1,
                                            oob_is_err=False).then_inc(put[r], 16)

            @groups(pool, GE // 2)
            def _(i):
                for r in range(2):
                    scatter(i, i * 2 + r, r)

            if GE % 2:
                scatter(GE // 2, GE - 1, 0)
            for r in range(2):
                pool.wait_ge(put[r], 128 * ((GE + 1 - r) // 2))

        @block.sync
        def _(sp):
            def load(i, whole=8, rest=0):
                sp.wait_ge(turned, 2 * i)
                for a, name in ((slice(0, EA), "edge_attr_32"), (slice(EA, EA + EB), "edge_attr_3")):
                    v = A[name]
                    sp.dma_start(attr[:, 0:whole, a], tiles(v, i * HALF, whole)).then_inc(loaded, 16)
                    if rest:
                        sp.dma_start(attr[0:rest, whole, a], v[i * HALF + whole * P:E, :]).then_inc(loaded, 16)
                sp.wait_ge(counted, 2 * i)
                sp.dma_start(kept[:, :], keep_line[bass.ds(i * 8, 8), :].rearrange("(a t) p -> a (t p)", a=1)
                             .to_broadcast([P, HALF])).then_inc(loadk, 16)

            def store(i):
                sp.wait_ge(moved, 2 * i + 2)
                sp.dma_start(attr_t[:, bass.ds(i * HALF, HALF)], attr_out[:, :]).then_inc(stored, 16)

            sp.wait_ge(fresh, 1)
            with nc.allow_non_contiguous_dma(reason="three edge features"):
                load(0)
                with sp.Fori(0, GE - 2) as i:
                    load(i + 1)
                    store(i)
                load(GE - 1, WHOLE, E - (GE - 1) * HALF - WHOLE * P)
                store(GE - 2)
            store(GE - 1)
            sp.wait_ge(stored, 16 * GE)

        def each(eng, body):
            body(0, False)
            with eng.Fori(1, GE - 1) as i:
                body(i, False)
            body(GE - 1, True)

        @block.tensor
        def _(pe):
            def body(i, tail):
                for c in range(2):
                    pe.wait_ge(loaded, 32 * i + (64 if tail else 32))
                    reuse(pe, moved, 2 * i + c - 1)
                    for j in range(4):
                        t = pe.transpose(bank[0][:, c, j * P:(j + 1) * P], attr[:, 4 * c + j, :], ident[:, :])
                    t.then_inc(turned, 1)
                for c in range(2):
                    pe.wait_ge(counted, 2 * i + c + 1)
                    reuse(pe, did, 2 * i + c - 1)
                    for j in range(4):
                        t = pe.matmul(bank[1][:, c, j:j + 1], run[:, c, j * P:(j + 1) * P], row0[:, 0:1],
                                      start=True, stop=True)
                    t.then_inc(picked, 1)

            each(pe, body)

        @block.scalar
        def _(act):
            def body(i, tail):
                for c in range(2):
                    act.wait_ge(turned, 2 * i + c + 1)
                    act.wait_ge(stored, 16 * i)
                    act.activation(attr_out[:, c * CH:(c + 1) * CH], bank[0][0:EA + EB, c, :],
                                   ACT.Copy).then_inc(moved, 1)

            each(act, body)

        @block.vector
        def _(dve):
            dve.memset(attr[:, :, :], 0.0).then_inc(fresh, 1)
            dve.memset(ones[:, :], 1.0).then_inc(fresh, 1)
            dve.memset(carry[:, :], 0.0).then_inc(fresh, 1)
            dve.wait_ge(fresh, 3)

            def body(i, tail):
                dve.wait_ge(loadk, 16 * i + 16)
                dve.wait_ge(picked, 2 * i)
                for c in range(2):
                    if c:
                        dve.wait_ge(counted, 2 * i + c)
                    else:
                        dve.wait_ge(fresh, i + 3)
                    dve.tensor_tensor_scan(run[:, c, :], kept[:, c * CH:(c + 1) * CH], ones[:, :],
                                           run[:, 0, CH - 1:CH] if c else carry[:, :],
                                           ALU.mult, ALU.add).then_inc(counted, 1)
                dve.wait_ge(counted, 2 * i + 2)
                dve.tensor_copy(carry[:, :], run[:, 1, CH - 1:CH]).then_inc(fresh, 1)
                for c in range(2):
                    dve.wait_ge(picked, 2 * i + c + 1)
                    dve.tensor_scalar(rcount[:, bass.ds(i * 8 + c * 4, 4)], bank[1][:, c, 0:4], 1.0, None,
                                      ALU.mult).then_inc(did, 1)

            each(dve, body)
            dve.wait_ge(did, 2 * GE)
            dve.reciprocal(rcount[:, :], rcount[:, :]).then_inc(did, 1)

    with stage() as ph:
        def tmp(name, shape, dt=F32):
            return ph.enter_context(nc.sbuf_tensor(name, shape, dt))

        mrow = tmp("mrow", [P, GD * 16], I32)
        mrowf = tmp("mrowf", [P, GD * 16])
        mask_t = tmp("mask_t", [P, 7, P], BF16)
        loaded, did, turned, stored = (sem("t_" + n) for n in ("loaded", "did", "turned", "stored"))
        block = ph.enter_context(nc.Block())
        MT = GD * 16 // 7

        @block.sync
        def _(sp):
            sp.dma_start(mrow[:, :].rearrange("p (h j) -> p h j", j=8),
                         table.rearrange("(h p j) a -> p h (j a)", p=P, j=8)).then_inc(loaded, 16)
            sp.wait_ge(did, 2 + 7)
            sp.dma_start(dense_mask.rearrange("(k r) p -> r k p", k=7), mask_t[0:MT, :, :]).then_inc(stored, 16)
            sp.wait_ge(stored, 16)

        @block.vector
        def _(dve):
            dve.wait_ge(loaded, 16)
            dve.tensor_copy(mrowf[:, :], mrow[:, :]).then_inc(did, 1)
            dve.wait_ge(did, 1)
            dve.tensor_scalar(mrowf[:, :], mrowf[:, :], float(ZR), None, ALU.not_equal).then_inc(did, 1)
            dve.wait_ge(did, 2)
            for k in range(7):
                dve.wait_ge(turned, k + 1)
                dve.tensor_copy(mask_t[0:MT, k, :], bank[k // 4][0:MT, k % 4, 0:P]).then_inc(did, 1)

        @block.tensor
        def _(pe):
            pe.wait_ge(did, 2)
            for k in range(7):
                pe.transpose(bank[k // 4][0:MT, k % 4, 0:P], mrowf[:, k * MT:(k + 1) * MT],
                             ident[:, :]).then_inc(turned, 1)

    def ln_sums(dve, steps, x_, st, mv, n, var_ready):
        for t in range(n):
            steps.did(dve.bn_stats(st[:, t, :], x_[:, t, :]))
        steps.sync()
        steps.did(dve.tensor_tensor(mv[:, 0, 0:n], st[:, 0:n, 1], st[:, 0:n, 4], ALU.add))
        steps.did(dve.tensor_tensor(mv[:, 1, 0:n], st[:, 0:n, 1], st[:, 0:n, 4], ALU.subtract))
        steps.did(dve.tensor_tensor(mv[:, 2, 0:n], st[:, 0:n, 2], st[:, 0:n, 5], ALU.add))
        steps.sync()
        steps.did(dve.tensor_scalar(mv[:, 0, 0:n], mv[:, 0, 0:n], -0.5, None, ALU.mult))
        steps.did(dve.tensor_tensor(mv[:, 1, 0:n], mv[:, 1, 0:n], mv[:, 1, 0:n], ALU.mult))
        steps.sync()
        dve.scalar_tensor_tensor(mv[:, 2, 0:n], mv[:, 1, 0:n], P / 4.0, mv[:, 2, 0:n], ALU.mult,
                                 ALU.add).then_inc(var_ready, 1)

    def ln_root(act, mv, n, sd_ready):
        act.activation(mv[:, 3, 0:n], mv[:, 2, 0:n], ACT.Sqrt, scale=1.0 / P, bias=eps[:, :]).then_inc(sd_ready, 1)

    def ln_apply(dve, steps, out_, x_, mv, n, normed, each=4):
        steps.did(dve.reciprocal(mv[:, 4, 0:n], mv[:, 3, 0:n]))
        steps.sync()
        for t in range(n):
            r = dve.tensor_scalar(out_[:, t, :], x_[:, t, :], mv[:, 0, t:t + 1], mv[:, 4, t:t + 1],
                                  ALU.add, ALU.mult)
            if t % each == each - 1:
                r.then_inc(normed, 1)

    LN_STEPS = 14

    def first(dense):
        G = GD if dense else GE
        tag = "fd_" if dense else "fe_"
        with stage() as ph:
            def tmp(name, shape, dt=F32):
                return ph.enter_context(nc.sbuf_tensor(tag + name, shape, dt))

            def sm(name):
                return sem(tag + name)

            xin, xn = tmp("xin", [P, 16, P]), tmp("xn", [P, 16, P])
            st = [tmp(f"st{k}", [P, 8, 6]) for k in range(2)]
            mv = [tmp(f"mv{k}", [P, 5, 8]) for k in range(2)]
            h = tmp("h", [P, U, CH])
            loaded = [sm(f"loaded{k}") for k in range(2)]
            stored_h = [sm(f"stored_h{k}") for k in range(2)]
            own, var_ready, sd_ready, normed, turned, h_ready = (
                sm(n) for n in ("own", "var", "sd", "normed", "turned", "h"))
            if dense:
                hid, z = tmp("hid", [P, U, CH]), tmp("z", [P, U, CH])
                zst = tmp("zst", [P, U, 6])
                mask = tmp("mask", [P, GRP], BF16)
                loaded_m, mm1, hid_ready, mm2, z_ready, z_stat, z_kept, mzero = (
                    sm(n) for n in ("loaded_m", "mm1", "hid", "mm2", "z", "zstat", "zkept", "mzero"))
                stored_z = [sm(f"stored_z{k}") for k in range(2)]
                rows, at_i, found = tmp("rows", [P, 16, P]), tmp("at_i", [P, 16], I32), tmp("found", [P, 8], I32)
                slot, looked, took = (sm(n) for n in ("slot", "looked", "took"))
                got, stored_x = ([sm(f"{n}{k}") for k in range(2)] for n in ("got", "stored_x"))
            block = ph.enter_context(nc.Block())

            @block.sync
            def _(sp):
                def store(g):
                    for k in range(2):
                        sp.wait_ge(h_ready, 4 * g + 2 * k + 2)
                        apart(sp, passed)
                        sp.dma_start((hd if dense else he)[:, bass.ds(g * GRP + k * HALF, HALF)],
                                     h[:, 2 * k:2 * k + 2, :].rearrange("p c n -> p (c n)")).then_inc(stored_h[k], 16)
                    for k in range(2 if dense else 0):
                        sp.wait_ge(z_ready, 4 * g + 2 * k + 2)
                        sp.dma_start(zd[:, bass.ds(g * GRP + k * HALF, HALF)],
                                     z[:, 2 * k:2 * k + 2, :].rearrange("p c n -> p (c n)")).then_inc(stored_z[k], 16)

                with sp.Fori(0, G) as g:
                    store(g)
                for k in range(2):
                    sp.wait_ge(stored_h[k], 16 * G)
                    if dense:
                        sp.wait_ge(stored_z[k], 16 * G)

            if dense:
                @block.gpsimd
                def _(pool):
                    def gather(g, k):
                        pool.wait_ge(got[k], 128 * g)
                        if k:
                            pool.wait_ge(looked, 128 * g)
                        pool.tensor_copy(at_i[:, 8 * k:8 * k + 8], (gdst_i, src_i)[k][:, bass.ds(g * 8, 8)])\
                            .then_inc(slot, 1)
                        pool.wait_ge(slot, 2 * g + k + 1)
                        pool.wait_ge(stored_x[k], 16 * g)
                        apart(pool, passed)
                        for t in range(8 * k, 8 * k + 8):
                            pool.indirect_dma_start(rows[:, t, :], None, x[:, :],
                                                    bass.IndirectOffsetOnAxis(ap=at_i[:, t:t + 1], axis=0),
                                                    bounds_check=N - 1, oob_is_err=False).then_inc(got[k], 16)

                    def store(g, k):
                        pool.wait_ge(got[k], 128 * g + 128)
                        apart(pool, passed)
                        pool.dma_start(tiles(xe, g * GRP + k * HALF, 8), rows[:, 8 * k:8 * k + 8, :])\
                            .then_inc(stored_x[k], 16)

                    def keep_found(g):
                        pool.wait_ge(looked, 128 * g + 128)
                        pool.tensor_copy(src_e[:, bass.ds(g * 8, 8)], found[:, :]).then_inc(took, 1)

                    @groups(pool, GE)
                    def _(g):
                        gather(g, 0)
                        gather(g, 1)
                        store(g, 0)
                        if not (isinstance(g, int) and g == 0):
                            keep_found(g - 1)
                        pool.wait_ge(took, g)
                        apart(pool, passed)
                        for t in range(8):
                            pool.indirect_dma_start(found[:, t:t + 1], None, table[:, :],
                                                    bass.IndirectOffsetOnAxis(ap=at_i[:, 8 + t:9 + t], axis=0),
                                                    bounds_check=N - 1, oob_is_err=False).then_inc(looked, 16)
                        store(g, 1)

                    keep_found(GE - 1)
                    for k in range(2):
                        pool.wait_ge(stored_x[k], 16 * GE)

            @block.vector
            def _(dve):
                steps = Steps(dve, own, 2 * LN_STEPS)

                def normalise(g):
                    steps.at(g)
                    for k in range(2):
                        dve.wait_ge(loaded[k], 16 * g + 16)
                        ln_sums(dve, steps, xin[:, 8 * k:8 * k + 8, :], st[k], mv[k], 8, var_ready)
                    for k in range(2):
                        dve.wait_ge(sd_ready, 2 * g + k + 1)
                        reuse(dve, turned, 4 * g + 2 * k - 2)
                        ln_apply(dve, steps, xn[:, 8 * k:8 * k + 8, :], xin[:, 8 * k:8 * k + 8, :], mv[k], 8, normed)
                    assert steps.k == steps.per

                if not dense:
                    @groups(dve, G)
                    def _(g):
                        normalise(g)
                    return
                dve.memset(mask[:, :], 0.0).then_inc(mzero, 1)
                normalise(0)

                @groups(dve, G, 1, 2)
                def _(g):
                    normalise(g)
                    z_out(dve, g - 1, mm2, stored_z, z, zst, z_ready, z_stat, z_kept, 0)

                z_out(dve, G - 1, mm2, stored_z, z, zst, z_ready, z_stat, z_kept, 0)

            @block.scalar
            def _(act):
                def load(g, tail=False):
                    for k in range(2):
                        reuse(act, normed, 4 * g + 2 * k - 2)
                        if not dense:
                            act.dma_start(xin[:, 8 * k:8 * k + 8, :],
                                          tiles(xe, g * GRP + k * HALF, 8)).then_inc(loaded[k], 16)
                        elif tail and k:
                            act.dma_start(xin[0:TAIL_P, 8:16, :].rearrange("p j f -> p (j f)"),
                                         x_tail(x)).then_inc(loaded[k], 16)
                        else:
                            act.dma_start(xin[:, 8 * k:8 * k + 8, :].rearrange("p j f -> p (j f)"),
                                         x_half(x, 2 * g + k)).then_inc(loaded[k], 16)
                    if not dense:
                        return
                    act.wait_ge(mm1, 4 * g)
                    act.dma_start(mask[0:1, :], dense_mask[bass.ds(g * 16, 16), :]
                                 .rearrange("(a j) p -> a (j p)", a=1)).then_inc(loaded_m, 16)

                if dense:
                    act.wait_ge(mzero, 1)
                load(0)

                @groups(act, G, ended=2)
                def _(g):
                    static = isinstance(g, int)
                    for k in range(2):
                        act.wait_ge(var_ready, 2 * g + k + 1)
                        ln_root(act, mv[k], 8, sd_ready)
                    if not dense and not (static and g == G - 1):
                        load(g + 1)
                    for c in range(U):
                        act.wait_ge(turned, 4 * g + c + 1)
                        act.wait_ge(stored_h[c // 2], 16 * g)
                        if dense:
                            reuse(act, mm1, 4 * g + c - 3)
                        act.activation(h[:, c, :], bank[0][:, c, :], ACT.Relu).then_inc(h_ready, 1)
                    if dense:
                        if not (static and g == G - 1):
                            load(g + 1, tail=static and g == G - 2)
                        hidden(act, g, 0, mm1, mm2, hid, hid_ready)

            @block.tensor
            def _(pe):
                @groups(pe, G)
                def _(g):
                    for c in range(U):
                        pe.wait_ge(normed, 4 * g + c + 1)
                        reuse(pe, h_ready, 4 * g + c - 3)
                        for j in range(4):
                            t = pe.transpose(bank[0][:, c, j * P:(j + 1) * P], xn[:, 4 * c + j, :], ident[:, :])
                        t.then_inc(turned, 1)
                    if dense:
                        products(pe, g, 0, h, h_ready, z_ready, mask, loaded_m, (0, 1, 2, 3), hid, hid_ready, mm1, mm2)

    def products(pe, g, l, h, h_ready, z_free, mask, loaded_m, masked, hid, hid_ready, mm1, mm2):
        for c in range(U):
            pe.wait_ge(h_ready, 4 * g + c + 1)
            reuse(pe, z_free, 4 * g + c - 3)
            m = pe.matmul(bank[1][:, c, :], w1[:, l, :], h[:, c, :], start=True, stop=c not in masked)
            if c in masked:
                if c == masked[0]:
                    pe.wait_ge(loaded_m, 16 * g + 16)
                m = pe.matmul(bank[1][:, c, :], big0[:, :], mask[:, c * CH:(c + 1) * CH], start=False, stop=True)
            m.then_inc(mm1, 1)
        for c in range(U):
            pe.wait_ge(hid_ready, 4 * g + c + 1)
            pe.matmul(bank[1][:, c, :], w2[:, l, :], hid[:, c, :], start=True, stop=True).then_inc(mm2, 1)

    def hidden(act, g, l, mm1, mm2, hid, hid_ready):
        for c in range(U):
            act.wait_ge(mm1, 4 * g + c + 1)
            reuse(act, mm2, 4 * g + c - 3)
            act.activation(hid[:, c, :], bank[1][:, c, :], ACT.Relu, bias=b1[:, l:l + 1]).then_inc(hid_ready, 1)

    def z_out(dve, g, mm2, stored_z, z, zst, z_ready, z_stat, z_kept, edge):
        with_stats = 2 if edge else U
        for c in range(U):
            dve.wait_ge(mm2, 4 * g + c + 1)
            dve.wait_ge(stored_z[c // 2], 16 * g)
            if c < with_stats:
                if c == 0:
                    dve.wait_ge(z_kept, g)
                dve.bn_stats(zst[:, c, :], bank[1][:, c, :]).then_inc(z_stat, 1)
            dve.tensor_copy(z[:, c, :], bank[1][:, c, :]).then_inc(z_ready, 1)
        dve.wait_ge(z_stat, with_stats * (g + 1))
        to = (stat_all[:, bass.ds(GD * U + g * 2, 2), :] if edge else stat_all[:, bass.ds(g * U, U), :])
        dve.tensor_scalar(to, zst[:, 0:with_stats, :], 1.0, None, ALU.mult).then_inc(z_kept, 1)

    def gather_sums(pool, g, of, sums, at_i, slot, got, turned, per):
        for k in range(2):
            pool.wait_ge(got[k], 64 * g)
            pool.tensor_copy(at_i[:, 4 * k:4 * k + 4], src_e[:, bass.ds(g * 8 + 4 * k, 4)]).then_inc(slot, 1)
            pool.wait_ge(slot, 2 * g + k + 1)
            reuse(pool, turned, per * g + k - 1)
            apart(pool, passed)
            for t in range(4 * k, 4 * k + 4):
                pool.indirect_dma_start(sums[:, t, :], None, of[:, :],
                                        bass.IndirectOffsetOnAxis(ap=at_i[:, t:t + 1], axis=0),
                                        bounds_check=ZR, oob_is_err=False).then_inc(got[k], 16)

    def layer(l, dense):
        G = GD if dense else GE
        tag = f"l{l}{'d' if dense else 'e'}_"
        bn = l > 0
        zt, ht = (zd, hd) if dense else (ze, he)
        with stage() as ph:
            def tmp(name, shape, dt=F32):
                return ph.enter_context(nc.sbuf_tensor(tag + name, shape, dt))

            def sm(name):
                return sem(tag + name)

            hin = tmp("hin", [P, U, CH])
            hid, z, zst = tmp("hid", [P, U, CH]), tmp("z", [P, U, CH]), tmp("zst", [P, U, 6])
            mask = tmp("mask", [P, GRP], BF16)
            loaded_h = [sm(f"loaded_h{k}") for k in range(2)]
            stored_z = [sm(f"stored_z{k}") for k in range(2)]
            loaded_m, mm1, hid_ready, mm2, z_ready, z_stat, z_kept, mzero, x_ready = (
                sm(n) for n in ("loaded_m", "mm1", "hid", "mm2", "z", "zstat", "zkept", "mzero", "x"))
            if bn:
                zin, unit, hout = tmp("zin", [P, U, CH]), tmp("unit", [P, U, CH]), tmp("hout", [P, U, CH])
                loaded_z = [sm(f"loaded_z{k}") for k in range(2)]
                stored_h = [sm(f"stored_h{k}") for k in range(2)]
                unit_ready, h_ready = sm("unit"), sm("h")
            if not dense:
                sums, summed = tmp("sums", [P, 16, P]), tmp("summed", [P, U, CH])
                at_i = tmp("at_i", [P, 8], I32)
                slot, turned = sm("slot"), sm("turned")
                got = [sm(f"got{k}") for k in range(3)]
            else:
                summed, turned = (hout, None) if bn else (None, None)
            lookup = dense and l == 1
            if lookup:
                at_i, found = tmp("at_i", [P, 8], I32), tmp("found", [P, 8], I32)
                slot, looked, took = (sm(n) for n in ("slot", "looked", "took"))
            block = ph.enter_context(nc.Block())
            h_used = h_ready if bn else x_ready

            @block.sync
            def _(sp):
                def store(g):
                    for k in range(2 if bn else 0):
                        sp.wait_ge(h_ready, 4 * g + 2 * k + 2)
                        sp.dma_start(ht[:, bass.ds(g * GRP + k * HALF, HALF)],
                                     hout[:, 2 * k:2 * k + 2, :].rearrange("p c n -> p (c n)")).then_inc(stored_h[k], 16)
                    for k in range(2):
                        sp.wait_ge(z_ready, 4 * g + 2 * k + 2)
                        sp.dma_start(zt[:, bass.ds(g * GRP + k * HALF, HALF)],
                                     z[:, 2 * k:2 * k + 2, :].rearrange("p c n -> p (c n)")).then_inc(stored_z[k], 16)

                with sp.Fori(0, G) as g:
                    store(g)
                for k in range(2):
                    if bn:
                        sp.wait_ge(stored_h[k], 16 * G)
                    sp.wait_ge(stored_z[k], 16 * G)

            if not dense:
                @block.gpsimd
                def _(pool):
                    @groups(pool, G)
                    def _(g):
                        gather_sums(pool, g, agg[0], sums[:, 8:16, :], at_i, slot, got[1:], turned, U)

            if lookup:
                @block.gpsimd
                def _(pool):
                    def keep_found(g):
                        pool.wait_ge(looked, 128 * g + 128)
                        pool.tensor_copy(dst_e[:, bass.ds(g * 8, 8)], found[:, :]).then_inc(took, 1)

                    @groups(pool, GE)
                    def _(g):
                        if not (isinstance(g, int) and g == 0):
                            keep_found(g - 1)
                        pool.tensor_copy(at_i[:, :], gdst_i[:, bass.ds(g * 8, 8)]).then_inc(slot, 1)
                        pool.wait_ge(slot, g + 1)
                        pool.wait_ge(took, g)
                        apart(pool, passed)
                        for t in range(8):
                            pool.indirect_dma_start(found[:, t:t + 1], None, table[:, :],
                                                    bass.IndirectOffsetOnAxis(ap=at_i[:, t:t + 1], axis=0),
                                                    bounds_check=N - 1, oob_is_err=False).then_inc(looked, 16)

                    keep_found(GE - 1)

            @block.scalar
            def _(act):
                def load(g):
                    for k in range(2):
                        cols_ = bass.ds(g * GRP + k * HALF, HALF)
                        if bn:
                            reuse(act, unit_ready, 4 * g + 2 * k - 2)
                            act.dma_start(zin[:, 2 * k:2 * k + 2, :].rearrange("p c n -> p (c n)"),
                                         zt[:, cols_]).then_inc(loaded_z[k], 16)
                        reuse(act, h_used, 4 * g + 2 * k - 2)
                        act.dma_start(hin[:, 2 * k:2 * k + 2, :].rearrange("p c n -> p (c n)"),
                                     ht[:, cols_]).then_inc(loaded_h[k], 16)
                    if dense:
                        act.wait_ge(mm1, 4 * g)
                        act.dma_start(mask[0:1, :], dense_mask[bass.ds(g * 16, 16), :]
                                     .rearrange("(a j) p -> a (j p)", a=1)).then_inc(loaded_m, 16)
                    else:
                        act.wait_ge(turned, 4 * g)
                        act.dma_start(sums[:, 0:8, :], tiles(agg[0], g * HALF, 8)).then_inc(got[0], 16)
                        act.wait_ge(mm1, 4 * g)
                        act.dma_start(mask[0:1, 0:HALF], edge_mask[bass.ds(g * 8, 8), :]
                                     .rearrange("(a j) p -> a (j p)", a=1)).then_inc(loaded_m, 16)

                act.wait_ge(mzero, 1)
                load(0)

                @groups(act, G, ended=1)
                def _(g):
                    for c in range(U if bn else 0):
                        act.wait_ge(loaded_z[c // 2], 16 * g + 16)
                        reuse(act, h_ready, 4 * g + c - 3)
                        act.activation(unit[:, c, :], zin[:, c, :], ACT.Relu, bias=norm_c[:, l - 1:l],
                                       scale=norm_a[:, l - 1:l]).then_inc(unit_ready, 1)
                    if not (isinstance(g, int) and g == G - 1):
                        load(g + 1)
                    hidden(act, g, l, mm1, mm2, hid, hid_ready)

            @block.vector
            def _(dve):
                def combine(g):
                    for c in range(U if bn else 0):
                        dve.wait_ge(loaded_h[c // 2], 16 * g + 16)
                        dve.wait_ge(unit_ready, 4 * g + c + 1)
                        dve.wait_ge(stored_h[c // 2], 16 * g)
                        reuse(dve, mm1 if dense else x_ready, 4 * g + c - 3)
                        dve.scalar_tensor_tensor(hout[:, c, :], hin[:, c, :], RES, unit[:, c, :], ALU.mult,
                                                 ALU.add).then_inc(h_ready, 1)
                    for c in range(0 if dense else U):
                        if bn:
                            dve.wait_ge(h_ready, 4 * g + c + 1)
                        else:
                            dve.wait_ge(loaded_h[c // 2], 16 * g + 16)
                        dve.wait_ge(turned, 4 * g + c + 1)
                        reuse(dve, mm1, 4 * g + c - 3)
                        dve.tensor_tensor(summed[:, c, :], (hout if bn else hin)[:, c, :], bank[0][:, c, :],
                                          ALU.add).then_inc(x_ready, 1)

                dve.memset(mask[:, :], 0.0).then_inc(mzero, 1)
                combine(0)

                @groups(dve, G, 1, 2)
                def _(g):
                    combine(g)
                    z_out(dve, g - 1, mm2, stored_z, z, zst, z_ready, z_stat, z_kept, not dense)

                z_out(dve, G - 1, mm2, stored_z, z, zst, z_ready, z_stat, z_kept, not dense)

            @block.tensor
            def _(pe):
                @groups(pe, G)
                def _(g):
                    for c in range(0 if dense else U):
                        pe.wait_ge(got[0 if c < 2 else c - 1], (16 if c < 2 else 64) * (g + 1))
                        reuse(pe, x_ready, 4 * g + c - 3)
                        for j in range(4):
                            t = pe.transpose(bank[0][:, c, j * P:(j + 1) * P], sums[:, 4 * c + j, :], ident[:, :])
                        t.then_inc(turned, 1)
                    products(pe, g, l, summed, h_ready if dense else x_ready, z_ready, mask, loaded_m,
                             (0, 1, 2, 3) if dense else (0, 1), hid, hid_ready, mm1, mm2)

    def messages(l):
        bn = l > 0
        tag = f"m{l}_"
        with stage() as ph:
            def tmp(name, shape, dt=F32):
                return ph.enter_context(nc.sbuf_tensor(tag + name, shape, dt))

            hin, attr = tmp("hin", [P, 2, CH]), tmp("attr", [P, 2, CH])
            kept = tmp("kept", [P, 2, CH], BF16)
            pre, msg, run, rows = (tmp(n, [P, 2, CH]) for n in ("pre", "msg", "run", "rows"))
            carry = tmp("carry", [P, 1])
            loaded_h, loaded_a, loaded_k, unit_ready, h_ready, mm, pre_ready, msg_ready, scanned, carried, turned, \
                row_ready, stored, zeroed = (sem(tag + n) for n in (
                    "loaded_h", "loaded_a", "loaded_k", "unit", "h", "mm", "pre", "msg", "scanned", "carried",
                    "turned", "row", "stored", "zeroed"))
            if bn:
                zin, unit, hout = tmp("zin", [P, 2, CH]), tmp("unit", [P, 2, CH]), tmp("hout", [P, 2, CH])
                loaded_z = sem(tag + "loaded_z")
            block = ph.enter_context(nc.Block())

            @block.sync
            def _(sp):
                def load(g):
                    s_cols = bass.ds(g * GRP + HALF, HALF)
                    if bn:
                        sp.wait_ge(unit_ready, 2 * g)
                        sp.dma_start(zin[:, :, :].rearrange("p c n -> p (c n)"), ze[:, s_cols]).then_inc(loaded_z, 16)
                    sp.wait_ge(h_ready if bn else pre_ready, 2 * g)
                    sp.dma_start(hin[:, :, :].rearrange("p c n -> p (c n)"), he[:, s_cols]).then_inc(loaded_h, 16)
                    sp.wait_ge(mm, 2 * g)
                    sp.dma_start(attr[0:EA, :, :].rearrange("p c n -> p (c n)"),
                                 attr_t[0:EA, bass.ds(g * HALF, HALF)]).then_inc(loaded_a, 16)
                    sp.wait_ge(scanned, 2 * g)
                    sp.dma_start(kept[:, :, :].rearrange("p c n -> p (c n)"), keep_line[bass.ds(g * 8, 8), :]
                                 .rearrange("(a t) p -> a (t p)", a=1).to_broadcast([P, HALF])).then_inc(loaded_k, 16)

                def store(g):
                    sp.wait_ge(row_ready, 2 * g + 2)
                    sp.dma_start(tiles(agg[0], g * HALF, 8),
                                 rows[:, :, :].rearrange("p c (t f) -> p (c t) f", f=P)).then_inc(stored, 16)

                sp.wait_ge(zeroed, 1)
                load(0)
                with sp.Fori(0, GE - 1) as g:
                    load(g + 1)
                    store(g)
                store(GE - 1)
                sp.wait_ge(stored, 16 * GE)

            @block.scalar
            def _(act):
                @groups(act, GE)
                def _(g):
                    for c in range(2 if bn else 0):
                        act.wait_ge(loaded_z, 16 * g + 16)
                        reuse(act, h_ready, 2 * g + c - 1)
                        act.activation(unit[:, c, :], zin[:, c, :], ACT.Relu, bias=norm_c[:, l - 1:l],
                                       scale=norm_a[:, l - 1:l]).then_inc(unit_ready, 1)
                    for c in range(2):
                        act.wait_ge(pre_ready, 2 * g + c + 1)
                        reuse(act, scanned, 2 * g + c - 1)
                        act.activation(msg[:, c, :], pre[:, c, :], ACT.Relu, bias=be[:, l:l + 1]).then_inc(msg_ready, 1)
                    for c in range(2):
                        act.wait_ge(turned, 2 * g + c + 1)
                        act.wait_ge(stored, 16 * g)
                        act.activation(rows[:, c, :], bank[1][:, c, :], ACT.Copy).then_inc(row_ready, 1)

            @block.vector
            def _(dve):
                dve.memset(attr[:, :, :], 0.0).then_inc(zeroed, 1)
                dve.memset(carry[:, :], 0.0).then_inc(carried, 1)
                @groups(dve, GE)
                def _(g):
                    for c in range(2 if bn else 0):
                        dve.wait_ge(loaded_h, 16 * g + 16)
                        dve.wait_ge(unit_ready, 2 * g + c + 1)
                        reuse(dve, pre_ready, 2 * g + c - 1)
                        dve.scalar_tensor_tensor(hout[:, c, :], hin[:, c, :], RES, unit[:, c, :], ALU.mult,
                                                 ALU.add).then_inc(h_ready, 1)
                    for c in range(2):
                        if bn:
                            dve.wait_ge(h_ready, 2 * g + c + 1)
                        else:
                            dve.wait_ge(loaded_h, 16 * g + 16)
                        dve.wait_ge(mm, 2 * g + c + 1)
                        reuse(dve, msg_ready, 2 * g + c - 1)
                        dve.tensor_tensor(pre[:, c, :], (hout if bn else hin)[:, c, :], bank[0][:, c, :],
                                          ALU.add).then_inc(pre_ready, 1)
                    dve.wait_ge(loaded_k, 16 * g + 16)
                    for c in range(2):
                        dve.wait_ge(msg_ready, 2 * g + c + 1)
                        reuse(dve, turned, 2 * g + c - 1)
                        scan(dve, g, c, run, kept, msg, carry, scanned, carried)

            @block.tensor
            def _(pe):
                @groups(pe, GE)
                def _(g):
                    pe.wait_ge(loaded_a, 16 * g + 16)
                    for c in range(2):
                        reuse(pe, pre_ready, 2 * g + c - 1)
                        pe.matmul(bank[0][:, c, :], w_e[:, l, :], attr[:, c, :], start=True, stop=True).then_inc(mm, 1)
                    for c in range(2):
                        pe.wait_ge(scanned, 2 * g + c + 1)
                        reuse(pe, row_ready, 2 * g + c - 1)
                        for j in range(4):
                            t = pe.transpose(bank[1][:, c, j * P:(j + 1) * P], run[:, c, j * P:(j + 1) * P], ident[:, :])
                        t.then_inc(turned, 1)

    def scan(dve, g, c, run, kept, of, carry, scanned, carried):
        if c:
            dve.wait_ge(scanned, 2 * g + 1)
        else:
            dve.wait_ge(carried, g + 1)
        dve.tensor_tensor_scan(run[:, c, :], kept[:, c, :], of[:, c, :],
                               run[:, 0, CH - 1:CH] if c else carry[:, :], ALU.mult, ALU.add).then_inc(scanned, 1)
        if c:
            dve.wait_ge(scanned, 2 * g + 2)
            dve.tensor_copy(carry[:, :], run[:, 1, CH - 1:CH]).then_inc(carried, 1)

    def batch_norm(l):
        tag = f"b{l}_"
        with stage() as ph:
            def tmp(name, shape, dt=F32):
                return ph.enter_context(nc.sbuf_tensor(tag + name, shape, dt))

            n = (GD * U + GE * 2) * 2
            parts = stat_all[:, :, :].rearrange("p n (a b) -> p (n a) b", a=2)
            sq = tmp("sq", [P, n])
            v = tmp("v", [P, 12])
            own, root = sem(tag + "own"), sem(tag + "root")
            block = ph.enter_context(nc.Block())

            @block.scalar
            def _(act):
                act.wait_ge(own, 9)
                act.activation(v[:, 7:8], v[:, 6:7], ACT.Sqrt, bias=eps[:, :]).then_inc(root, 1)

            @block.vector
            def _(dve):
                k = [0]

                def link(ins):
                    k[0] += 1
                    ins.then_inc(own, 1)
                    dve.wait_ge(own, k[0])

                each = float(CH // 2)
                link(dve.tensor_tensor(sq[:, :], parts[:, :, 1], parts[:, :, 1], ALU.mult))
                link(dve.tensor_reduce(v[:, 0:1], parts[:, :, 1], axis=AX.X, op=ALU.add))
                link(dve.tensor_reduce(v[:, 1:2], sq[:, :], axis=AX.X, op=ALU.add))
                link(dve.tensor_reduce(v[:, 2:3], parts[:, :, 2], axis=AX.X, op=ALU.add))
                link(dve.tensor_scalar(v[:, 3:4], v[:, 0:1], each / N, None, ALU.mult))
                link(dve.scalar_tensor_tensor(v[:, 4:5], v[:, 1:2], each, v[:, 2:3], ALU.mult, ALU.add))
                link(dve.tensor_tensor(v[:, 5:6], v[:, 3:4], v[:, 3:4], ALU.mult))
                link(dve.tensor_scalar(v[:, 4:5], v[:, 4:5], 1.0 / N, None, ALU.mult))
                link(dve.tensor_tensor(v[:, 6:7], v[:, 4:5], v[:, 5:6], ALU.subtract))
                dve.wait_ge(root, 1)
                link(dve.reciprocal(v[:, 8:9], v[:, 7:8]))
                link(dve.tensor_tensor(norm_a[:, l:l + 1], v[:, 8:9], gamma[:, l:l + 1], ALU.mult))
                link(dve.tensor_tensor(v[:, 9:10], v[:, 3:4], b2[:, l:l + 1], ALU.add))
                link(dve.tensor_tensor(v[:, 9:10], b2[:, l:l + 1], v[:, 9:10], ALU.subtract))
                link(dve.tensor_tensor(v[:, 10:11], v[:, 9:10], norm_a[:, l:l + 1], ALU.mult))
                link(dve.tensor_tensor(norm_c[:, l:l + 1], v[:, 10:11], beta[:, l:l + 1], ALU.add))

    def leave():
        tag = "v_"
        with stage() as ph:
            def tmp(name, shape, dt=F32):
                return ph.enter_context(nc.sbuf_tensor(tag + name, shape, dt))

            zin, hin, unit, h3 = (tmp(n, [P, U, CH]) for n in ("zin", "hin", "unit", "h3"))
            xin, x1, xn = tmp("xin", [P, 16, P]), tmp("x1", [P, 16, P]), tmp("xn", [P, 8, P])
            st, mv, h = tmp("st", [P, 8, 6]), tmp("mv", [P, 5, 8]), tmp("h", [P, 2, CH])
            own, var_ready, sd_ready, normed, unit_ready, h3_ready, turned, x1_ready, turned_h, h_ready, stored_h = (
                sem(tag + n) for n in ("own", "var", "sd", "normed", "unit", "h3", "turned", "x1", "turned_h",
                                       "h", "stored_h"))
            loaded_z, loaded_h, loaded_x, stored_x = (
                [sem(f"{tag}{n}{k}") for k in range(2)] for n in ("loaded_z", "loaded_h", "loaded_x", "stored_x"))
            block = ph.enter_context(nc.Block())

            @block.sync
            def _(sp):
                def load(g):
                    for k in range(2):
                        cols_ = bass.ds(g * GRP + k * HALF, HALF)
                        reuse(sp, unit_ready, 4 * g + 2 * k - 2)
                        sp.dma_start(zin[:, 2 * k:2 * k + 2, :].rearrange("p c n -> p (c n)"),
                                     ze[:, cols_]).then_inc(loaded_z[k], 16)
                        reuse(sp, h3_ready, 4 * g + 2 * k - 2)
                        sp.dma_start(hin[:, 2 * k:2 * k + 2, :].rearrange("p c n -> p (c n)"),
                                     he[:, cols_]).then_inc(loaded_h[k], 16)
                        reuse(sp, x1_ready, 4 * g + 2 * k - 2)
                        sp.dma_start(xin[:, 8 * k:8 * k + 8, :],
                                     tiles(xe, g * GRP + k * HALF, 8)).then_inc(loaded_x[k], 16)

                def store(g):
                    for k in range(2):
                        sp.wait_ge(x1_ready, 4 * g + 2 * k + 2)
                        sp.dma_start(tiles(xe, g * GRP + k * HALF, 8), x1[:, 8 * k:8 * k + 8, :])\
                          .then_inc(stored_x[k], 16)
                    sp.wait_ge(h_ready, 2 * g + 2)
                    apart(sp, passed)
                    sp.dma_start(he[:, bass.ds(g * GRP + HALF, HALF)],
                                 h[:, :, :].rearrange("p c n -> p (c n)")).then_inc(stored_h, 16)

                load(0)
                with sp.Fori(0, GE - 1) as g:
                    load(g + 1)
                    store(g)
                store(GE - 1)
                sp.wait_ge(stored_h, 16 * GE)
                for k in range(2):
                    sp.wait_ge(stored_x[k], 16 * GE)

            @block.scalar
            def _(act):
                @groups(act, GE)
                def _(g):
                    for c in range(U):
                        act.wait_ge(loaded_z[c // 2], 16 * g + 16)
                        reuse(act, h3_ready, 4 * g + c - 3)
                        act.activation(unit[:, c, :], zin[:, c, :], ACT.Relu, bias=norm_c[:, LAYERS - 1:],
                                       scale=norm_a[:, LAYERS - 1:]).then_inc(unit_ready, 1)
                    act.wait_ge(var_ready, g + 1)
                    ln_root(act, mv, 8, sd_ready)
                    for c in range(2):
                        act.wait_ge(turned_h, 2 * g + c + 1)
                        act.wait_ge(stored_h, 16 * g)
                        act.activation(h[:, c, :], bank[1][:, c, :], ACT.Relu).then_inc(h_ready, 1)

            @block.vector
            def _(dve):
                steps = Steps(dve, own, LN_STEPS)
                @groups(dve, GE)
                def _(g):
                    steps.at(g)
                    for c in range(U):
                        dve.wait_ge(loaded_h[c // 2], 16 * g + 16)
                        dve.wait_ge(unit_ready, 4 * g + c + 1)
                        reuse(dve, turned, 4 * g + c - 3)
                        dve.scalar_tensor_tensor(h3[:, c, :], hin[:, c, :], RES, unit[:, c, :], ALU.mult,
                                                 ALU.add).then_inc(h3_ready, 1)
                    for c in range(U):
                        dve.wait_ge(turned, 4 * g + c + 1)
                        dve.wait_ge(loaded_x[c // 2], 16 * g + 16)
                        dve.wait_ge(stored_x[c // 2], 16 * g)
                        dve.tensor_tensor(x1[:, 4 * c:4 * c + 4, :].rearrange("p t f -> p (t f)"),
                                          xin[:, 4 * c:4 * c + 4, :].rearrange("p t f -> p (t f)"),
                                          bank[0][:, c, :], ALU.add).then_inc(x1_ready, 1)
                    dve.wait_ge(x1_ready, 4 * g + 4)
                    ln_sums(dve, steps, x1[:, 8:16, :], st, mv, 8, var_ready)
                    dve.wait_ge(sd_ready, g + 1)
                    dve.wait_ge(turned_h, 2 * g)
                    ln_apply(dve, steps, xn, x1[:, 8:16, :], mv, 8, normed)

            @block.tensor
            def _(pe):
                @groups(pe, GE)
                def _(g):
                    for c in range(U):
                        pe.wait_ge(h3_ready, 4 * g + c + 1)
                        reuse(pe, x1_ready, 4 * g + c - 3)
                        for j in range(4):
                            t = pe.transpose(bank[0][:, c, j * P:(j + 1) * P], h3[:, c, j * P:(j + 1) * P], ident[:, :])
                        t.then_inc(turned, 1)
                    for c in range(2):
                        pe.wait_ge(normed, 2 * g + c + 1)
                        reuse(pe, h_ready, 2 * g + c - 1)
                        for j in range(4):
                            t = pe.transpose(bank[1][:, c, j * P:(j + 1) * P], xn[:, 4 * c + j, :], ident[:, :])
                        t.then_inc(turned_h, 1)

    def mean(r):
        tag = f"a{r}_"
        of, to = agg[(r + 1) % 2], agg[r % 2]
        last_one = r == 2
        with stage() as ph:
            def tmp(name, shape, dt=F32):
                return ph.enter_context(nc.sbuf_tensor(tag + name, shape, dt))

            h = tmp("h", [P, 2, CH])
            kept = tmp("kept", [P, 2, CH], BF16)
            run, rows = tmp("run", [P, 2, CH]), tmp("rows", [P, 8, P])
            carry = tmp("carry", [P, 1])
            h_ready, loaded_k, scanned, carried, turned, row_ready, stored = (
                sem(tag + n) for n in ("h", "loaded_k", "scanned", "carried", "turned", "row", "stored"))
            if r:
                sums, at_i = tmp("sums", [P, 8, P]), tmp("at_i", [P, 8], I32)
                slot, turned_s, got = sem(tag + "slot"), sem(tag + "turned_s"), [sem(f"{tag}got{k}") for k in range(2)]
            if last_one:
                x1, x2 = tmp("x1", [P, 8, P]), tmp("x2", [P, 8, P])
                loaded_x, x_ready, stored_x = (sem(tag + n) for n in ("loaded_x", "x", "stored_x"))
            block = ph.enter_context(nc.Block())

            @block.sync
            def _(sp):
                def load(g):
                    if not r:
                        sp.wait_ge(scanned, 2 * g)
                        sp.dma_start(h[:, :, :].rearrange("p c n -> p (c n)"),
                                     he[:, bass.ds(g * GRP + HALF, HALF)]).then_inc(h_ready, 16)
                    sp.wait_ge(scanned, 2 * g)
                    sp.dma_start(kept[:, :, :].rearrange("p c n -> p (c n)"), keep_line[bass.ds(g * 8, 8), :]
                                 .rearrange("(a t) p -> a (t p)", a=1).to_broadcast([P, HALF])).then_inc(loaded_k, 16)
                    if last_one:
                        sp.wait_ge(x_ready, 2 * g)
                        sp.dma_start(x1[:, :, :], tiles(xe, g * GRP, 8)).then_inc(loaded_x, 16)

                def store(g):
                    sp.wait_ge(row_ready, 2 * g + 2)
                    sp.dma_start(tiles(to, g * HALF, 8), rows[:, :, :]).then_inc(stored, 16)
                    if last_one:
                        sp.wait_ge(x_ready, 2 * g + 2)
                        sp.dma_start(tiles(x2d, g * HALF, 8), x2[:, :, :]).then_inc(stored_x, 16)

                load(0)
                with sp.Fori(0, GE - 1) as g:
                    load(g + 1)
                    store(g)
                store(GE - 1)
                sp.wait_ge(stored, 16 * GE)
                if last_one:
                    sp.wait_ge(stored_x, 16 * GE)

            if r:
                @block.gpsimd
                def _(pool):
                    @groups(pool, GE)
                    def _(g):
                        gather_sums(pool, g, of, sums, at_i, slot, got, turned_s, 2)

                @block.scalar
                def _(act):
                    @groups(act, GE)
                    def _(g):
                        for c in range(2):
                            act.wait_ge(turned_s, 2 * g + c + 1)
                            reuse(act, scanned, 2 * g + c - 1)
                            act.activation(h[:, c, :], bank[0][:, c, :], ACT.Copy).then_inc(h_ready, 1)

            @block.vector
            def _(dve):
                dve.memset(carry[:, :], 0.0).then_inc(carried, 1)
                @groups(dve, GE)
                def _(g):
                    dve.wait_ge(loaded_k, 16 * g + 16)
                    for c in range(2):
                        dve.wait_ge(h_ready, 2 * g + c + 1 if r else 16 * g + 16)
                        reuse(dve, turned, 2 * g + c - 1)
                        scan(dve, g, c, run, kept, h, carry, scanned, carried)
                    for c in range(2):
                        t4 = slice(4 * c, 4 * c + 4)
                        dve.wait_ge(turned, 2 * g + c + 1)
                        dve.wait_ge(stored, 16 * g)
                        dve.tensor_tensor(rows[:, t4, :], bank[1][:, c, :].rearrange("p (t f) -> p t f", f=P),
                                          rcount[:, bass.ds(g * 8 + 4 * c, 4)].unsqueeze(2).to_broadcast([P, 4, P]),
                                          ALU.mult).then_inc(row_ready, 1)
                    for c in range(2 if last_one else 0):
                        t4 = slice(4 * c, 4 * c + 4)
                        dve.wait_ge(row_ready, 2 * g + c + 1)
                        dve.wait_ge(loaded_x, 16 * g + 16)
                        dve.wait_ge(stored_x, 16 * g)
                        dve.tensor_tensor(x2[:, t4, :], x1[:, t4, :], rows[:, t4, :], ALU.add).then_inc(x_ready, 1)

            @block.tensor
            def _(pe):
                @groups(pe, GE)
                def _(g):
                    for c in range(2 if r else 0):
                        pe.wait_ge(got[c], 64 * g + 64)
                        reuse(pe, h_ready, 2 * g + c - 1)
                        for j in range(4):
                            t = pe.transpose(bank[0][:, c, j * P:(j + 1) * P], sums[:, 4 * c + j, :], ident[:, :])
                        t.then_inc(turned_s, 1)
                    for c in range(2):
                        pe.wait_ge(scanned, 2 * g + c + 1)
                        reuse(pe, row_ready, 2 * g + c - 1)
                        for j in range(4):
                            t = pe.transpose(bank[1][:, c, j * P:(j + 1) * P], run[:, c, j * P:(j + 1) * P], ident[:, :])
                        t.then_inc(turned, 1)

    def logits():
        tag = "q_"
        with stage() as ph:
            def tmp(name, shape, dt=F32):
                return ph.enter_context(nc.sbuf_tensor(tag + name, shape, dt))

            got_rows = tmp("got_rows", [P, 16, P])
            x1, x2, xn = tmp("x1", [P, 8, P]), tmp("x2", [P, 8, P]), tmp("xn", [P, 16, P])
            st = [tmp(f"st{k}", [P, 8, 6]) for k in range(2)]
            mv = [tmp(f"mv{k}", [P, 5, 8]) for k in range(2)]
            at_i = tmp("at_i", [P, 16], I32)
            h, q, v = tmp("h", [P, U, CH]), tmp("q", [P, 2, CH]), tmp("v", [P, 2, CH])
            qk, raw, lr = (tmp(n, [P, 2, CH]) for n in ("qk", "raw", "lr"))
            attr = tmp("attr", [P, 2, CH])
            peak = tmp("peak", [P, 2])
            (own, var_ready, sd_ready, normed, slot, x2_ready, turned, h_ready, loaded_x, loaded_a, stored_v, stored_l,
             mm_q, q_ready, mm_k, mm_v, v_ready, qk_ready, mm_l, raw_ready, lr_ready, peaked, zeroed,
             topped) = (
                sem(tag + n) for n in ("own", "var", "sd", "normed", "slot", "x2", "turned", "h", "loaded_x", "loaded_a",
                                       "stored_v", "stored_l", "mm_q", "q", "mm_k", "mm_v", "v", "qk", "mm_l", "raw",
                                       "lr", "peaked", "zeroed", "topped"))
            got, stored_x, stored_h = ([sem(f"{tag}{n}{k}") for k in range(2)] for n in ("got", "stored_x", "stored_h"))
            block = ph.enter_context(nc.Block())

            @block.gpsimd
            def _(pool):
                @groups(pool, GE)
                def _(g):
                    for k, (ids, of) in enumerate(((dst_e, x2d), (src_e, agg[0]))):
                        pool.wait_ge(got[k], 128 * g)
                        pool.tensor_copy(at_i[:, 8 * k:8 * k + 8], ids[:, bass.ds(g * 8, 8)]).then_inc(slot, 1)
                        pool.wait_ge(slot, 2 * g + k + 1)
                        if k:
                            pool.wait_ge(x2_ready, 2 * g)
                        else:
                            reuse(pool, normed, 4 * g - 2)
                            pool.wait_ge(stored_x[0], 16 * g)
                        apart(pool, passed)
                        for t in range(8):
                            pool.indirect_dma_start(got_rows[:, 8 * k + t, :], None, of[:, :],
                                                    bass.IndirectOffsetOnAxis(ap=at_i[:, 8 * k + t:8 * k + t + 1],
                                                                              axis=0),
                                                    bounds_check=ZR, oob_is_err=False).then_inc(got[k], 16)
                pool.wait_ge(peaked, 2 * GE + 1)
                pool.partition_all_reduce(top[:, 0:1], peak[:, 0:1], P, REDUCE_MAX).then_inc(topped, 1)

            def start(g):
                return isinstance(g, int) and g == 0

            @block.sync
            def _(sp):
                def load_x(g):
                    sp.wait_ge(x2_ready, 2 * g)
                    sp.dma_start(x1[:, :, :], tiles(xe, g * GRP + HALF, 8)).then_inc(loaded_x, 16)

                def load_attr(g):
                    sp.wait_ge(mm_l, 2 * g)
                    sp.dma_start(attr[0:EB, :, :].rearrange("p c n -> p (c n)"),
                                 attr_t[EA:EA + EB, bass.ds(g * HALF, HALF)]).then_inc(loaded_a, 16)
                    sp.dma_start(attr[HD:HD + 1, :, :].rearrange("p c n -> p (c n)"),
                                 pad_line[:, bass.ds(g * HALF, HALF)]).then_inc(loaded_a, 16)

                def store_h(g, k):
                    sp.wait_ge(h_ready, 4 * g + 2 * k + 2)
                    apart(sp, passed)
                    sp.dma_start(he[:, bass.ds(g * GRP + k * HALF, HALF)],
                                 h[:, 2 * k:2 * k + 2, :].rearrange("p c n -> p (c n)")).then_inc(stored_h[k], 16)

                def store_v(g):
                    sp.wait_ge(v_ready, 2 * g + 2)
                    sp.dma_start(v_t[:, bass.ds(g * HALF, HALF)],
                                 v[:, :, :].rearrange("p c n -> p (c n)")).then_inc(stored_v, 16)

                def store_logits(g):
                    sp.wait_ge(lr_ready, 2 * g + 2)
                    sp.dma_start(attn_t[:, bass.ds(g * HALF, HALF)],
                                 lr[:, :, :].rearrange("p c n -> p (c n)")).then_inc(stored_l, 16)

                sp.wait_ge(zeroed, 1)
                load_x(0)

                @groups(sp, GE, ended=1)
                def _(g):
                    sp.wait_ge(got[0], 128 * g + 128)
                    sp.dma_start(tiles(xe, g * GRP, 8), got_rows[:, 0:8, :]).then_inc(stored_x[0], 16)
                    if not start(g):
                        store_v(g - 1)
                    load_attr(g)
                    store_h(g, 0)
                    if not (isinstance(g, int) and g == GE - 1):
                        load_x(g + 1)
                    sp.wait_ge(x2_ready, 2 * g + 2)
                    sp.dma_start(tiles(xe, g * GRP + HALF, 8), x2[:, :, :]).then_inc(stored_x[1], 16)
                    if not start(g):
                        store_logits(g - 1)
                    store_h(g, 1)

                store_v(GE - 1)
                store_logits(GE - 1)
                for s in (*stored_x, *stored_h, stored_v, stored_l):
                    sp.wait_ge(s, 16 * GE)

            @block.scalar
            def _(act):
                def values(g):
                    for c in range(2):
                        act.wait_ge(mm_v, 2 * g + c + 1)
                        act.wait_ge(stored_v, 16 * g)
                        act.activation(v[:, c, :], bank[0][:, 2 + c, :], ACT.Copy).then_inc(v_ready, 1)

                def raws(g):
                    for c in range(2):
                        act.wait_ge(mm_l, 2 * g + c + 1)
                        reuse(act, lr_ready, 2 * g + c - 1)
                        act.activation(raw[:, c, :], bank[1][:, c, :], ACT.Copy).then_inc(raw_ready, 1)

                @groups(act, GE, written=2)
                def _(g):
                    for k in range(2):
                        act.wait_ge(var_ready, 2 * g + k + 1)
                        ln_root(act, mv[k], 8, sd_ready)
                        if k == 0 and not start(g):
                            values(g - 1)
                            raws(g - 1)
                        for c in (2 * k, 2 * k + 1):
                            act.wait_ge(turned, 4 * g + c + 1)
                            act.wait_ge(stored_h[k], 16 * g)
                            act.wait_ge(mm_v if k else mm_q, 2 * g)
                            act.activation(h[:, c, :], bank[0][:, c, :], ACT.Relu).then_inc(h_ready, 1)
                        for c in range(0 if k else 2):
                            act.wait_ge(mm_q, 2 * g + c + 1)
                            reuse(act, qk_ready, 2 * g + c - 1)
                            act.activation(q[:, c, :], bank[1][:, c, :], ACT.Copy).then_inc(q_ready, 1)

                values(GE - 1)
                raws(GE - 1)

            @block.vector
            def _(dve):
                steps = Steps(dve, own, 2 * LN_STEPS)
                dve.memset(attr[:, :, :], 0.0).then_inc(zeroed, 1)
                dve.memset(peak[:, :], -3e38).then_inc(peaked, 1)

                def normalise(g, k):
                    dve.wait_ge(sd_ready, 2 * g + k + 1)
                    reuse(dve, turned, 4 * g + 2 * k - 2)
                    ln_apply(dve, steps, xn[:, 8 * k:8 * k + 8, :], got_rows[:, 0:8, :] if k == 0 else x2, mv[k],
                             8, normed)

                def pairs(g):
                    for c in range(2):
                        dve.wait_ge(q_ready, 2 * g + c + 1)
                        dve.wait_ge(mm_k, 2 * g + c + 1)
                        reuse(dve, mm_l, 2 * g + c - 1)
                        dve.tensor_tensor(qk[:, c, :], q[:, c, :], bank[1][:, 2 + c, :], ALU.mult).then_inc(qk_ready, 1)

                def leaky(g):
                    for c in range(2):
                        dve.wait_ge(raw_ready, 2 * g + c + 1)
                        dve.wait_ge(stored_l, 16 * g)
                        dve.wait_ge(peaked, 2 * g + 1)
                        dve.scalar_tensor_tensor(lr[:, c, :], raw[:, c, :], 0.2, raw[:, c, :], ALU.mult,
                                                 ALU.max).then_inc(lr_ready, 1)
                    dve.wait_ge(lr_ready, 2 * g + 2)
                    dve.tensor_reduce(peak[:, 1:2], lr[:, :, :], axis=AX.XY, op=ALU.max).then_inc(peaked, 1)
                    dve.wait_ge(peaked, 2 * g + 2)
                    dve.tensor_tensor(peak[:, 0:1], peak[:, 0:1], peak[:, 1:2], ALU.max).then_inc(peaked, 1)

                @groups(dve, GE, written=2)
                def _(g):
                    steps.at(g)
                    dve.wait_ge(got[0], 128 * g + 128)
                    ln_sums(dve, steps, got_rows[:, 0:8, :], st[0], mv[0], 8, var_ready)
                    if not start(g):
                        pairs(g - 1)
                    normalise(g, 0)
                    for c in range(2):
                        t4 = slice(4 * c, 4 * c + 4)
                        dve.wait_ge(loaded_x, 16 * g + 16)
                        dve.wait_ge(got[1], 128 * g + 128)
                        dve.wait_ge(stored_x[1], 16 * g)
                        dve.tensor_tensor(x2[:, t4, :], x1[:, t4, :], got_rows[:, 8 + 4 * c:12 + 4 * c, :],
                                          ALU.add).then_inc(x2_ready, 1)
                    dve.wait_ge(x2_ready, 2 * g + 2)
                    ln_sums(dve, steps, x2, st[1], mv[1], 8, var_ready)
                    if not start(g):
                        leaky(g - 1)
                    normalise(g, 1)

                pairs(GE - 1)
                leaky(GE - 1)

            @block.tensor
            def _(pe):
                def sums_of_heads(g):
                    for c in range(2):
                        pe.wait_ge(qk_ready, 2 * g + c + 1)
                        pe.matmul(bank[1][:, c, :], heads[:, :], qk[:, c, :], start=True, stop=False)
                        pe.wait_ge(loaded_a, 32 * g + 32)
                        pe.matmul(bank[1][:, c, :], w_bias[:, :], attr[:, c, :], start=False, stop=True).then_inc(mm_l, 1)

                def turn(g, k):
                    for c in (2 * k, 2 * k + 1):
                        pe.wait_ge(normed, 4 * g + c + 1)
                        reuse(pe, h_ready, 4 * g + c - 3)
                        if k:
                            pe.wait_ge(v_ready, 2 * g)
                        for j in range(4):
                            t = pe.transpose(bank[0][:, c, j * P:(j + 1) * P], xn[:, 4 * c + j, :], ident[:, :])
                        t.then_inc(turned, 1)

                @groups(pe, GE, written=2)
                def _(g):
                    if not start(g):
                        sums_of_heads(g - 1)
                    turn(g, 0)
                    for c in range(2):
                        pe.wait_ge(h_ready, 4 * g + c + 1)
                        reuse(pe, raw_ready, 2 * g + c - 1)
                        pe.matmul(bank[1][:, c, :], wq[:, :], h[:, c, :], start=True, stop=True).then_inc(mm_q, 1)
                    turn(g, 1)
                    for c in range(2):
                        pe.wait_ge(h_ready, 4 * g + 2 + c + 1)
                        reuse(pe, qk_ready, 2 * g + c - 1)
                        pe.matmul(bank[1][:, 2 + c, :], wk[:, :], h[:, 2 + c, :], start=True, stop=True).then_inc(mm_k, 1)
                    for c in range(2):
                        pe.matmul(bank[0][:, 2 + c, :], wv[:, :], h[:, 2 + c, :], start=True, stop=True).then_inc(mm_v, 1)

                sums_of_heads(GE - 1)

    def softmax():
        tag = "s_"
        with stage() as ph:
            def tmp(name, shape, dt=F32):
                return ph.enter_context(nc.sbuf_tensor(tag + name, shape, dt))

            lr, v, ex, ev, run, runx = (tmp(n, [P, 2, CH]) for n in ("lr", "v", "ex", "ev", "run", "runx"))
            total, inv = tmp("total", [P, 8 * H]), tmp("inv", [P, 8 * H])
            kept, rows = tmp("kept", [P, 2, CH], BF16), tmp("rows", [P, 8, P])
            carry, carryx = tmp("carry", [P, 1]), tmp("carryx", [P, 1])
            (loaded_l, loaded_v, loaded_k, ex_ready, ev_ready, scanned, scannedx, carried, carriedx, inverted, turned,
             row_ready, stored, negated, floored) = (
                sem(tag + n) for n in ("loaded_l", "loaded_v", "loaded_k", "ex", "ev", "scanned", "scannedx", "carried",
                                       "carriedx", "inverted", "turned", "row", "stored", "negated", "floored"))
            block = ph.enter_context(nc.Block())

            @block.sync
            def _(sp):
                def load(g):
                    cols_ = bass.ds(g * HALF, HALF)
                    sp.wait_ge(ex_ready, 2 * g)
                    sp.dma_start(lr[:, :, :].rearrange("p c n -> p (c n)"), attn_t[:, cols_]).then_inc(loaded_l, 16)
                    sp.wait_ge(ev_ready, 2 * g)
                    sp.dma_start(v[:, :, :].rearrange("p c n -> p (c n)"), v_t[:, cols_]).then_inc(loaded_v, 16)
                    sp.wait_ge(scanned, 2 * g)
                    sp.wait_ge(scannedx, 2 * g)
                    sp.dma_start(kept[:, :, :].rearrange("p c n -> p (c n)"), keep_line[bass.ds(g * 8, 8), :]
                                 .rearrange("(a t) p -> a (t p)", a=1).to_broadcast([P, HALF])).then_inc(loaded_k, 16)

                def store(g):
                    sp.wait_ge(row_ready, 2 * g + 2)
                    sp.dma_start(tiles(agg[1], g * HALF, 8), rows[:, :, :]).then_inc(stored, 16)

                load(0)
                with sp.Fori(0, GE - 1) as g:
                    load(g + 1)
                    store(g)
                store(GE - 1)
                sp.wait_ge(stored, 16 * GE)

            @block.scalar
            def _(act):
                act.wait_ge(negated, 1)
                @groups(act, GE)
                def _(g):
                    for c in range(2):
                        act.wait_ge(loaded_l, 16 * g + 16)
                        reuse(act, ev_ready, 2 * g + c - 1)
                        reuse(act, scannedx, 2 * g + c - 1)
                        act.activation(ex[:, c, :], lr[:, c, :], ACT.Exp, bias=top[:, 1:2]).then_inc(ex_ready, 1)
            @block.vector
            def _(dve):
                dve.tensor_scalar(top[:, 1:2], top[:, 0:1], -1.0, None, ALU.mult).then_inc(negated, 1)
                dve.memset(carry[:, :], 0.0).then_inc(carried, 1)
                dve.memset(carryx[:, :], 0.0).then_inc(carriedx, 1)
                @groups(dve, GE)
                def _(g):
                    for c in range(2):
                        dve.wait_ge(loaded_v, 16 * g + 16)
                        dve.wait_ge(ex_ready, 2 * g + c + 1)
                        reuse(dve, scanned, 2 * g + c - 1)
                        dve.tensor_tensor(ev[:, c, :], ex[:, c, :], v[:, c, :], ALU.mult).then_inc(ev_ready, 1)
                    dve.wait_ge(loaded_k, 16 * g + 16)
                    dve.wait_ge(turned, 2 * g)
                    for c in range(2):
                        dve.wait_ge(ev_ready, 2 * g + c + 1)
                        scan(dve, g, c, run, kept, ev, carry, scanned, carried)
                        scan(dve, g, c, runx, kept, ex, carryx, scannedx, carriedx)
                    for c in range(2):
                        s4 = slice(4 * H * c, 4 * H * c + 4 * H)
                        dve.wait_ge(turned, 2 * g + c + 1)
                        dve.tensor_scalar(total[:, s4], bank[1][:, c, 0:4 * H], 1e-12, None, ALU.max).then_inc(floored, 1)
                        dve.wait_ge(floored, 2 * g + c + 1)
                        reuse(dve, row_ready, 2 * g + c - 1)
                        dve.reciprocal(inv[:, s4], total[:, s4]).then_inc(inverted, 1)
                        dve.wait_ge(inverted, 2 * g + c + 1)
                        dve.wait_ge(stored, 16 * g)
                        dve.tensor_tensor(rows[:, 4 * c:4 * c + 4, :].rearrange("p t (h d) -> p (t h) d", h=H),
                                          bank[0][:, c, :].rearrange("p (a d) -> p a d", d=HD),
                                          inv[:, s4].unsqueeze(2).to_broadcast([P, 4 * H, HD]),
                                          ALU.mult).then_inc(row_ready, 1)

            @block.tensor
            def _(pe):
                @groups(pe, GE)
                def _(g):
                    for c in range(2):
                        pe.wait_ge(scanned, 2 * g + c + 1)
                        pe.wait_ge(scannedx, 2 * g + c + 1)
                        reuse(pe, row_ready, 2 * g + c - 1)
                        for j in range(4):
                            s = slice(j * P, (j + 1) * P)
                            pe.transpose(bank[0][:, c, s], run[:, c, s], ident[:, :])
                            t = pe.matmul(bank[1][:, c, j * H:(j + 1) * H], runx[:, c, s], ident[:, 0:P:HD],
                                          start=True, stop=True)
                        t.then_inc(turned, 1)

    def finish():
        tag = "f_"
        with stage() as ph:
            def tmp(name, shape, dt=F32):
                return ph.enter_context(nc.sbuf_tensor(tag + name, shape, dt))

            zin, hin, unit, h = (tmp(n, [P, U, CH]) for n in ("zin", "hin", "unit", "h"))
            xin, x1, xn, x3, x3b, hn, res = (tmp(n, [P, 16, P]) for n in ("xin", "x1", "xn", "x3", "x3b", "hn", "res"))
            b2r = tmp("b2r", [P, 1, P])
            st = [tmp(f"st{k}", [P, 8, 6]) for k in range(4)]
            mv = [tmp(f"mv{k}", [P, 5, 8]) for k in range(4)]
            (own, own3_0, own3_1, var1, sd1, var3, sd3, normed, unit_ready, mm_x, x1_ready, turned, h_ready, mixed, x3_ready,
             x3b_ready, hn_ready, res_ready, scaled, b2_ready) = (
                sem(tag + n) for n in ("own", "own3_0", "own3_1", "var1", "sd1", "var3", "sd3", "normed", "unit", "mm_x", "x1", "turned", "h",
                                       "mixed", "x3", "x3b", "hn", "res", "scaled", "b2"))
            loaded_z, loaded_h, loaded_x, stored = (
                [sem(f"{tag}{n}{k}") for k in range(2)] for n in ("loaded_z", "loaded_h", "loaded_x", "stored"))
            block = ph.enter_context(nc.Block())

            def flat(t, c):
                return t[:, 4 * c:4 * c + 4, :].rearrange("p t f -> p (t f)")

            @block.sync
            def _(sp):
                def load_z(g, k):
                    reuse(sp, unit_ready, 4 * g + 2 * k - 2)
                    sp.dma_start(zin[:, 2 * k:2 * k + 2, :].rearrange("p c n -> p (c n)"),
                                  zd[:, bass.ds(g * GRP + k * HALF, HALF)]).then_inc(loaded_z[k], 16)

                def load_hx(g, k, tail=False):
                    reuse(sp, mm_x, 4 * g + 2 * k - 2)
                    sp.dma_start(hin[:, 2 * k:2 * k + 2, :].rearrange("p c n -> p (c n)"),
                                  hd[:, bass.ds(g * GRP + k * HALF, HALF)]).then_inc(loaded_h[k], 16)
                    if tail:
                        sp.dma_start(xin[0:TAIL_P, 8:16, :].rearrange("p j f -> p (j f)"),
                                      x_tail(x)).then_inc(loaded_x[k], 16)
                    else:
                        sp.dma_start(xin[:, 8 * k:8 * k + 8, :].rearrange("p j f -> p (j f)"),
                                      x_half(x, 2 * g + k)).then_inc(loaded_x[k], 16)

                def store(g, k, tail=False):
                    sp.wait_ge(res_ready, 4 * g + 2 * k + 2)
                    if tail:
                        sp.dma_start(x_tail(out), res[0:TAIL_P, 8:16, :].rearrange("p j f -> p (j f)"))\
                          .then_inc(stored[k], 16)
                    else:
                        sp.dma_start(x_half(out, 2 * g + k), res[:, 8 * k:8 * k + 8, :]
                                     .rearrange("p j f -> p (j f)")).then_inc(stored[k], 16)

                for k in range(2):
                    load_z(0, k)
                    load_hx(0, k)
                for k in range(2):
                    load_z(1, k)

                @groups(sp, GD, written=2, ended=2)
                def _(g):
                    static = isinstance(g, int)
                    more = not (static and g == GD - 1)
                    if more:
                        load_hx(g + 1, 0)
                    for k in range(2):
                        if not (static and g >= GD - 2):
                            load_z(g + 2, k)
                        if k == 0 and more:
                            load_hx(g + 1, 1, tail=static and g == GD - 2)
                        if not (static and g == 0):
                            store(g - 1, k)

                store(GD - 1, 0)
                store(GD - 1, 1, tail=True)
                for k in range(2):
                    sp.wait_ge(stored[k], 16 * GD)

            @block.gpsimd
            def _(pool):
                pool.wait_ge(b2_ready, 1)

                @groups(pool, GD)
                def _(g):
                    for c in range(U):
                        pool.wait_ge(x3_ready, 4 * g + c + 1)
                        reuse(pool, res_ready, 4 * g + c - 3)
                        apart(pool, passed)
                        pool.tensor_tensor(x3b[:, 4 * c:4 * c + 4, :], x3[:, 4 * c:4 * c + 4, :],
                                           b2r[:, :, :].to_broadcast([P, 4, P]), ALU.add).then_inc(x3b_ready, 1)

            @block.scalar
            def _(act):
                def units(g, k):
                    for c in (2 * k, 2 * k + 1):
                        act.wait_ge(loaded_z[k], 16 * g + 16)
                        reuse(act, mm_x, 4 * g + c - 3)
                        act.activation(unit[:, c, :], zin[:, c, :], ACT.Relu, bias=norm_c[:, LAYERS - 1:],
                                       scale=norm_a[:, LAYERS - 1:]).then_inc(unit_ready, 1)

                def x1_out(g, k):
                    for c in (2 * k, 2 * k + 1):
                        act.wait_ge(mm_x, 4 * g + c + 1)
                        reuse(act, x3_ready, 4 * g + c - 3)
                        act.activation(flat(x1, c), bank[0][:, c, :], ACT.Copy).then_inc(x1_ready, 1)

                def root1(g, k):
                    act.wait_ge(var1, 2 * g + k + 1)
                    ln_root(act, mv[k], 8, sd1)

                def h_out(g, k):
                    for c in (2 * k, 2 * k + 1):
                        act.wait_ge(turned, 4 * g + c + 1)
                        reuse(act, mixed, 4 * g + c - 3)
                        act.activation(h[:, c, :], bank[1][:, c, :], ACT.Relu).then_inc(h_ready, 1)

                def root3(g, k):
                    act.wait_ge(var3, 2 * g + k + 1)
                    ln_root(act, mv[2 + k], 8, sd3)

                def relu_ln3(g, k):
                    act.wait_ge(scaled, 2 * g + k + 1)
                    m = mv[2 + k]
                    for c in (2 * k, 2 * k + 1):
                        reuse(act, res_ready, 4 * g + c - 3)
                        for t in range(4 * c, 4 * c + 4):
                            i = t % 8
                            a = act.activation(hn[:, t, :], x3[:, t, :], ACT.Relu, bias=m[:, 0, i:i + 1],
                                               scale=m[:, 4, i:i + 1])
                        a.then_inc(hn_ready, 1)

                units(0, 0)
                x1_out(0, 0)
                units(0, 1)

                @groups(act, GD, written=2, ended=1)
                def _(g):
                    static = isinstance(g, int)
                    more = not (static and g == GD - 1)
                    for k in range(2):
                        root1(g, k)
                        if k == 0:
                            x1_out(g, 1)
                        elif more:
                            x1_out(g + 1, 0)
                        h_out(g, k)
                        begun = k or not (static and g == 0)
                        if begun:
                            root3(g if k else g - 1, 1 - k)
                        if more:
                            units(g + 1, k)
                        if begun:
                            relu_ln3(g if k else g - 1, 1 - k)

                root3(GD - 1, 1)
                relu_ln3(GD - 1, 1)

            @block.vector
            def _(dve):
                steps = Steps(dve, own, 2 * LN_STEPS)
                steps3 = [Steps(dve, o, LN_STEPS) for o in (own3_0, own3_1)]
                dve.tensor_scalar(b2r[:, 0, :], b2_row[:, :], 0.0, None, ALU.max).then_inc(b2_ready, 1)

                def sums1(g, k):
                    dve.wait_ge(x1_ready, 4 * g + 2 * k + 2)
                    ln_sums(dve, steps, x1[:, 8 * k:8 * k + 8, :], st[k], mv[k], 8, var1)

                def apply1(g, k):
                    dve.wait_ge(sd1, 2 * g + k + 1)
                    reuse(dve, turned, 4 * g + 2 * k - 2)
                    ln_apply(dve, steps, xn[:, 8 * k:8 * k + 8, :], x1[:, 8 * k:8 * k + 8, :], mv[k], 8, normed)

                def third(g, k):
                    for c in (2 * k, 2 * k + 1):
                        dve.wait_ge(mixed, 4 * g + c + 1)
                        reuse(dve, x3b_ready, 4 * g + c - 3)
                        reuse(dve, hn_ready, 4 * g + c - 3)
                        dve.scalar_tensor_tensor(flat(x3, c), bank[1][:, c, :], 0.0, flat(x1, c), ALU.max,
                                                 ALU.add).then_inc(x3_ready, 1)

                def sums3(g, k):
                    steps3[k].at(g)
                    dve.wait_ge(x3_ready, 4 * g + 2 * k + 2)
                    ln_sums(dve, steps3[k], x3[:, 8 * k:8 * k + 8, :], st[2 + k], mv[2 + k], 8, var3)

                def scale3(g, k):
                    m = mv[2 + k]
                    dve.wait_ge(sd3, 2 * g + k + 1)
                    steps3[k].did(dve.reciprocal(m[:, 4, :], m[:, 3, :]))
                    steps3[k].sync()
                    dve.tensor_tensor(m[:, 0, :], m[:, 0, :], m[:, 4, :], ALU.mult).then_inc(scaled, 1)

                def result(g, k):
                    for c in (2 * k, 2 * k + 1):
                        dve.wait_ge(hn_ready, 4 * g + c + 1)
                        dve.wait_ge(x3b_ready, 4 * g + c + 1)
                        reuse(dve, stored[k], 16 * g)
                        dve.tensor_tensor(flat(res, c), flat(x3b, c), flat(hn, c), ALU.add).then_inc(res_ready, 1)

                @groups(dve, GD, written=2)
                def _(g):
                    steps.at(g)
                    for k in range(2):
                        of = g if k else g - 1
                        begun = k or not (isinstance(g, int) and g == 0)
                        sums1(g, k)
                        if begun:
                            third(of, 1 - k)
                        apply1(g, k)
                        if begun:
                            sums3(of, 1 - k)
                        if not (isinstance(g, int) and g == 0):
                            result(g - 1, k)
                        if begun:
                            scale3(of, 1 - k)

                third(GD - 1, 1)
                sums3(GD - 1, 1)
                result(GD - 1, 0)
                scale3(GD - 1, 1)
                result(GD - 1, 1)

            @block.tensor
            def _(pe):
                def add_up(g, k):
                    for c in (2 * k, 2 * k + 1):
                        pe.wait_ge(loaded_x[k], 16 * g + 16)
                        reuse(pe, x1_ready, 4 * g + c - 3)
                        pe.matmul(bank[0][:, c, :], ident[:, :], flat(xin, c), start=True, stop=False)
                        pe.wait_ge(loaded_h[k], 16 * g + 16)
                        pe.wait_ge(unit_ready, 4 * g + c + 1)
                        for j in range(4):
                            s = slice(j * P, (j + 1) * P)
                            pe.matmul(bank[0][:, c, s], hin[:, c, s], tenth[:, :], start=False, stop=False)
                            m = pe.matmul(bank[0][:, c, s], unit[:, c, s], ident[:, :], start=False, stop=j == 3)
                        m.then_inc(mm_x, 1)

                def turn(g, c):
                    pe.wait_ge(normed, 4 * g + c + 1)
                    reuse(pe, x3_ready, 4 * g + c - 3)
                    for j in range(4):
                        t = pe.transpose(bank[1][:, c, j * P:(j + 1) * P], xn[:, 4 * c + j, :], ident[:, :])
                    t.then_inc(turned, 1)

                def mix(g, c):
                    pe.wait_ge(h_ready, 4 * g + c + 1)
                    pe.matmul(bank[1][:, c, :], three[:, :], c_parts[:, :, :].rearrange("p a f -> p (a f)"),
                              start=True, stop=False)
                    for j in range(4):
                        m = pe.matmul(bank[1][:, c, j * P:(j + 1) * P], h[:, c, j * P:(j + 1) * P], wm[:, 0, :],
                                      start=False, stop=j == 3)
                    m.then_inc(mixed, 1)

                add_up(0, 0)

                @groups(pe, GD, written=2, ended=1)
                def _(g):
                    for k in range(2):
                        if k == 0:
                            add_up(g, 1)
                        elif not (isinstance(g, int) and g == GD - 1):
                            add_up(g + 1, 0)
                        for c in (2 * k, 2 * k + 1):
                            turn(g, c)
                        for c in (2 * k, 2 * k + 1):
                            mix(g, c)

    def last_layers():
        tag = "z_"
        with stage() as ph:
            def tmp(name, shape, dt=F32):
                return ph.enter_context(nc.sbuf_tensor(tag + name, shape, dt))

            sums, xin, x3 = tmp("sums", [P, 16, P]), tmp("xin", [P, 16, P]), tmp("x3", [P, 16, P])
            hin, agg_t = tmp("hin", [P, U, CH]), tmp("agg_t", [P, U, CH])
            xn, hs, m1, m2, run, hid = (tmp(n, [P, 2, CH]) for n in ("xn", "hs", "m1", "m2", "run", "hid"))
            hn, part, res = tmp("hn", [P, 8, P]), tmp("part", [P, 8, P]), tmp("res", [P, 8, P])
            weight, kept, carry = tmp("weight", [P, 2, CH]), tmp("kept", [P, 2, CH], BF16), tmp("carry", [P, 1])
            st = [tmp(f"st{k}", [P, 8, 6]) for k in range(2)]
            mv = [tmp(f"mv{k}", [P, 5, 8]) for k in range(2)]
            at_i, to_i = tmp("at_i", [P, 8], I32), tmp("to_i", [P, 8], I32)
            (own, var_ready, sd_ready, normed, slot, got_d, loaded_w, loaded_k, turned, t_ready, mixed,
             x3_ready, applied, turned_s, hs_ready, mm1, m1_ready, m2_ready, scanned, carried, mm2, hid_ready, turned_o,
             part_ready, res_ready, put, slot_put) = (
                sem(tag + n) for n in ("own", "var", "sd", "normed", "slot", "got_d", "loaded_w",
                                       "loaded_k", "turned", "t", "mixed", "x3", "applied", "turned_s", "hs", "mm1", "m1",
                                       "m2", "scanned", "carried", "mm2", "hid", "turned_o", "part", "res", "put",
                                       "slot_put"))
            got, loaded_h, loaded_x = ([sem(f"{tag}{n}{k}") for k in range(2)] for n in ("got", "loaded_h", "loaded_x"))
            block = ph.enter_context(nc.Block())

            def flat(t, c):
                return t[:, 4 * c:4 * c + 4, :].rearrange("p t f -> p (t f)")

            def start(g):
                return isinstance(g, int) and g == 0

            def end(g):
                return isinstance(g, int) and g == GE - 1

            @block.gpsimd
            def _(pool):
                def gather(g):
                    gather_sums(pool, g, agg[1], sums[:, 8:16, :], at_i, slot, got, turned, U)

                def scatter(g):
                    pool.wait_ge(put, 128 * g)
                    pool.tensor_copy(to_i[:, :], put_i[:, bass.ds(g * 8, 8)]).then_inc(slot_put, 1)
                    pool.wait_ge(slot_put, g + 1)
                    for c in range(2):
                        pool.wait_ge(res_ready, 2 * g + c + 1)
                        apart(pool, passed)
                        for t in range(4 * c, 4 * c + 4):
                            pool.indirect_dma_start(out[:, :], bass.IndirectOffsetOnAxis(ap=to_i[:, t:t + 1], axis=0),
                                                    res[:, t, :], None, bounds_check=N - 1,
                                                    oob_is_err=False).then_inc(put, 16)

                gather(0)

                @groups(pool, GE, written=2, ended=1)
                def _(g):
                    if not end(g):
                        gather(g + 1)
                    if not start(g):
                        scatter(g - 1)

                scatter(GE - 1)
                pool.wait_ge(put, 128 * GE)

            @block.sync
            def _(sp):
                edge_w = A["edge_weight"].rearrange("(a n) -> a n", a=1)

                def load_x(g, k):
                    reuse(sp, mixed, 4 * g + 2 * k - 2)
                    sp.dma_start(hin[:, 2 * k:2 * k + 2, :].rearrange("p c n -> p (c n)"),
                                 he[:, bass.ds(g * GRP + k * HALF, HALF)]).then_inc(loaded_h[k], 16)
                    reuse(sp, x3_ready, 4 * g + 2 * k - 2)
                    sp.dma_start(xin[:, 8 * k:8 * k + 8, :], tiles(xe, g * GRP + k * HALF, 8)).then_inc(loaded_x[k], 16)

                def load_sums(g):
                    reuse(sp, turned, 4 * g - 2)
                    sp.dma_start(sums[:, 0:8, :], tiles(agg[1], g * HALF, 8)).then_inc(got_d, 16)

                load_sums(0)
                load_x(0, 0)
                load_x(0, 1)

                @groups(sp, GE, ended=1)
                def _(g):
                    if not end(g):
                        load_sums(g + 1)
                        load_x(g + 1, 0)
                    cols_w = E - (GE - 1) * HALF if end(g) else HALF
                    sp.wait_ge(m2_ready, 2 * g)
                    apart(sp, passed)
                    sp.dma_start(weight[:, :, :].rearrange("p c n -> p (c n)")[:, 0:cols_w],
                                 edge_w[:, bass.ds(g * HALF, cols_w)].to_broadcast([P, cols_w])).then_inc(loaded_w, 16)
                    sp.wait_ge(scanned, 2 * g)
                    sp.dma_start(kept[:, :, :].rearrange("p c n -> p (c n)"), keep_line[bass.ds(g * 8, 8), :]
                                 .rearrange("(a t) p -> a (t p)", a=1).to_broadcast([P, HALF])).then_inc(loaded_k, 16)
                    if not end(g):
                        load_x(g + 1, 1)

            @block.scalar
            def _(act):
                def sums_t(g, c):
                    act.wait_ge(turned, 4 * g + c + 1)
                    reuse(act, mixed, 4 * g + c - 3)
                    act.activation(agg_t[:, c, :], bank[0][:, c % 2, :], ACT.Copy).then_inc(t_ready, 1)

                def first_relu(g, c):
                    act.wait_ge(mm1, 2 * g + c + 1)
                    reuse(act, m2_ready, 2 * g + c - 1)
                    act.activation(m1[:, c, :], bank[1][:, 1, :], ACT.Relu, bias=gcols[:, 0:1]).then_inc(m1_ready, 1)

                def second_relu(g, c):
                    act.wait_ge(mm2, 2 * g + c + 1)
                    reuse(act, turned_o, 2 * g + c - 1)
                    act.activation(hid[:, c, :], bank[1][:, 2, :], ACT.Relu, bias=gcols[:, 1:2]).then_inc(hid_ready, 1)

                def sources(g, c):
                    act.wait_ge(turned_s, 2 * g + c + 1)
                    reuse(act, mm1, 2 * g + c - 1)
                    act.activation(hs[:, c, :], bank[1][:, 3 * c, :], ACT.Relu).then_inc(hs_ready, 1)

                def edges(g):
                    for c in range(2):
                        sources(g, c)
                    for c in range(2):
                        first_relu(g, c)

                @groups(act, GE, written=2)
                def _(g):
                    sums_t(g, 0)
                    sums_t(g, 1)
                    if not start(g):
                        edges(g - 1)
                    sums_t(g, 2)
                    sums_t(g, 3)
                    act.wait_ge(var_ready, 2 * g + 1)
                    ln_root(act, mv[0], 8, sd_ready)
                    for c in range(0 if start(g) else 2):
                        second_relu(g - 1, c)
                    act.wait_ge(var_ready, 2 * g + 2)
                    ln_root(act, mv[1], 8, sd_ready)

                edges(GE - 1)
                for c in range(2):
                    second_relu(GE - 1, c)

            @block.vector
            def _(dve):
                steps = Steps(dve, own, 2 * LN_STEPS)
                dve.memset(carry[:, :], 0.0).then_inc(carried, 1)

                def third(g, c):
                    dve.wait_ge(mixed, 4 * g + c + 1)
                    dve.wait_ge(loaded_x[c // 2], 16 * g + 16)
                    dve.wait_ge(part_ready if c < 2 else normed, 2 * g)
                    dve.scalar_tensor_tensor(flat(x3, c), bank[0][:, 2 + c % 2, :], 0.0, flat(xin, c), ALU.max,
                                             ALU.add).then_inc(x3_ready, 1)

                def weigh(g, c):
                    dve.wait_ge(m1_ready, 2 * g + c + 1)
                    dve.wait_ge(loaded_w, 16 * g + 16)
                    reuse(dve, scanned, 2 * g + c - 1)
                    dve.tensor_tensor(m2[:, c, :], m1[:, c, :], weight[:, c, :], ALU.mult).then_inc(m2_ready, 1)

                def sum_up(g):
                    dve.wait_ge(loaded_k, 16 * g + 16)
                    dve.wait_ge(mm2, 2 * g)
                    for c in range(2):
                        dve.wait_ge(m2_ready, 2 * g + c + 1)
                        scan(dve, g, c, run, kept, m2, carry, scanned, carried)

                def result(g):
                    for c in range(2):
                        dve.wait_ge(turned_o, 2 * g + c + 1)
                        dve.wait_ge(part_ready, 2 * g + c + 1)
                        dve.wait_ge(put, 128 * g)
                        dve.tensor_tensor(flat(res, c), flat(part, c), bank[1][:, 3 * c, :], ALU.add).then_inc(res_ready, 1)

                def normalise(g, k):
                    dve.wait_ge(sd_ready, 2 * g + k + 1)
                    if k:
                        dve.wait_ge(turned_s, 2 * g)
                        ln_apply(dve, steps, xn[:, :, :].rearrange("p c (t f) -> p (c t) f", f=P), x3[:, 8:16, :],
                                 mv[k], 8, normed)
                    else:
                        ln_apply(dve, steps, hn, x3[:, 0:8, :], mv[k], 8, applied)

                @groups(dve, GE, written=2)
                def _(g):
                    steps.at(g)
                    third(g, 0)
                    third(g, 1)
                    dve.wait_ge(x3_ready, 4 * g + 2)
                    ln_sums(dve, steps, x3[:, 0:8, :], st[0], mv[0], 8, var_ready)
                    if not start(g):
                        weigh(g - 1, 0)
                        weigh(g - 1, 1)
                        sum_up(g - 1)
                    third(g, 2)
                    third(g, 3)
                    dve.wait_ge(x3_ready, 4 * g + 4)
                    ln_sums(dve, steps, x3[:, 8:16, :], st[1], mv[1], 8, var_ready)
                    normalise(g, 1)
                    normalise(g, 0)
                    if not start(g):
                        result(g - 1)
                    for c in range(2):
                        dve.wait_ge(applied, 2 * g + c + 1)
                        reuse(dve, res_ready, 2 * g + c - 1)
                        dve.scalar_tensor_tensor(flat(part, c), flat(hn, c), 0.0, flat(x3, c), ALU.max,
                                                 ALU.add).then_inc(part_ready, 1)

                for c in range(2):
                    weigh(GE - 1, c)
                sum_up(GE - 1)
                result(GE - 1)

            @block.tensor
            def _(pe):
                def turn(g, c):
                    if c < 2:
                        pe.wait_ge(got_d, 16 * g + 16)
                    else:
                        pe.wait_ge(got[c - 2], 64 * g + 64)
                    reuse(pe, t_ready, 4 * g + c - 1)
                    for j in range(4):
                        t = pe.transpose(bank[0][:, c % 2, j * P:(j + 1) * P], sums[:, 4 * c + j, :], ident[:, :])
                    t.then_inc(turned, 1)

                def mix(g, c):
                    b = bank[0][:, 2 + c % 2, :]
                    reuse(pe, x3_ready, 4 * g + c - 1)
                    pe.matmul(b, three[:, :], c_parts[:, :, :].rearrange("p a f -> p (a f)"), start=True, stop=False)
                    pe.wait_ge(loaded_h[c // 2], 16 * g + 16)
                    pe.wait_ge(t_ready, 4 * g + c + 1)
                    for j in range(4):
                        s = slice(j * P, (j + 1) * P)
                        pe.matmul(b[:, s], hin[:, c, s], wm[:, 0, :], start=False, stop=False)
                        m = pe.matmul(b[:, s], agg_t[:, c, s], w_om[:, :], start=False, stop=j == 3)
                    m.then_inc(mixed, 1)

                def turn_sources(g, c):
                    pe.wait_ge(normed, 2 * g + c + 1)
                    reuse(pe, res_ready, 2 * g + c - 1)
                    for j in range(4):
                        t = pe.transpose(bank[1][:, 3 * c, j * P:(j + 1) * P], xn[:, c, j * P:(j + 1) * P], ident[:, :])
                    t.then_inc(turned_s, 1)

                def first_product(g, c):
                    pe.wait_ge(hs_ready, 2 * g + c + 1)
                    reuse(pe, m1_ready, 2 * g + c)
                    pe.matmul(bank[1][:, 1, :], wg1[:, :], hs[:, c, :], start=True, stop=True).then_inc(mm1, 1)

                def second_product(g, c):
                    pe.wait_ge(scanned, 2 * g + c + 1)
                    reuse(pe, hid_ready, 2 * g + c)
                    pe.matmul(bank[1][:, 2, :], wg2[:, :], run[:, c, :], start=True, stop=True).then_inc(mm2, 1)

                def turn_out(g, c):
                    pe.wait_ge(hid_ready, 2 * g + c + 1)
                    reuse(pe, res_ready, 2 * g + c - 1)
                    for j in range(4):
                        t = pe.transpose(bank[1][:, 3 * c, j * P:(j + 1) * P], hid[:, c, j * P:(j + 1) * P], ident[:, :])
                    t.then_inc(turned_o, 1)

                def edges(g):
                    for c in range(2):
                        turn_sources(g, c)
                    for c in range(2):
                        first_product(g, c)

                def put_out(g):
                    for c in range(2):
                        second_product(g, c)
                    for c in range(2):
                        turn_out(g, c)

                @groups(pe, GE, written=2)
                def _(g):
                    turn(g, 0)
                    turn(g, 1)
                    mix(g, 0)
                    mix(g, 1)
                    if not start(g):
                        edges(g - 1)
                    turn(g, 2)
                    turn(g, 3)
                    mix(g, 2)
                    mix(g, 3)
                    if not start(g):
                        put_out(g - 1)

                edges(GE - 1)
                put_out(GE - 1)

    first(True)
    first(False)
    for l in range(LAYERS):
        messages(l)
        if l:
            layer(l, True)
        layer(l, False)
        batch_norm(l)
    leave()
    for r in range(3):
        mean(r)
    finish()
    logits()
    softmax()
    last_layers()


NAMES = ["x", "src", "dst", "edge_attr_3", "edge_attr_32", "edge_weight",
         *(f"L0_gnn_{n}" for n in ("We", "be", "W1", "b1", "W2", "b2", "gamma", "beta")),
         *(f"L2_gnn_{n}" for n in ("Wq", "Wk", "Wv", "We", "Wo", "bo", "Wm", "bm")),
         *(f"L3_gnn_{n}" for n in ("W1", "b1", "W2", "b2"))]


def kernel(**inputs):
    import numpy as _np
    import concourse.bacc as _bacc
    from concourse import mybir as _mybir
    from concourse.bass_utils import run_bass_kernel_spmd as _run

    nc = _bacc.Bacc("TRN2", target_bir_lowering=False, num_devices=1)
    arrays, aps = {}, {}
    for name in NAMES:
        a = _np.ascontiguousarray(inputs[name])
        arrays[f"in_{name}"] = a
        aps[name] = nc.dram_tensor(f"in_{name}", a.shape, _mybir.dt.from_np(a.dtype), kind="ExternalInput").ap()
    out = nc.dram_tensor("out", (N, P), F32, kind="ExternalOutput").ap()
    gnn_kernel(nc, aps, out)
    r = _run(nc, [arrays], core_ids=[0])
    return r.results[0]["out"]
```
